# Optimizing a Trainium2 kernel written in Bass

```python
import numpy as np
import jax
import jax.numpy as jnp

def _softmax(x, axis=-1):
    return jax.nn.softmax(x, axis=axis)

def _gelu(x):
    return jax.nn.gelu(x, approximate=True)

def _silu(x):
    return jax.nn.silu(x)

def _sigmoid(x):
    return jax.nn.sigmoid(x)

def _layernorm(x, axis=-1, eps=1e-05):
    m = jnp.mean(x, axis=axis, keepdims=True)
    v = jnp.var(x, axis=axis, keepdims=True)
    return (x - m) / jnp.sqrt(v + eps)

def _scatter_add(tgt, idx, src, axis=0):
    return tgt.at[idx].add(src)

def _segment_sum(src, seg, n):
    return jax.ops.segment_sum(src, seg, n)
kernel_name = 'mk_adaln_attn_ffn_d1_seqx_r8_1f92c8'

def setup_inputs(seed: int=0):
    np.random.seed(seed)
    _w = jnp.asarray

    def _rec_inputs():
        import jax
        import jax.numpy as jnp
        _rk = jax.random.key(seed)
        x = -1.394e-06 + 0.9999 * jax.random.normal(jax.random.fold_in(_rk, 1), (4, 256, 256), jnp.float32)
        _lenS = 256 - jax.random.randint(jax.random.fold_in(_rk, 7), (4,), 0, max(1, 256 // 4) + 1, jnp.int32)
        _lenS2 = 256 - jax.random.randint(jax.random.fold_in(_rk, 8), (4,), 0, max(1, 256 // 4) + 1, jnp.int32)
        cond_2048 = -0.00499425 + 1.0058 * jax.random.normal(jax.random.fold_in(_rk, 11), (4, 256), jnp.float32)
        return (x, cond_2048)
    x, cond_2048 = _rec_inputs()

    def _L0_cond_setup():
        import jax, jax.numpy as jnp
        import numpy as np
        B, T, D = (16, 128, 256)
        key = jax.random.key(seed)
        k0, k1, k2, k3 = jax.random.split(key, 4)
        scale = 1.0 / np.sqrt(D)
        return {'initial_state': jax.random.normal(k0, (B, D), jnp.float32), 'inputs': jax.random.normal(k1, (B, T, D), jnp.float32), 'W_ih': jax.random.normal(k2, (D, 3 * D), jnp.float32) * scale, 'W_hh': jax.random.normal(k3, (D, 3 * D), jnp.float32) * scale, 'b_ih': jnp.zeros((3 * D,), jnp.float32), 'b_hh': jnp.zeros((3 * D,), jnp.float32)}
    _L0_cond_all = _L0_cond_setup()
    _L0_cond_in = {k: v for k, v in _L0_cond_all.items() if k in ('W_ih', 'W_hh', 'b_ih', 'b_hh')}
    del _L0_cond_all

    def _L0_attn_setup():
        import jax, jax.numpy as jnp
        import numpy as np
        EPS_NORM = 1e-08
        EPS_Q = 1e-05

        def rms_norm(x, w):
            var = jnp.mean(x * x, axis=-1, keepdims=True)
            return x * jax.lax.rsqrt(var + EPS_NORM) * w

        def activation_quant(x):
            scale = 127.0 / jnp.clip(jnp.max(jnp.abs(x), axis=-1, keepdims=True), EPS_Q, None)
            return jnp.clip(jnp.round(x * scale), -128, 127) / scale

        def weight_quant(w):
            scale = 1.0 / jnp.clip(jnp.mean(jnp.abs(w)), EPS_Q, None)
            return jnp.clip(jnp.round(w * scale), -1, 1) / scale

        def bitlinear(x, w, norm_w):
            xn = rms_norm(x, norm_w)
            xq = xn + jax.lax.stop_gradient(activation_quant(xn) - xn)
            wq = w + jax.lax.stop_gradient(weight_quant(w) - w)
            return jnp.einsum('bsh,oh->bso', xq, wq)
        key = jax.random.key(seed)
        k1, k2, k3 = jax.random.split(key, 3)
        H, I = (256, 704)
        x = jax.random.normal(k1, (4, 256, H), dtype=jnp.float32)
        w_gate = jax.random.normal(k2, (2 * I, H), dtype=jnp.float32) * (1.0 / np.sqrt(H))
        w_down = jax.random.normal(k3, (H, I), dtype=jnp.float32) * (1.0 / np.sqrt(I))
        norm_gate = jnp.ones((H,), dtype=jnp.float32)
        norm_down = jnp.ones((I,), dtype=jnp.float32)
        return {'x': x, 'w_gate': w_gate, 'norm_gate': norm_gate, 'w_down': w_down, 'norm_down': norm_down}
    _L0_attn_all = _L0_attn_setup()
    _L0_attn_in = {k: v for k, v in _L0_attn_all.items() if k in ('w_gate', 'norm_gate', 'w_down', 'norm_down')}
    del _L0_attn_all

    def _L0_cond2_setup():
        import jax, jax.numpy as jnp
        import numpy as np
        key = jax.random.key(seed)
        k1, k2 = jax.random.split(key)
        B, T, C, K = (4, 512, 256, 4)
        x = jax.random.normal(k1, (B, T, C), dtype=jnp.float32)
        w = jax.random.normal(k2, (K, 1, C), dtype=jnp.float32) * 0.1
        return {'x': x, 'w': w}
    _L0_cond2_all = _L0_cond2_setup()
    _L0_cond2_in = {k: v for k, v in _L0_cond2_all.items() if k in ()}
    del _L0_cond2_all

    def _L0_ffn_setup():
        import jax, jax.numpy as jnp
        import numpy as np
        from jax import lax
        H = 256
        I = 176
        E = 16
        TOP_K = 6
        IS = 2 * I

        def _swiglu(x, w13_, w2_):
            gu = x @ w13_.T
            g, u = jnp.split(gu, 2, axis=-1)
            return jax.nn.silu(g) * u @ w2_.T
        key = jax.random.key(seed)
        ks = jax.random.split(key, 6)
        return {'hidden_states': jax.random.normal(ks[0], (1, 256, H), jnp.float32), 'gate_w': jax.random.normal(ks[1], (E, H), jnp.float32) * 0.02, 'w13': jax.random.normal(ks[2], (E, 2 * I, H), jnp.float32) * 0.02, 'w2': jax.random.normal(ks[3], (E, H, I), jnp.float32) * 0.02, 'sw13': jax.random.normal(ks[4], (2 * IS, H), jnp.float32) * 0.02, 'sw2': jax.random.normal(ks[5], (H, IS), jnp.float32) * 0.02}
    _L0_ffn_all = _L0_ffn_setup()
    _L0_ffn_in = {k: v for k, v in _L0_ffn_all.items() if k in ('gate_w', 'w13', 'w2', 'sw13', 'sw2')}
    del _L0_ffn_all
    return {'x': x, 'cond_2048': cond_2048, 'L0_cond_W_ih': _L0_cond_in['W_ih'], 'L0_cond_W_hh': _L0_cond_in['W_hh'], 'L0_cond_b_ih': _L0_cond_in['b_ih'], 'L0_cond_b_hh': _L0_cond_in['b_hh'], 'L0_attn_w_gate': _L0_attn_in['w_gate'], 'L0_attn_norm_gate': _L0_attn_in['norm_gate'], 'L0_attn_w_down': _L0_attn_in['w_down'], 'L0_attn_norm_down': _L0_attn_in['norm_down'], 'L0_ffn_gate_w': _L0_ffn_in['gate_w'], 'L0_ffn_w13': _L0_ffn_in['w13'], 'L0_ffn_w2': _L0_ffn_in['w2'], 'L0_ffn_sw13': _L0_ffn_in['sw13'], 'L0_ffn_sw2': _L0_ffn_in['sw2']}

def reference(x, cond_2048, L0_cond_W_ih, L0_cond_W_hh, L0_cond_b_ih, L0_cond_b_hh, L0_attn_w_gate, L0_attn_norm_gate, L0_attn_w_down, L0_attn_norm_down, L0_ffn_gate_w, L0_ffn_w13, L0_ffn_w2, L0_ffn_sw13, L0_ffn_sw2):
    import jax
    import jax.numpy as jnp

    def _L0_cond_ref(initial_state, inputs, W_ih, W_hh, b_ih, b_hh):
        import jax, jax.numpy as jnp
        import numpy as np
        B, T, D = (16, 128, 256)
        "ScanOverTime(GRU cell): sequential per-timestep module call with\n            dict-state passing; merge_dict_trees stacks the per-step\n            'state_predicted' tensors along axis=1 -> [B, T, D]."

        def cell(h, x):
            gi = x @ W_ih + b_ih
            gh = h @ W_hh + b_hh
            i_r, i_z, i_n = jnp.split(gi, 3, axis=-1)
            h_r, h_z, h_n = jnp.split(gh, 3, axis=-1)
            r = jax.nn.sigmoid(i_r + h_r)
            z = jax.nn.sigmoid(i_z + h_z)
            n = jnp.tanh(i_n + r * h_n)
            h_new = (1.0 - z) * n + z * h
            return (h_new, h_new)
        xs = jnp.swapaxes(inputs, 0, 1)
        _, hs = jax.lax.scan(cell, initial_state, xs)
        return jnp.swapaxes(hs, 0, 1)

    def _L0_attn_ref(x, w_gate, norm_gate, w_down, norm_down):
        import jax, jax.numpy as jnp
        import numpy as np
        EPS_NORM = 1e-08
        EPS_Q = 1e-05

        def rms_norm(x, w):
            var = jnp.mean(x * x, axis=-1, keepdims=True)
            return x * jax.lax.rsqrt(var + EPS_NORM) * w

        def activation_quant(x):
            scale = 127.0 / jnp.clip(jnp.max(jnp.abs(x), axis=-1, keepdims=True), EPS_Q, None)
            return jnp.clip(jnp.round(x * scale), -128, 127) / scale

        def weight_quant(w):
            scale = 1.0 / jnp.clip(jnp.mean(jnp.abs(w)), EPS_Q, None)
            return jnp.clip(jnp.round(w * scale), -1, 1) / scale

        def bitlinear(x, w, norm_w):
            xn = rms_norm(x, norm_w)
            xq = xn + jax.lax.stop_gradient(activation_quant(xn) - xn)
            wq = w + jax.lax.stop_gradient(weight_quant(w) - w)
            return jnp.einsum('bsh,oh->bso', xq, wq)
        y = bitlinear(x, w_gate, norm_gate)
        gate, up = jnp.split(y, 2, axis=-1)
        h = gate * jax.nn.sigmoid(gate) * up
        return bitlinear(h, w_down, norm_down)

    def _L0_cond2_ref(x, w):
        import jax, jax.numpy as jnp
        import numpy as np
        K = w.shape[0]
        C = x.shape[-1]
        y = jax.lax.conv_general_dilated(x, w, window_strides=(1,), padding=[(K - 1, 0)], dimension_numbers=('NHC', 'HIO', 'NHC'), feature_group_count=C)
        return y

    def _L0_ffn_ref(hidden_states, gate_w, w13, w2, sw13, sw2):
        import jax, jax.numpy as jnp
        import numpy as np
        from jax import lax
        H = 256
        I = 176
        E = 16
        TOP_K = 6
        IS = 2 * I

        def _swiglu(x, w13_, w2_):
            gu = x @ w13_.T
            g, u = jnp.split(gu, 2, axis=-1)
            return jax.nn.silu(g) * u @ w2_.T
        B, S, Hd = hidden_states.shape
        x = hidden_states.reshape(-1, Hd)
        T = x.shape[0]
        scores = jax.nn.softmax(x @ gate_w.T, axis=-1)
        topk_w, topk_ids = lax.top_k(scores, TOP_K)
        topk_w = topk_w / (topk_w.sum(-1, keepdims=True) + 1e-20)
        combine = jnp.einsum('tk,tke->te', topk_w, jax.nn.one_hot(topk_ids, E, dtype=topk_w.dtype))

        def body(acc, ew):
            w13_e, w2_e, c_e = ew
            y = _swiglu(x, w13_e, w2_e)
            return (acc + c_e[:, None] * y, None)
        out, _ = lax.scan(body, jnp.zeros_like(x), (w13, w2, combine.T))
        out = out + _swiglu(x, sw13, sw2)
        return out.reshape(B, S, Hd)
    x = x + _L0_attn_ref(_L0_cond_ref(cond_2048, x, L0_cond_W_ih, L0_cond_W_hh, L0_cond_b_ih, L0_cond_b_hh), L0_attn_w_gate, L0_attn_norm_gate, L0_attn_w_down, L0_attn_norm_down)
    x = x + _L0_ffn_ref(_L0_cond2_ref(x, cond_2048[:, None, :]), L0_ffn_gate_w, L0_ffn_w13, L0_ffn_w2, L0_ffn_sw13, L0_ffn_sw2)
    return x

_drawn_inputs = setup_inputs


def setup_inputs(seed=0):
    import zlib

    import numpy as np

    out = dict(_drawn_inputs(seed))
    spreads = {'L0_cond_b_ih': (0.0, 0.1),
     'L0_cond_b_hh': (0.0, 0.1),
     'L0_attn_norm_gate': (1.0, 0.2),
     'L0_attn_norm_down': (1.0, 0.2)}
    factors = {}
    for name, (base, spread) in spreads.items():
        noise = np.random.default_rng([zlib.crc32(name.encode()), seed]).standard_normal(out[name].shape)
        drawn = base * np.exp(spread * noise) if base else spread * noise
        out[name] = jnp.asarray(drawn.astype(out[name].dtype))
    for name, factor in factors.items():
        out[name] = (out[name] * factor).astype(out[name].dtype)
    return out
```

```python
from contextlib import ExitStack

import concourse.bass as bass
from concourse import mybir

F32 = mybir.dt.float32
F32R = mybir.dt.float32r
F16 = mybir.dt.float16
BF16 = mybir.dt.bfloat16
ALU = mybir.AluOpType
ACT = mybir.ActivationFunctionType
X = mybir.AxisListType.X

P = 128
D = 256
NC = D // P
NB = 4
T = 256
STEPS = P // NB
TILES = T // STEPS
FF = 704
FC = 6
UNITS = ((0, 256), (256, 256), (512, 192))
E, TOPK, EI = 16, 6, 176
ROWS = E * EI
SI = 2 * EI
NF = (ROWS + SI + P - 1) // P
NSH = NF - ROWS // P
ORDER = [*range(ROWS // P, NF), *range(ROWS // P)]
BLOCK = 2 * P
BLOCKS = TILES // 2
RING = 16
KK = 4
HALO = NB * (KK - 1)

WS = 256.0
MAGIC = 12582912.0
EPS_NORM, EPS_Q, QMAX = 1e-8, 1e-5, 127.0

S_HT, S_STAT, S_AMAX, S_MAG, S_Q, S_QT = 1, 2, 3, 5, 6, 7
S_UNIT = (8, 11, 14)
S_K2, S_MAG2, S_Q2, S_Q2T, S_DOWN, S_X1T = 18, 21, 22, 23, 24, 25
S_CONV, S_HALO = (26, 27), 28
R_LOG, R_DIFF, R_SIG, R_SUM, R_TOP, R_REP, R_SEL, R_CT = 0, 1, 2, 3, 4, 5, 6, 8
M_G, M_U, M_SIG, M_T2, M_C, M_A, M_SPLIT, M_OUT, M_OUT2 = 0, 1, 2, 3, 3, 4, 5, 6, 7


def start(j):
    return 2 + (9 * j) // 4


def at_slot(q, after, lo=0):
    return [j for j in range(lo, NF) if start(j) + after == q]


PREP = NF + (NF + 1) // 2
PREP_AT = 4
Q_ABS, Q_SUM, Q_RED, Q_CLIP, Q_INV, Q_DIV, Q_TERN = 0, 6, 7, 8, 9, 10, 11
SS, AM, VAR, RR, MC, RC, K1, OSC, O2, VAR2, R2, OR2, AMX, MC2, RC2, K2, OSC2 = range(17)
SS2, AM2 = 17, 20
LINK1, LINK2, LINKR = 6, 11, 9


def adaln_kernel(nc, xT, xtok, w_ih, w_hh, condT, b_ih, b_hh, wgT, wdT, ng, nd, gwT, w13, w2, sel, idf, idb, out):
    ctx = ExitStack()
    with ctx:
        def sb(name, shape, dt):
            return ctx.enter_context(nc.sbuf_tensor(name, shape, dt))

        def pb(name, shape, dt):
            return ctx.enter_context(nc.psum_tensor(name, shape, dt))

        def sem(name):
            return ctx.enter_context(nc.semaphore(name))

        whh_hi, whh_lo = sb("whh_hi", [P, NC, 768], F16), sb("whh_lo", [P, NC, 768], F16)
        tg, td = sb("tg", [P, NC, 2 * FF], BF16), sb("td", [P, FC, D], BF16)
        identf, identb = sb("identf", [P, P], F32), sb("identb", [P, P], BF16)
        selb = sb("selb", [48, ROWS], BF16)
        ng_b, nd_b = sb("ng_b", [P, D], F32), sb("nd_b", [P, FF], F32)
        cond = sb("cond", [P, NC, NB], F32)
        gw = sb("gw", [P, NC, E], F32)
        ones = sb("ones", [P, P], F32)
        pw = sb("pw", [P, 32], F32)
        qp, qm = sb("qp", [P, 6], F32), sb("qm", [P, 2], F32)
        qc = sb("qc", [P, 3, 2], F32)
        gi = sb("gi", [P, 2, STEPS, 24], F32)
        bias = sb("bias", [P, 2, 6], F32)
        bsc = sb("bsc", [P, 2, 6], F32)
        tmpl = sb("tmpl", [P, 8, 2], F32)
        n_mul = sb("n_mul", [P, 8, 3], F32)
        n_sum = sb("n_sum", [P, 8, 3], F32)
        h_mul = sb("h_mul", [P, 8, 3], F32)
        steps = sb("steps", [P, RING, 25], F32)
        h16 = sb("h16", [P, 2, 24], F16)
        hist = sb("hist", [P, 2, NC, P], F32)
        hw, qb, qT = sb("hw", [P, D], F32), sb("qb", [P, D], BF16), sb("qT", [P, NC, P], BF16)
        junk = sb("junk", [P, D], F32)
        sg = sb("sg", [P, 256], F32)
        v = sb("v", [P, FF], F32)
        q2b, q2T = sb("q2b", [P, FF], BF16), sb("q2T", [P, FC, P], BF16)
        sm = sb("sm", [P, 24], F32)
        xt = sb("xt", [P, 2, D], F32)
        x1, x1b, yt = sb("x1", [P, 2, D], F32), sb("x1b", [P, 2, D], F32), sb("yt", [P, 2, D], F32)
        x1T = sb("x1T", [P, NC, HALO + 2 * P], F32)
        xc = sb("xc", [P, NC, BLOCK], F32)
        xc_hi, xc_lo = sb("xc_hi", [P, NC, BLOCK], F32R), sb("xc_lo", [P, NC, BLOCK], F32R)
        cT = sb("cT", [48, BLOCK], BF16)
        c3 = sb("c3", [P, 2, 3 * E], BF16)
        rt = sb("rt", [P, 8, 2, E + 2], F32)
        rs = sb("rs", [P, 8, 2], F32)
        m8 = sb("m8", [P, 2, 8], F32)

        base = nc.sbuf_base if not callable(nc.sbuf_base) else nc.sbuf_base()
        base = (int(base) + 63) // 64 * 64
        w13_bytes, w2_bytes = NF * 512 * 4, NF * 256 * 4
        arena = sb("arena", [P, (2 * w13_bytes + 2 * w2_bytes + 7 * BLOCK * 4 + 64) // 4], F32)

        place = [base]

        def at(name, shape, dt, size):
            t = nc.alloc_sbuf_tensor_at(name, shape, dt, offset=place[0])
            place[0] += size
            return t

        w13_hi = at("w13_hi", [P, NF, 2, NC, P], F32R, w13_bytes)
        w13_lo = at("w13_lo", [P, NF, 2, NC, P], F32R, w13_bytes)
        w2_hi = at("w2_hi", [P, NF, D], F32R, w2_bytes)
        w2_lo = at("w2_lo", [P, NF, D], F32R, w2_bytes)
        act = at("act", [P, 3, BLOCK], F32, 3 * BLOCK * 4)
        act_hi, act_lo = at("act_hi", [P, 2, BLOCK], F32R, 2 * BLOCK * 4), at("act_lo", [P, 2, BLOCK], F32R, 2 * BLOCK * 4)
        place[0] -= 7 * BLOCK * 4
        stage = at("stage", [P, 3, 512], F32, 6144)
        place[0] = base
        xf = at("xf", [P, NC, 1024], F32, 8192)
        xh = at("xh", [P, NC, 1024], F32R, 8192)
        xl = at("xl", [P, NC, 1024], F32R, 8192)
        wf = at("wf", [P, NC, 768], F32, 6144)
        wh = at("wh", [P, NC, 768], F32R, 6144)
        wl = at("wl", [P, NC, 768], F32R, 6144)
        whf = at("whf", [P, NC, 768], F32, 6144)
        gis = at("gis", [P, 128, 24], F32, 12288)
        gis2 = at("gis2", [P, 128, 24], F32, 12288)
        zer = at("zer", [P, 512], BF16, 1024)
        place[0] = base + 2 * w13_bytes
        wgf = at("wgf", [P, 4, FF], F32, 11264)
        wdf = at("wdf", [P, 2, 768], F32, 6144)

        bR, bZ = pb("bR", [P, 512], F32), pb("bZ", [P, 512], F32)
        bN = pb("bN", [P, 512], F32)
        bA = pb("bA", [P, 512], F32)
        bM = [pb("bM0", [P, 512], F32), pb("bM1", [P, 512], F32)]
        bC = pb("bC", [P, 512], F32)
        bO = pb("bO", [P, 512], F32)
        R = bR[:, 0:RING * 8].rearrange("p (s c b) -> p s c b", s=RING, c=NC)
        Z = bZ[:, 0:RING * 8].rearrange("p (s c b) -> p s c b", s=RING, c=NC)
        N = bN[:, 0:RING * 24].rearrange("p (s c b e) -> p s c b e", s=RING, c=NC, e=3)
        bA16 = bA[:, :].bitcast(BF16)
        bC16 = bC[:, :].bitcast(BF16)

        gi_dram = nc.dram_tensor("gi_scratch", [TILES + 1, P, STEPS * 24], F32, kind="Internal").ap()

        names = """ld_first ld_whh ld_x ld_const ld_quant x_split w_split x_hi w_hi gi_pe gi_ev gi_out gi_in0 gi_in1 gi_used
            setup zero banks_set b_scaled whh_high h0_high whh_split
            r_ready n_ready z_ready r_done z_done n_summed n_done h_hi h_full h_lo hist_done
            q_abs q_pe q_step q_tern
            st_in0 st_in1 st_in2 prep_hi prep_lo
            ht_pe sq_act hw_dve amax_dve k_pool mag_dve q_dve qT_pe qT_act
            gu_pe sg_act gt_dve v_dve sq2_act vw_pool max2_dve k2_pool mag2_dve q2_dve q2T_pe q2T_act
            down_pe x1_dve x1T_pe x1T_act conv_dve halo_act x1_kept xhi_act xlo_pool
            xt_in0 xt_in1 sm_link r_link
            r_log r_max r_d r_sig r_e r_sum r_p r_m8 r_m8set r_rep r_cun r_ssel r_c3 r_cT r_cT_act
            m_g m_u m_c m_sig m_t m_t2 m_a m_hi m_lo m_o y_done y_out""".split()
        S = {n: sem(n) for n in names}
        block = ctx.enter_context(nc.Block())

        def some(count):
            return not isinstance(count, int) or count > 0

        def fixed(e, count):
            if isinstance(count, int):
                return count
            count = e.snap(e.to_reg(count))
            e.wait_ge(S["setup"], 1)
            return count

        def flat(ap):
            return ap.rearrange("p a b -> p (a b)")

        def program(e, gru, rest):
            def half(i, par, prep=None, with_gru=True, attn=True, moe=True):
                m = 2 * i + par
                for s in range(STEPS):
                    if with_gru:
                        gru(m, par, s)
                    B, q = (i - 1, s) if par else (i - 2, STEPS + s)
                    rest(s, prep, m - 1 if attn else None, 1 - par, B if moe else None, q)
            half(0, 0, prep=0, attn=False, moe=False)
            half(0, 1, prep=1, moe=False)
            half(1, 0, moe=False)
            half(1, 1)
            with e.Fori(2, TILES // 2) as i:
                half(i, 0)
                half(i, 1)
            half(TILES // 2, 0, with_gru=False)
            half(TILES // 2, 1, with_gru=False, attn=False)
            half(TILES // 2 + 1, 0, with_gru=False, attn=False)

        def prep_piece(prep, s):
            k = s - PREP_AT if prep == 0 else s + STEPS - PREP_AT if prep == 1 else -1
            return k if 0 <= k < PREP else None

        def prep_views(k):
            if k < NF:
                return (stage[:, k % 3, :].rearrange("p (g c f) -> p g c f", g=2, c=NC), w13_hi[:, k], w13_lo[:, k])
            f = 2 * (k - NF)
            n = min(2, NF - f)
            return (stage[:, k % 3, 0:n * D].rearrange("p (f d) -> p f d", f=n), w2_hi[:, f:f + n, :], w2_lo[:, f:f + n, :])

        def released(j, B):
            return ("m_a", NF * B + j + 1) if j < NSH else ("m_t2", (NF - NSH) * B + j - NSH + 1)

        @block.sync
        def _(e):
            e.dma_start(wf[:, :, :], w_ih).then_inc(S["ld_first"], 16)
            e.dma_start(xf[:, :, 0:512], xT[:, :, 0:512]).then_inc(S["ld_first"], 16)
            e.dma_start(whf[:, :, :], w_hh).then_inc(S["ld_whh"], 16)
            e.dma_start(cond[:, :, :], condT).then_inc(S["ld_whh"], 16)
            e.dma_start(bias[:, 0, :], b_ih).then_inc(S["ld_whh"], 16)
            e.dma_start(bias[:, 1, :], b_hh).then_inc(S["ld_whh"], 16)
            e.dma_start(xf[:, :, 512:1024], xT[:, :, 512:1024]).then_inc(S["ld_x"], 16)
            e.dma_start(wgf[:, :, :], wgT).then_inc(S["ld_quant"], 16)
            e.dma_start(wdf[:, :, :], wdT).then_inc(S["ld_quant"], 16)
            e.dma_start(identf[:, :], idf).then_inc(S["ld_const"], 16)
            e.dma_start(identb[:, :], idb).then_inc(S["ld_const"], 16)
            e.dma_start(selb[:, :], sel).then_inc(S["ld_const"], 16)
            e.dma_start(gw[:, :, :], gwT).then_inc(S["ld_const"], 16)
            e.dma_start(ng_b[:, :], ng.broadcast_to([P, D])).then_inc(S["ld_const"], 16)
            e.dma_start(nd_b[:, :], nd.broadcast_to([P, FF])).then_inc(S["ld_const"], 16)
            for g, buf in ((0, gis), (1, gis2)):
                e.wait_ge(S["gi_ev"], 6 * (g + 1))
                for k in range(4):
                    e.dma_start(gi_dram[4 * g + k], flat(buf[:, 32 * k:32 * k + 32, :])).then_inc(S["gi_out"], 16)
                if g == 0:
                    e.wait_ge(S["gi_out"], 64)
                    for k in range(2):
                        e.dma_start(flat(gi[:, k, :, :]), gi_dram[k]).then_inc(S[f"gi_in{k}"], 16)
            e.dma_start(gi_dram[TILES], flat(gis2[:, 96:128, :])).then_inc(S["gi_out"], 16)
            e.wait_ge(S["gi_out"], 16 * (TILES + 1))

            def tile(dram, n):
                return dram[n] if isinstance(n, int) else dram[bass.ds(n, 1), :, :].rearrange("a p f -> (a p) f")

            def loads(m, par, gru=True, attn=True):
                if gru:
                    e.wait_ge(S["gi_used"], m)
                    e.dma_start(flat(gi[:, 1 - par, :, :]), tile(gi_dram, m + 1)).then_inc(S[f"gi_in{1 - par}"], 16)
                if attn:
                    if some(m - 2):
                        e.wait_ge(S["x1_dve"], m - 2)
                    e.dma_start(xt[:, 1 - par, :], tile(xtok, m - 1)).then_inc(S[f"xt_in{1 - par}"], 16)

            def result(B):
                e.wait_ge(S["y_done"], B + 1)
                for k in range(2):
                    e.dma_start(tile(out, 2 * B + k), yt[:, k, :]).then_inc(S["y_out"], 16)

            for k in range(PREP):
                if k >= 3:
                    e.wait_ge(S["prep_lo"], k - 2)
                src = w13[:, k, :] if k < NF else w2[:, 512 * (k - NF):min(512 * (k - NF + 1), NF * D)]
                e.dma_start(stage[:, k % 3, 0:src.shape[1]], src).then_inc(S[f"st_in{k % 3}"], 16)
            loads(1, 1)
            loads(2, 0)
            loads(3, 1)
            with e.Fori(2, TILES // 2) as i:
                loads(2 * i, 0)
                loads(2 * i + 1, 1)
                result(i - 2)
            loads(TILES, 0, gru=False)
            result(2)
            result(3)
            e.wait_ge(S["y_out"], 16 * TILES)

        @block.tensor
        def _(e):
            gi_banks = (bM[0], bM[1], bC, bO)

            e.wait_ge(S["zero"], 1)
            for bank in (bR, bZ, bN):
                mm = e.matmul(bank[:, :], zer[:, 0:P], zer[:, :], start=True, stop=True)
            mm.then_inc(S["banks_set"], 1)
            for g in range(2):
                for m6 in range(6):
                    q = 6 * g + m6
                    if m6 == 0:
                        e.wait_ge(S["w_split"], 1)
                        e.wait_ge(S["x_split"], g + 1)
                    if some(q - 3):
                        e.wait_ge(S["gi_ev"], q - 3)
                    terms = [(wt, xp, k) for wt, xp in ((wh, xh), (wh, xl), (wl, xh)) for k in range(NC)]
                    for t, (wt, xp, k) in enumerate(terms):
                        mm = e.matmul(gi_banks[q % 4][:, :], wt[:, k, m6 * P:(m6 + 1) * P], xp[:, k, 512 * g:512 * g + 512],
                                      start=(t == 0), stop=(t == len(terms) - 1))
                    mm.then_inc(S["gi_pe"], 1)
            e.wait_ge(S["ld_const"], 96)
            e.wait_ge(S["whh_split"], 1)

            def gate(out_of, g, wts, part):
                for c in range(NC):
                    for k in range(NC):
                        for wt in wts:
                            mm = e.matmul(out_of(c), wt[:, k, g * D + c * P:g * D + (c + 1) * P],
                                          h16[:, part, 12 * k + 2:12 * k + 12:3],
                                          start=False, stop=False, skip_group_check=True)
                return mm

            def gru(m, par, s):
                n, slot = 32 * m + s, s % RING
                r_of, z_of = lambda c: R[:, slot, c, :], lambda c: Z[:, slot, c, :]
                e.wait_ge(S["h_hi"], n + 1)
                gate(r_of, 0, (whh_hi, whh_lo), 0)
                gate(lambda c: N[:, slot, c, :, 0], 2, (whh_lo,), 0)
                e.wait_ge(S["h_lo"], n + 1)
                gate(r_of, 0, (whh_hi,), 1).then_inc(S["r_ready"], 1)
                for c in range(NC):
                    for k in range(NC):
                        mm = e.matmul(N[:, slot, c, :, 0:2].rearrange("p b e -> p e b"),
                                      whh_hi[:, k, 2 * D + c * P:2 * D + (c + 1) * P],
                                      h16[:, :, 12 * k + 2:12 * k + 12:3],
                                      start=False, stop=False, skip_group_check=True)
                mm.then_inc(S["n_ready"], 1)
                gate(z_of, 1, (whh_hi, whh_lo), 0)
                gate(z_of, 1, (whh_hi,), 1).then_inc(S["z_ready"], 1)

            def attn(s, n):
                if s == S_HT:
                    e.wait_ge(S["hist_done"], 4 * n + 4)
                    if some(n):
                        e.wait_ge(S["x1T_act"], n)
                    for c in range(NC):
                        mm = e.transpose(bA[:, c * P:(c + 1) * P], hist[:, tp[0], c, :], identf[:, :])
                    mm.then_inc(S["ht_pe"], 1)
                if s == S_QT:
                    e.wait_ge(S["q_dve"], n + 1)
                    for c in range(NC):
                        mm = e.transpose(bA16[:, c * P:(c + 1) * P], qb[:, c * P:(c + 1) * P], identb[:, :])
                    mm.then_inc(S["qT_pe"], 1)
                for u, (off, w) in enumerate(UNITS):
                    if s == S_UNIT[u]:
                        if u == 0:
                            e.wait_ge(S["qT_act"], n + 1)
                            e.wait_ge(S["q_tern"], 6)
                        else:
                            e.wait_ge(S["v_dve"], 3 * n + u)
                        for g in range(2):
                            for k in range(NC):
                                mm = e.matmul(bA[:, 256 * g:256 * g + w], qT[:, k, :], tg[:, k, FF * g + off:FF * g + off + w],
                                              start=(k == 0), stop=(k == NC - 1))
                        mm.then_inc(S["gu_pe"], 1)
                if s == S_Q2T:
                    e.wait_ge(S["q2_dve"], n + 1)
                    for c in range(FC):
                        w = min(P, FF - c * P)
                        mm = e.transpose(bA16[0:w, c * P:(c + 1) * P], q2b[:, c * P:c * P + w], identb[:, :])
                    mm.then_inc(S["q2T_pe"], 1)
                if s == S_DOWN:
                    e.wait_ge(S["q2T_act"], n + 1)
                    for c in range(FC):
                        w = min(P, FF - c * P)
                        mm = e.matmul(bA[:, 0:D], q2T[0:w, c, :], td[0:w, c, :], start=(c == 0), stop=(c == FC - 1))
                    mm.then_inc(S["down_pe"], 1)
                if s == S_X1T:
                    e.wait_ge(S["x1_dve"], n + 1)
                    for c in range(NC):
                        mm = e.transpose(bA[:, c * P:(c + 1) * P], x1[:, tp[0], c * P:(c + 1) * P], identf[:, :])
                    mm.then_inc(S["x1T_pe"], 1)

            def moe(q, B):
                if q == R_LOG:
                    e.wait_ge(S["conv_dve"], 8 * (2 * B + 2))
                    if some(NF * B):
                        e.wait_ge(S["m_a"], NF * B)
                    for t in range(2):
                        for c in range(NC):
                            mm = e.matmul(bC[:, t * E:(t + 1) * E], xc[:, c, t * P:(t + 1) * P], gw[:, c, :],
                                          start=(c == 0), stop=(c == NC - 1))
                    mm.then_inc(S["r_log"], 1)
                if q == R_CT:
                    count = fixed(e, B + 1)
                    e.wait_ge(S["r_c3"], count)
                    for t in range(2):
                        mm = e.transpose(bC16[0:48, t * P:(t + 1) * P], c3[:, t, :], identb[:, :])
                    mm.then_inc(S["r_cT"], 1)
                for stage_at, gu, done in ((M_G, 0, "m_g"), (M_U, 1, "m_u")):
                    for j in at_slot(q, stage_at):
                        f, bank = ORDER[j], bM[j % 2]
                        if gu == 0 and j == 0:
                            e.wait_ge(S["xhi_act"], B + 1)
                            e.wait_ge(S["xlo_pool"], B + 1)
                            e.wait_ge(S["prep_lo"], PREP)
                            if some((NF - NSH) * B):
                                e.wait_ge(S["m_t2"], (NF - NSH) * B)
                        if gu == 0 and j >= 2:
                            name, count = released(j - 2, B)
                            e.wait_ge(S[name], count)
                        terms = [(wt, xp, k) for wt, xp in ((w13_hi, xc_hi), (w13_lo, xc_hi), (w13_hi, xc_lo)) for k in range(NC)]
                        for t, (wt, xp, k) in enumerate(terms):
                            mm = e.matmul(bank[:, 256 * gu:256 * gu + 256], wt[:, f, gu, k, :], xp[:, k, :],
                                          start=(t == 0), stop=(t == len(terms) - 1))
                        mm.then_inc(S[done], 1)
                for j in at_slot(q, M_C, NSH):
                    if (j - NSH) % 2 == 0:
                        if j == NSH:
                            e.wait_ge(S["r_cT_act"], B + 1)
                        else:
                            e.wait_ge(S["m_a"], NF * B + j)
                        for d in range(2):
                            mm = e.matmul(bC[:, 256 * d:256 * d + 256], selb[:, (j + d - NSH) * P:(j + d - NSH + 1) * P], cT[:, :],
                                          start=True, stop=True)
                        mm.then_inc(S["m_c"], 1)
                for j in at_slot(q, M_OUT):
                    if j == 0:
                        if some(B):
                            e.wait_ge(S["y_done"], B)
                    e.wait_ge(S["m_hi"], NF * B + j + 1)
                    for wt in (w2_hi, w2_lo):
                        for t in range(2):
                            e.matmul(bO[:, t * D:(t + 1) * D], act_hi[:, j % 2, t * P:(t + 1) * P], wt[:, ORDER[j], :],
                                     start=(j == 0 and t == 0 and wt is w2_hi), stop=False, skip_group_check=True)
                for j in at_slot(q, M_OUT2):
                    e.wait_ge(S["m_lo"], NF * B + j + 1)
                    for t in range(2):
                        mm = e.matmul(bO[:, t * D:(t + 1) * D], act_lo[:, j % 2, t * P:(t + 1) * P], w2_hi[:, ORDER[j], :],
                                      start=False, stop=(j == NF - 1), skip_group_check=True)
                    mm.then_inc(S["m_o"], 1)

            tp = [0]

            def rest(s, prep, n, npar, B, q):
                tp[0] = npar
                if prep == 0 and s == Q_SUM:
                    e.wait_ge(S["q_abs"], 6)
                    e.wait_ge(S["setup"], 1)
                    e.matmul(bA[:, 0:6], ones[:, :], qp[:, :], start=True, stop=True).then_inc(S["q_pe"], 1)
                if n is not None:
                    attn(s, n)
                if B is not None:
                    moe(q, B)

            program(e, gru, rest)

        @block.scalar
        def _(e):
            e.wait_ge(S["ld_first"], 32)
            e.activation(wh[:, :, :], wf[:, :, :], ACT.Copy).then_inc(S["w_hi"], 1)
            e.activation(xh[:, :, 0:512], xf[:, :, 0:512], ACT.Copy).then_inc(S["x_hi"], 1)
            e.wait_ge(S["ld_x"], 16)
            e.activation(xh[:, :, 512:1024], xf[:, :, 512:1024], ACT.Copy).then_inc(S["x_hi"], 1)
            e.wait_ge(S["b_scaled"], 2)
            for g, buf in ((0, gis), (1, gis2)):
                for m6 in range(6):
                    q = 6 * g + m6
                    e.wait_ge(S["gi_pe"], q + 1)
                    e.activation(buf[:, :, 4 * m6:4 * m6 + 4], (bM[0], bM[1], bC, bO)[q % 4][:, :].rearrange("p (s b) -> p s b", b=NB),
                                 ACT.Identity, scale=WS, bias=bsc[:, 0, m6:m6 + 1]).then_inc(S["gi_ev"], 1)
            e.wait_ge(S["gi_out"], 16 * (TILES + 1))
            e.wait_ge(S["whh_split"], 1)
            e.wait_ge(S["banks_set"], 1)

            def gru(m, par, s):
                n, slot = 32 * m + s + 1, s % RING
                e.wait_ge(S["r_ready"], n)
                e.activation(n_mul[:, :, 2], flat(R[:, slot, :, :]), ACT.Sigmoid, scale=1 / WS).then_inc(S["r_done"], 1)
                e.wait_ge(S["z_ready"], n)
                e.activation(h_mul[:, :, 2], flat(Z[:, slot, :, :]), ACT.Sigmoid, scale=1 / WS).then_inc(S["z_done"], 1)
                e.wait_ge(S["n_summed"], n)
                e.activation(steps[:, slot, 1:25].rearrange("p (a b) -> p a b", b=3)[:, :, 0:3:2],
                             n_sum[:, :, 2:3].broadcast_to([P, 8, 2]), ACT.Tanh, scale=1 / WS).then_inc(S["n_done"], 1)

            def attn(s, n, npar):
                if s == S_STAT:
                    e.wait_ge(S["ht_pe"], n + 1)
                    e.activation(junk[:, :], bA[:, 0:D], ACT.Square, accum_out=sm[:, SS:SS + 1]).then_inc(S["sq_act"], 1)
                if s == S_QT:
                    e.wait_ge(S["qT_pe"], n + 1)
                    e.activation(flat(qT[:, :, :]), bA16[:, 0:D], ACT.Copy).then_inc(S["qT_act"], 1)
                for u, (off, w) in enumerate(UNITS):
                    if s == S_UNIT[u] + 1:
                        if some(3 * n + u):
                            e.wait_ge(S["gt_dve"], 3 * n + u)
                        e.wait_ge(S["gu_pe"], 3 * n + u + 1)
                        e.activation(sg[:, 0:w], bA[:, 0:w], ACT.Sigmoid, scale=sm[:, OSC:OSC + 1]).then_inc(S["sg_act"], 1)
                    if s == S_UNIT[u] + 3:
                        e.wait_ge(S["v_dve"], 3 * n + u + 1)
                        e.activation(junk[:, 0:w], v[:, off:off + w], ACT.Square,
                                     accum_out=sm[:, SS2 + u:SS2 + u + 1]).then_inc(S["sq2_act"], 1)
                if s == S_Q2T:
                    e.wait_ge(S["q2T_pe"], n + 1)
                    last = FF - (FC - 1) * P
                    e.activation(flat(q2T[:, 0:FC - 1, :]), bA16[:, 0:(FC - 1) * P], ACT.Copy)
                    e.activation(q2T[0:last, FC - 1, :], bA16[0:last, (FC - 1) * P:FC * P], ACT.Copy).then_inc(S["q2T_act"], 1)
                if s == S_X1T:
                    if some(8 * n):
                        e.wait_ge(S["conv_dve"], 8 * n)
                    e.wait_ge(S["x1T_pe"], n + 1)
                    e.activation(x1T[:, :, HALO + npar * P:HALO + npar * P + P], bA[:, 0:D].rearrange("p (c t) -> p c t", c=NC),
                                 ACT.Copy).then_inc(S["x1T_act"], 1)
                if s == S_HALO and npar == 1:
                    e.wait_ge(S["conv_dve"], 8 * n + 8)
                    e.activation(x1T[:, :, 0:HALO], x1T[:, :, BLOCK:BLOCK + HALO], ACT.Copy).then_inc(S["halo_act"], 1)

            def moe(q, B):
                if q == 0:
                    e.wait_ge(S["conv_dve"], 8 * (2 * B + 2))
                    if some(NF * B):
                        e.wait_ge(S["m_u"], NF * B)
                    e.activation(xc_hi[:, :, :], xc[:, :, :], ACT.Copy).then_inc(S["xhi_act"], 1)
                if q == R_SIG:
                    e.wait_ge(S["r_d"], B + 1)
                    e.activation(rt[:, 1, :, 0:E], rt[:, 0, :, 0:E], ACT.Sigmoid)
                    e.activation(rt[:, 2, :, 0:E], rt[:, 0, :, 0:E], ACT.Sigmoid, scale=-1.0).then_inc(S["r_sig"], 1)
                if q == R_CT:
                    e.wait_ge(S["r_cT"], B + 1)
                    e.activation(cT[:, :], bC16[0:48, 0:BLOCK], ACT.Copy).then_inc(S["r_cT_act"], 1)
                for j in at_slot(q, M_SIG):
                    if some(NF * B + max(0, j - 2)):
                        e.wait_ge(S["m_lo"], NF * B + max(0, j - 2))
                    e.wait_ge(S["m_u"], NF * B + j + 1)
                    e.activation(act[:, j % 3, :], bM[j % 2][:, 0:256], ACT.Sigmoid).then_inc(S["m_sig"], 1)
                for j in at_slot(q, M_SPLIT):
                    if some(NF * B + max(0, j - 1)):
                        e.wait_ge(S["m_o"], NF * B + max(0, j - 1))
                    e.wait_ge(S["m_a"], NF * B + j + 1)
                    e.activation(act_hi[:, j % 2, :], act[:, j % 3, :], ACT.Copy).then_inc(S["m_hi"], 1)

            def rest(s, prep, n, npar, B, q):
                k = prep_piece(prep, s)
                if k is not None:
                    if k == NF:
                        e.wait_ge(S["q_tern"], 6)
                    e.wait_ge(S[f"st_in{k % 3}"], 16 * (k // 3 + 1))
                    src, hi, _ = prep_views(k)
                    e.activation(hi, src, ACT.Copy).then_inc(S["prep_hi"], 1)
                if n is not None:
                    attn(s, n, npar)
                if B is not None:
                    moe(q, B)

            program(e, gru, rest)

        @block.vector
        def _(e):
            e.memset(zer[:, :], 0.0).then_inc(S["zero"], 1)
            e.memset(n_mul[:, :, :], 0.0)
            e.memset(h_mul[:, :, :], 0.0)
            e.memset(h16[:, :, :], 0.0)
            e.memset(tmpl[:, :, :], 0.0)
            e.memset(x1T[:, :, 0:HALO], 0.0)
            e.memset(rt[:, 4, :, E:E + 2], -1.0)
            e.memset(steps[:, :, :], 0.0).then_inc(S["zero"], 1)
            e.wait_ge(S["zero"], 2)
            e.memset(n_mul[:, :, 1], 1.0)
            e.memset(h_mul[:, :, 1], -1.0).then_inc(S["zero"], 1)
            e.wait_ge(S["w_hi"], 1)
            e.tensor_tensor(wl[:, :, :], wf[:, :, :], wh[:, :, :].bitcast(F32), ALU.subtract).then_inc(S["w_split"], 1)
            e.wait_ge(S["x_hi"], 1)
            e.tensor_tensor(xl[:, :, 0:512], xf[:, :, 0:512], xh[:, :, 0:512].bitcast(F32), ALU.subtract).then_inc(S["x_split"], 1)
            e.wait_ge(S["ld_whh"], 64)
            e.tensor_scalar(whh_hi[:, :, :], whf[:, :, :], WS, None, ALU.mult).then_inc(S["whh_high"], 1)
            e.wait_ge(S["whh_high"], 1)
            e.scalar_tensor_tensor(whh_lo[:, :, :], whf[:, :, :], WS, whh_hi[:, :, :], ALU.mult, ALU.subtract).then_inc(S["whh_split"], 1)
            e.wait_ge(S["x_hi"], 2)
            e.tensor_tensor(xl[:, :, 512:1024], xf[:, :, 512:1024], xh[:, :, 512:1024].bitcast(F32), ALU.subtract).then_inc(S["x_split"], 1)
            h_at = lambda ap: ap.rearrange("p (c b) -> p c b", c=NC)
            e.tensor_copy(h_at(steps[:, 0, 2:25:3]), cond[:, :, :])
            e.tensor_copy(h_at(h16[:, 0, 2:24:3]), cond[:, :, :]).then_inc(S["h0_high"], 1)
            e.wait_ge(S["h0_high"], 1)
            e.tensor_tensor(h_at(h16[:, 1, 2:24:3]), cond[:, :, :], h_at(h16[:, 0, 2:24:3]), ALU.subtract)
            e.wait_ge(S["b_scaled"], 2)
            for c in range(NC):
                e.tensor_scalar(tmpl[:, 4 * c:4 * c + 4, 0], n_mul[:, 0:4, 1], bsc[:, 1, 4 + c:5 + c], None, ALU.mult)
            e.tensor_scalar(tmpl[:, :, 1], n_mul[:, :, 0], 0.0, None, ALU.mult).then_inc(S["zero"], 1)
            e.wait_ge(S["zero"], 4)
            e.wait_ge(S["banks_set"], 1)
            e.wait_ge(S["gi_in0"], 16)
            e.wait_ge(S["ld_const"], 96)

            def seed(which, par, s):
                src, o, r = gi[:, par if s < STEPS else 1 - par], s % STEPS, s % RING
                if which == 0:
                    return e.tensor_copy(R[:, r:r + 8].rearrange("p s c b -> p s (c b)"), src[:, o:o + 8, 0:8])
                if which == 1:
                    e.tensor_copy(N[:, r:r + 8, :, :, 2].rearrange("p s c b -> p s (c b)"), src[:, o:o + 8, 16:24])
                    return e.tensor_copy(N[:, r:r + 8, :, :, 0:2].rearrange("p s c b e -> p s (c b) e"),
                                         tmpl[:, :, :].rearrange("p (a f) e -> p a f e", a=1).broadcast_to([P, 8, 8, 2]))
                return e.tensor_copy(Z[:, r:r + 8].rearrange("p s c b -> p s (c b)"), src[:, o:o + 8, 8:16])

            seed(0, 0, 0)
            seed(1, 0, 0).then_inc(S["h_hi"], 1)
            seed(2, 0, 0).then_inc(S["h_lo"], 1)

            def gru(m, par, s):
                n, slot, nxt = 32 * m + s + 1, s % RING, (s + 1) % RING
                if s % 8 == 0:
                    if some(4 * m + s // 8 - 1):
                        e.wait_ge(S["hist_done"], 4 * m + s // 8 - 1)
                e.wait_ge(S["r_done"], n)
                e.wait_ge(S["n_ready"], n)
                e.tensor_tensor_scan(flat(n_sum[:, :, :]), flat(n_mul[:, :, :]), N[:, slot].rearrange("p c b e -> p (c b e)"),
                                     0.0, ALU.mult, ALU.add).then_inc(S["n_summed"], 1)
                if s % 8 == 0:
                    if s == STEPS - 8:
                        e.wait_ge(S[f"gi_in{1 - par}"], 8 * m + 8 * par + 16)
                    seed(0, par, s + 8)
                if s % 8 == 1:
                    seed(1, par, s + 7)
                if s % 8 == 2:
                    e.wait_ge(S["z_done"], n)
                    last = seed(2, par, s + 6)
                    if s == STEPS - 14:
                        last.then_inc(S["gi_used"], 1)
                e.wait_ge(S["n_done"], n)
                e.wait_ge(S["z_done"], n)
                row, nrow = steps[:, slot, 1:25], steps[:, nxt, 0:24]
                e.tensor_tensor_scan(h16[:, 0, :], flat(h_mul[:, :, :]), row, 0.0, ALU.mult, ALU.add).then_inc(S["h_hi"], 1)
                e.tensor_tensor_scan(nrow, flat(h_mul[:, :, :]), row, 0.0, ALU.mult, ALU.add).then_inc(S["h_full"], 1)
                e.wait_ge(S["h_full"], n)
                e.tensor_tensor(h16[:, 1, 2:24:3], steps[:, nxt, 2:25:3], h16[:, 0, 2:24:3], ALU.subtract).then_inc(S["h_lo"], 1)

            def quant(s):
                src = lambda j: wgf[:, j, :] if j < 4 else wdf[:, j - 4, :]
                if Q_ABS <= s < Q_ABS + 6:
                    if s == Q_ABS:
                        e.wait_ge(S["ld_quant"], 32)
                    e.tensor_reduce(qp[:, s:s + 1], src(s), X, ALU.add, apply_absolute_value=True).then_inc(S["q_abs"], 1)
                if s == Q_RED:
                    e.wait_ge(S["q_pe"], 1)
                    e.tensor_reduce(qm[:, 0:1], bA[:, 0:4], X, ALU.add)
                    e.tensor_reduce(qm[:, 1:2], bA[:, 4:6], X, ALU.add).then_inc(S["q_step"], 1)
                if s == Q_CLIP:
                    e.wait_ge(S["q_step"], 1)
                    e.tensor_scalar(qc[:, 0, 0:1], qm[:, 0:1], 1.0 / (2 * FF * D), EPS_Q, ALU.mult, ALU.max)
                    e.tensor_scalar(qc[:, 0, 1:2], qm[:, 1:2], 1.0 / (FF * D), EPS_Q, ALU.mult, ALU.max).then_inc(S["q_step"], 1)
                if s == Q_INV:
                    e.wait_ge(S["q_step"], 2)
                    e.reciprocal(qc[:, 1, :], qc[:, 0, :]).then_inc(S["q_step"], 1)
                if s == Q_DIV:
                    e.tensor_scalar(qc[:, 2, :], qc[:, 0, :], 1.0 / QMAX, None, ALU.mult).then_inc(S["q_step"], 1)
                if Q_TERN <= s < Q_TERN + 18:
                    o = s - Q_TERN
                    j, step = o // 3, o % 3
                    w = src(j)
                    e.wait_ge(S["q_step"], 4 + 2 * j + step)
                    if step == 0:
                        which = 0 if j < 4 else 1
                        e.tensor_scalar(w, w, qc[:, 1, which:which + 1], MAGIC, ALU.mult, ALU.add).then_inc(S["q_step"], 1)
                    elif step == 1:
                        e.tensor_scalar(w, w, MAGIC, 1.0, ALU.subtract, ALU.min).then_inc(S["q_step"], 1)
                    else:
                        dst = tg[:, j // 2, (j % 2) * FF:(j % 2) * FF + FF] if j < 4 else flat(td[:, 3 * (j - 4):3 * (j - 4) + 3, :])
                        e.tensor_scalar(dst, w, -1.0, None, ALU.max).then_inc(S["q_tern"], 1)

            def attn(s, n, npar):
                if s == S_STAT:
                    e.wait_ge(S["sq_act"], n + 1)
                    e.tensor_tensor(hw[:, :], bA[:, 0:D], ng_b[:, :], ALU.mult).then_inc(S["hw_dve"], 1)
                if s == S_AMAX:
                    e.wait_ge(S["hw_dve"], n + 1)
                    e.tensor_reduce(sm[:, AM:AM + 1], hw[:, :], X, ALU.max, apply_absolute_value=True).then_inc(S["amax_dve"], 1)
                if s == S_MAG:
                    e.wait_ge(S["k_pool"], n + 1)
                    e.tensor_scalar(hw[:, :], hw[:, :], sm[:, K1:K1 + 1], MAGIC, ALU.mult, ALU.add).then_inc(S["mag_dve"], 1)
                if s == S_Q:
                    e.wait_ge(S["mag_dve"], n + 1)
                    if some(n):
                        e.wait_ge(S["qT_pe"], n)
                    e.tensor_scalar(qb[:, :], hw[:, :], MAGIC, None, ALU.subtract).then_inc(S["q_dve"], 1)
                for u, (off, w) in enumerate(UNITS):
                    if s == S_UNIT[u] + 1:
                        e.wait_ge(S["sg_act"], 3 * n + u + 1)
                        e.tensor_tensor(v[:, off:off + w], bA[:, 0:w], sg[:, 0:w], ALU.mult).then_inc(S["gt_dve"], 1)
                    if s == S_UNIT[u] + 2:
                        e.wait_ge(S["gt_dve"], 3 * n + u + 1)
                        e.tensor_tensor(v[:, off:off + w], bA[:, 256:256 + w], v[:, off:off + w], ALU.mult).then_inc(S["v_dve"], 1)
                    if s == S_UNIT[u] + 4:
                        e.wait_ge(S["vw_pool"], 3 * n + u + 1)
                        e.tensor_reduce(sm[:, AM2 + u:AM2 + u + 1], v[:, off:off + w], X, ALU.max,
                                        apply_absolute_value=True).then_inc(S["max2_dve"], 1)
                if s == S_MAG2:
                    e.wait_ge(S["k2_pool"], n + 1)
                    e.tensor_scalar(v[:, :], v[:, :], sm[:, K2:K2 + 1], MAGIC, ALU.mult, ALU.add).then_inc(S["mag2_dve"], 1)
                if s == S_Q2:
                    e.wait_ge(S["mag2_dve"], n + 1)
                    if some(n):
                        e.wait_ge(S["q2T_pe"], n)
                    e.tensor_scalar(q2b[:, :], v[:, :], MAGIC, None, ALU.subtract).then_inc(S["q2_dve"], 1)
                if s == S_DOWN:
                    e.wait_ge(S[f"xt_in{npar}"], 8 * n - 8 * npar + 16)
                    if some(kept(n, npar)):
                        e.wait_ge(S["x1_kept"], kept(n, npar))
                    e.wait_ge(S["down_pe"], n + 1)
                    e.scalar_tensor_tensor(x1[:, npar, :], bA[:, 0:D], sm[:, OSC2:OSC2 + 1], xt[:, npar, :],
                                           ALU.mult, ALU.add).then_inc(S["x1_dve"], 1)
                if s in S_CONV:
                    for o in range(4 * (s - S_CONV[0]), 4 * (s - S_CONV[0]) + 4):
                        k, c = o // 2, o % 2
                        if o == 0:
                            e.wait_ge(S["x1T_act"], n + 1)
                            if some(kept(n, npar)):
                                e.wait_ge(S["xlo_pool"], kept(n, npar))
                            if some(kept(n, npar)):
                                e.wait_ge(S["r_log"], kept(n, npar))
                            if npar == 0:
                                if some(kept(n, npar)):
                                    e.wait_ge(S["halo_act"], kept(n, npar))
                        src = x1T[:, c, npar * P + NB * k:npar * P + NB * k + P]
                        dst = xc[:, c, npar * P:npar * P + P]
                        if k == 0:
                            e.tensor_scalar(dst, src, cond[:, c, k:k + 1], None, ALU.mult).then_inc(S["conv_dve"], 1)
                        else:
                            e.wait_ge(S["conv_dve"], 8 * n + o - 1)
                            e.scalar_tensor_tensor(dst, src, cond[:, c, k:k + 1], dst, ALU.mult, ALU.add).then_inc(S["conv_dve"], 1)

            def kept(n, npar):
                return n // 2 if isinstance(n, int) else blocks_behind[0]

            blocks_behind = [0]

            def result(B):
                e.wait_ge(S["m_o"], NF * (B + 1))
                e.wait_ge(S["x1_kept"], B + 1)
                e.tensor_tensor(flat(yt[:, :, :]), bO[:, :], flat(x1b[:, :, :]), ALU.add).then_inc(S["y_done"], 1)

            def moe(q, B):
                logits = bC[:, 0:2 * E].rearrange("p (t e) -> p t e", t=2)
                if q == 0 and not (isinstance(B, int) and B == 0):
                    result(B - 1)
                if q == STEPS - 1:
                    if some(32 * B):
                        e.wait_ge(S["y_out"], 32 * B)
                if q == R_LOG:
                    e.wait_ge(S["r_log"], B + 1)
                    e.tensor_reduce(rs[:, 0, :], logits, X, ALU.max).then_inc(S["r_max"], 1)
                if q == R_DIFF:
                    e.wait_ge(S["r_max"], B + 1)
                    e.tensor_tensor(rt[:, 0, :, 0:E], logits, rs[:, 0, :].rearrange("p (t a) -> p t a", a=1).broadcast_to([P, 2, E]),
                                    ALU.subtract).then_inc(S["r_d"], 1)
                if q == R_SUM:
                    e.wait_ge(S["r_e"], B + 1)
                    e.tensor_reduce(rs[:, 1, :], rt[:, 3, :, 0:E], X, ALU.add).then_inc(S["r_sum"], 1)
                if q == R_TOP:
                    count = fixed(e, B + 1)
                    e.wait_ge(S["r_p"], count)
                    e.max(m8[:, 0, :], rt[:, 4, 0, 0:E])
                    e.max(m8[:, 1, :], rt[:, 4, 1, 0:E]).then_inc(S["r_m8"], 1)
                if q == R_REP:
                    count = fixed(e, B + 1)
                    e.wait_ge(S["r_m8set"], count)
                    e.match_replace(rt[:, 5, 0, :], m8[:, 0, :], rt[:, 4, 0, :], -2.0)
                    e.match_replace(rt[:, 5, 1, :], m8[:, 1, :], rt[:, 4, 1, :], -2.0).then_inc(S["r_rep"], 1)
                if q == R_SEL:
                    e.wait_ge(S["r_cun"], B + 1)
                    e.tensor_reduce(rs[:, 3, :], rt[:, 7, :, 0:E], X, ALU.add).then_inc(S["r_ssel"], 1)
                for j in at_slot(q, M_SIG):
                    e.wait_ge(S["m_sig"], NF * B + j + 1)
                    e.tensor_tensor(act[:, j % 3, :], bM[j % 2][:, 0:256], act[:, j % 3, :], ALU.mult).then_inc(S["m_t"], 1)
                for j in at_slot(q, M_T2):
                    e.wait_ge(S["m_t"], NF * B + j + 1)
                    e.tensor_tensor(act[:, j % 3, :], bM[j % 2][:, 256:512], act[:, j % 3, :],
                                    ALU.mult).then_inc(S["m_a" if j < NSH else "m_t2"], 1)
                for j in at_slot(q, M_A, NSH):
                    d = (j - NSH) % 2
                    e.wait_ge(S["m_c"], (NF - NSH) // 2 * B + (j - NSH) // 2 + 1)
                    e.wait_ge(S["m_t2"], (NF - NSH) * B + j - NSH + 1)
                    e.tensor_tensor(act[:, j % 3, :], bC[:, 256 * d:256 * d + 256], act[:, j % 3, :], ALU.mult).then_inc(S["m_a"], 1)

            def rest(s, prep, n, npar, B, q):
                if n is not None and not isinstance(n, int):
                    blocks_behind[0] = B + 1
                if prep == 0:
                    quant(s)
                if n is not None:
                    attn(s, n, npar)
                if B is not None:
                    moe(q, B)

            program(e, gru, rest)
            result(BLOCKS - 1)

        @block.gpsimd
        def _(e):
            e.memset(ones[:, :], 1.0)
            e.memset(pw[:, :], -1.0).then_inc(S["b_scaled"], 1)
            e.wait_ge(S["b_scaled"], 1)
            e.memset(pw[:, 0:1], -0.5)
            e.wait_ge(S["ld_whh"], 64)
            e.tensor_scalar(bsc[:, :, :], bias[:, :, :], WS, None, ALU.mult).then_inc(S["r_link"], 1)
            e.wait_ge(S["r_link"], 1)
            e.tensor_tensor(bsc[:, 0, 0:4], bsc[:, 0, 0:4], bsc[:, 1, 0:4], ALU.add).then_inc(S["b_scaled"], 1)
            e.memset(m8[:, :, :], 0.0).then_inc(S["setup"], 1)
            e.wait_ge(S["ld_const"], 96)
            col = lambda k: sm[:, k:k + 1]
            half_, one_ = pw[:, 0:1], pw[:, 1:2]

            def gru(m, par, s):
                if s % 8 == 7:
                    count = fixed(e, 32 * m + s + 1)
                    e.wait_ge(S["h_full"], count)
                    if some(m - 1):
                        e.wait_ge(S["ht_pe"], m - 1)
                    first = (s - 6) % RING
                    runs = ((first, 8),) if first + 8 <= RING else ((first, RING - first), (0, 8 - (RING - first)))
                    t = NB * (s - 7)
                    for r, cnt in runs:
                        ins = e.tensor_copy(hist[:, par, :, t:t + NB * cnt].rearrange("p c (s b) -> p c s b", b=NB),
                                            steps[:, r:r + cnt, 2:25:3].rearrange("p s (c b) -> p c s b", c=NC))
                        t += NB * cnt
                    ins.then_inc(S["hist_done"], 1)

            def attn(s, n, npar):
                if s == S_AMAX:
                    count = fixed(e, n + 1)
                    e.wait_ge(S["sq_act"], count)
                    b = (LINK1 + LINK2) * n
                    e.tensor_scalar(col(VAR), col(SS), 1.0 / D, EPS_NORM, ALU.mult, ALU.add).then_inc(S["sm_link"], 1)
                    e.wait_ge(S["sm_link"], b + 1)
                    e.tensor_tensor(col(RR), col(VAR), half_, ALU.pow).then_inc(S["sm_link"], 1)
                    count = fixed(e, b + 2)
                    e.wait_ge(S["sm_link"], count)
                    count = fixed(e, n + 1)
                    e.wait_ge(S["amax_dve"], count)
                    e.tensor_scalar(col(MC), col(AM), col(RR), EPS_Q, ALU.mult, ALU.max).then_inc(S["sm_link"], 1)
                    e.wait_ge(S["sm_link"], b + 3)
                    e.tensor_tensor(col(RC), col(MC), one_, ALU.pow).then_inc(S["sm_link"], 1)
                    count = fixed(e, b + 4)
                    e.wait_ge(S["sm_link"], count)
                    e.tensor_scalar(col(K1), col(RC), QMAX, col(RR), ALU.mult, ALU.mult).then_inc(S["sm_link"], 1)
                    e.wait_ge(S["sm_link"], b + 5)
                    e.tensor_tensor(col(OSC), col(MC), qc[:, 2, 0:1], ALU.mult).then_inc(S["sm_link"], 1)
                    e.wait_ge(S["sm_link"], b + 6)
                    e.tensor_tensor(col(O2), col(OSC), col(OSC), ALU.mult).then_inc(S["k_pool"], 1)
                for u, (off, w) in enumerate(UNITS):
                    if s == S_UNIT[u] + 3:
                        e.wait_ge(S["sq2_act"], 3 * n + u + 1)
                        e.tensor_tensor(v[:, off:off + w], v[:, off:off + w], nd_b[:, off:off + w], ALU.mult).then_inc(S["vw_pool"], 1)
                if s == S_K2:
                    b = (LINK1 + LINK2) * n + LINK1
                    e.wait_ge(S["sq2_act"], 3 * n + 3)
                    e.wait_ge(S["k_pool"], n + 1)
                    e.tensor_tensor(col(VAR2), col(SS2), col(SS2 + 1), ALU.add).then_inc(S["sm_link"], 1)
                    e.wait_ge(S["sm_link"], b + 1)
                    e.tensor_tensor(col(VAR2), col(VAR2), col(SS2 + 2), ALU.add).then_inc(S["sm_link"], 1)
                    count = fixed(e, b + 2)
                    e.wait_ge(S["sm_link"], count)
                    e.tensor_scalar(col(VAR2), col(VAR2), col(O2), col(O2), ALU.mult, ALU.mult).then_inc(S["sm_link"], 1)
                    count = fixed(e, b + 3)
                    e.wait_ge(S["sm_link"], count)
                    e.tensor_scalar(col(VAR2), col(VAR2), 1.0 / FF, EPS_NORM, ALU.mult, ALU.add).then_inc(S["sm_link"], 1)
                    e.wait_ge(S["sm_link"], b + 4)
                    e.tensor_tensor(col(R2), col(VAR2), half_, ALU.pow).then_inc(S["sm_link"], 1)
                    e.wait_ge(S["sm_link"], b + 5)
                    e.tensor_tensor(col(OR2), col(R2), col(O2), ALU.mult).then_inc(S["sm_link"], 1)
                    count = fixed(e, b + 6)
                    e.wait_ge(S["sm_link"], count)
                    count = fixed(e, 3 * n + 3)
                    e.wait_ge(S["max2_dve"], count)
                    e.tensor_scalar(col(AMX), col(AM2), col(AM2 + 1), col(AM2 + 2), ALU.max, ALU.max).then_inc(S["sm_link"], 1)
                    count = fixed(e, b + 7)
                    e.wait_ge(S["sm_link"], count)
                    e.tensor_scalar(col(MC2), col(AMX), col(OR2), EPS_Q, ALU.mult, ALU.max).then_inc(S["sm_link"], 1)
                    e.wait_ge(S["sm_link"], b + 8)
                    e.tensor_tensor(col(RC2), col(MC2), one_, ALU.pow).then_inc(S["sm_link"], 1)
                    count = fixed(e, b + 9)
                    e.wait_ge(S["sm_link"], count)
                    e.tensor_scalar(col(K2), col(RC2), QMAX, col(OR2), ALU.mult, ALU.mult).then_inc(S["sm_link"], 1)
                    e.wait_ge(S["sm_link"], b + 10)
                    e.tensor_tensor(col(OSC2), col(MC2), qc[:, 2, 1:2], ALU.mult).then_inc(S["sm_link"], 1)
                    count = fixed(e, b + 11)
                    e.wait_ge(S["sm_link"], count)
                    e.tensor_copy(col(O2), col(O2)).then_inc(S["k2_pool"], 1)

            def moe(q, B):
                lb = 1 + LINKR * B
                t_ = lambda k: rt[:, k, :, 0:E]
                if q == 0:
                    e.wait_ge(S["xhi_act"], B + 1)
                    e.tensor_tensor(xc_lo[:, :, :], xc[:, :, :], xc_hi[:, :, :].bitcast(F32), ALU.subtract).then_inc(S["xlo_pool"], 1)
                if q == 1:
                    count = fixed(e, 2 * B + 2)
                    e.wait_ge(S["x1_dve"], count)
                    if some(B):
                        e.wait_ge(S["y_done"], B)
                    e.tensor_copy(flat(x1b[:, :, :]), flat(x1[:, :, :])).then_inc(S["x1_kept"], 1)
                if q == R_SIG:
                    e.wait_ge(S["r_sig"], B + 1)
                    e.tensor_tensor(t_(2), t_(2), pw32(one=True), ALU.pow).then_inc(S["r_link"], 1)
                    e.wait_ge(S["r_link"], lb + 1)
                    e.tensor_tensor(t_(3), t_(1), t_(2), ALU.mult).then_inc(S["r_e"], 1)
                if q == R_SUM:
                    e.wait_ge(S["r_sum"], B + 1)
                    e.tensor_tensor(rs[:, 2, :], rs[:, 1, :], pw[:, 1:3], ALU.pow).then_inc(S["r_link"], 1)
                    count = fixed(e, lb + 2)
                    e.wait_ge(S["r_link"], count)
                    e.tensor_scalar(rt[:, 4, 0, 0:E], rt[:, 3, 0, 0:E], rs[:, 2, 0:1], None, ALU.mult)
                    e.tensor_scalar(rt[:, 4, 1, 0:E], rt[:, 3, 1, 0:E], rs[:, 2, 1:2], None, ALU.mult).then_inc(S["r_p"], 1)
                if q == R_TOP:
                    count = fixed(e, B + 1)
                    e.wait_ge(S["r_m8"], count)
                    e.memset(m8[:, :, TOPK:8], -1.0).then_inc(S["r_m8set"], 1)
                if q == R_REP:
                    count = fixed(e, B + 1)
                    e.wait_ge(S["r_rep"], count)
                    e.tensor_scalar(t_(6), t_(5), 0.0, None, ALU.is_lt).then_inc(S["r_link"], 1)
                    e.wait_ge(S["r_link"], lb + 3)
                    e.tensor_tensor(t_(7), t_(6), t_(4), ALU.mult).then_inc(S["r_cun"], 1)
                if q == R_SEL:
                    count = fixed(e, B + 1)
                    e.wait_ge(S["r_ssel"], count)
                    if some(B):
                        e.wait_ge(S["r_cT"], B)
                    e.tensor_scalar(rs[:, 4, :], rs[:, 3, :], 1e-20, None, ALU.add).then_inc(S["r_link"], 1)
                    e.wait_ge(S["r_link"], lb + 4)
                    e.tensor_tensor(rs[:, 4, :], rs[:, 4, :], pw[:, 1:3], ALU.pow).then_inc(S["r_link"], 1)
                    count = fixed(e, lb + 5)
                    e.wait_ge(S["r_link"], count)
                    e.tensor_scalar(rt[:, 1, 0, 0:E], rt[:, 7, 0, 0:E], rs[:, 4, 0:1], None, ALU.mult)
                    e.tensor_scalar(rt[:, 1, 1, 0:E], rt[:, 7, 1, 0:E], rs[:, 4, 1:2], None, ALU.mult).then_inc(S["r_link"], 1)
                    count = fixed(e, lb + 6)
                    e.wait_ge(S["r_link"], count)
                    e.tensor_copy(c3[:, :, 0:E], t_(1)).then_inc(S["r_link"], 1)
                    e.wait_ge(S["r_link"], lb + 7)
                    e.tensor_tensor(t_(2), t_(1), c3[:, :, 0:E], ALU.subtract)
                    e.tensor_tensor(t_(3), t_(1), c3[:, :, 0:E], ALU.subtract).then_inc(S["r_link"], 1)
                    count = fixed(e, lb + 8)
                    e.wait_ge(S["r_link"], count)
                    e.tensor_copy(c3[:, :, E:2 * E], t_(2)).then_inc(S["r_link"], 1)
                    e.wait_ge(S["r_link"], lb + 9)
                    e.tensor_tensor(c3[:, :, 2 * E:3 * E], t_(3), c3[:, :, E:2 * E], ALU.subtract).then_inc(S["r_c3"], 1)
                for j in at_slot(q, M_SPLIT):
                    e.wait_ge(S["m_hi"], NF * B + j + 1)
                    e.tensor_tensor(act_lo[:, j % 2, :], act[:, j % 3, :], act_hi[:, j % 2, :].bitcast(F32), ALU.subtract).then_inc(S["m_lo"], 1)

            def pw32(one):
                return pw[:, 1:2].rearrange("p (a b) -> p a b", a=1).broadcast_to([P, 2, E])

            def rest(s, prep, n, npar, B, q):
                k = prep_piece(prep, s)
                if k is not None:
                    e.wait_ge(S["prep_hi"], k + 1)
                    src, hi, lo = prep_views(k)
                    e.tensor_tensor(lo, src, hi.bitcast(F32), ALU.subtract).then_inc(S["prep_lo"], 1)
                if n is not None:
                    attn(s, n, npar)
                if B is not None:
                    moe(q, B)

            program(e, gru, rest)


def kernel(x, cond_2048, L0_cond_W_ih, L0_cond_W_hh, L0_cond_b_ih, L0_cond_b_hh, L0_attn_w_gate, L0_attn_norm_gate,
           L0_attn_w_down, L0_attn_norm_down, L0_ffn_gate_w, L0_ffn_w13, L0_ffn_w2, L0_ffn_sw13, L0_ffn_sw2):
    import numpy as np
    import ml_dtypes
    import concourse.bacc as bacc
    from concourse.bass_utils import run_bass_kernel_spmd as run

    f = np.ascontiguousarray
    x, cond = np.asarray(x), np.asarray(cond_2048)
    tokens = x.transpose(1, 0, 2).reshape(T * NB, D)

    def by_chunk(a):
        return f(a.reshape(-1, P, a.shape[1]).transpose(1, 0, 2))

    w13, w2 = np.asarray(L0_ffn_w13), np.asarray(L0_ffn_w2)
    sw13, sw2 = np.asarray(L0_ffn_sw13), np.asarray(L0_ffn_sw2)
    gu = np.zeros((2, NF * P, D), np.float32)
    gu[0, :ROWS], gu[1, :ROWS] = w13[:, :EI].reshape(ROWS, D), w13[:, EI:].reshape(ROWS, D)
    gu[0, ROWS:ROWS + SI], gu[1, ROWS:ROWS + SI] = sw13[:SI], sw13[SI:]
    down = np.zeros((NF * P, D), np.float32)
    down[:ROWS], down[ROWS:ROWS + SI] = w2.transpose(0, 2, 1).reshape(ROWS, D), sw2.T
    w13_l = gu.reshape(2, NF, P, NC, P).transpose(4, 1, 0, 3, 2).reshape(P, NF, 512)
    w2_l = down.reshape(NF, P, D).transpose(1, 0, 2).reshape(P, NF * D)
    wg = np.asarray(L0_attn_w_gate).T.reshape(NC, P, 2 * FF).transpose(1, 0, 2).reshape(P, 4, FF)
    wd = np.zeros((FC * P, D), np.float32)
    wd[:FF] = np.asarray(L0_attn_w_down).T
    wd = wd.reshape(FC, P, D).transpose(1, 0, 2).reshape(P, 2, 768)
    sel = np.tile(np.repeat(np.eye(E), EI, axis=1), (3, 1)).astype(ml_dtypes.bfloat16)
    ins = {
        "xT": by_chunk(tokens.T), "xtok": f(tokens.reshape(TILES, P, D)),
        "w_ih": by_chunk(np.asarray(L0_cond_W_ih)), "w_hh": by_chunk(np.asarray(L0_cond_W_hh)),
        "condT": by_chunk(cond.T),
        "b_ih": f(np.asarray(L0_cond_b_ih).reshape(6, P).T), "b_hh": f(np.asarray(L0_cond_b_hh).reshape(6, P).T),
        "wgT": f(wg), "wdT": f(wd),
        "ng": f(np.asarray(L0_attn_norm_gate).reshape(1, D)), "nd": f(np.asarray(L0_attn_norm_down).reshape(1, FF)),
        "gwT": by_chunk(np.asarray(L0_ffn_gate_w).T), "w13": f(w13_l), "w2": f(w2_l),
        "sel": f(sel), "idf": np.eye(P, dtype=np.float32), "idb": np.eye(P).astype(ml_dtypes.bfloat16),
    }
    nc = bacc.Bacc("TRN2", target_bir_lowering=False, num_devices=1, dynamic_dma_scratch_size=1024)
    aps = {n: nc.dram_tensor(f"in_{n}", a.shape, mybir.dt.from_np(a.dtype), kind="ExternalInput").ap() for n, a in ins.items()}
    out = nc.dram_tensor("out_0", (TILES, P, D), F32, kind="ExternalOutput").ap()
    adaln_kernel(nc, out=out, **aps)
    r = run(nc, [{f"in_{n}": a for n, a in ins.items()}], core_ids=[0])
    y = r.results[0]["out_0"]
    return f(y.reshape(T, NB, D).transpose(1, 0, 2))
```

```python
from contextlib import ExitStack

import concourse.bass as bass
from concourse import mybir

F32 = mybir.dt.float32
F32R = mybir.dt.float32r
F16 = mybir.dt.float16
BF16 = mybir.dt.bfloat16
ALU = mybir.AluOpType
ACT = mybir.ActivationFunctionType
X = mybir.AxisListType.X

P = 128
D = 256
NC = D // P
NB = 4
T = 256
STEPS = P // NB
TILES = T // STEPS
FF = 704
FC = 6
UNITS = ((0, 256), (256, 256), (512, 192))
E, TOPK, EI = 16, 6, 176
ROWS = E * EI
SI = 2 * EI
NF = (ROWS + SI + P - 1) // P
NSH = NF - ROWS // P
ORDER = [*range(ROWS // P, NF), *range(ROWS // P)]
BLOCK = 2 * P
BLOCKS = TILES // 2
RING = 16
KK = 4
HALO = NB * (KK - 1)

WS = 256.0
MAGIC = 12582912.0
EPS_NORM, EPS_Q, QMAX = 1e-8, 1e-5, 127.0

S_HT, S_STAT, S_AMAX, S_MAG, S_Q, S_QT = 1, 2, 3, 5, 6, 7
S_UNIT = (8, 11, 14)
S_K2, S_MAG2, S_Q2, S_Q2T, S_DOWN, S_X1T = 18, 21, 22, 23, 24, 25
S_CONV, S_HALO = (26, 27, 28, 29), 30
R_LOG, R_DIFF, R_SIG, R_EXP, R_SUM, R_P, R_TOP, R_REP, R_SEL, R_C3, R_CT = 0, 0, 1, 2, 3, 4, 5, 6, 7, 8, 11
M_G, M_U, M_SIG, M_T2, M_C, M_A, M_SPLIT = 0, 1, 2, 3, 3, 4, 5
M_OUT = ((7, 8, 8), (6, 6, 7), (6, 7, 8), (7, 8, 9))
WARM = {0: 4, 1: 4, 58: 4, 59: 4, 60: 4, 61: 4, 62: 4, 63: 4}
FIRST_WARM = {29: 6, 30: 12, 31: 12}
M_RESULT, M_KEEP = 6, 7


def start(j):
    return 2 + (9 * j) // 4


def at_slot(q, after, B, lo=0):
    slot = [start(j) + (after if isinstance(after, int) else after[j % 4]) for j in range(NF)]
    last = [(j, B - 1) for j in range(lo, NF) if slot[j] == q + 2 * STEPS and not (isinstance(B, int) and B == 0)]
    return last + [(j, B) for j in range(lo, NF) if slot[j] == q and not (isinstance(B, int) and B >= BLOCKS)]


def kept(n, B):
    return n // 2 if isinstance(n, int) else B + 1


PREP = NF + (NF + 1) // 2
PREP_AT = [q for q in range(38, 3 * STEPS) if q % STEPS not in (3, 4, *range(17, 23))][:PREP]
GROUP = 2 * P
GROUPS = T * NB // GROUP
GI_AT = 3
Q_ABS, Q_SUM, Q_RED, Q_CLIP, Q_INV, Q_DIV, Q_TERN = 0, 6, 7, 8, 9, 10, 11
SS, AM, VAR, RR, MC, RC, K1, OSC, O2, VAR2, R2, OR2, AMX, MC2, RC2, K2, OSC2 = range(17)
SS2, AM2 = 17, 20
LINK1, LINK2, LINKR = 6, 11, 3


def adaln_kernel(nc, xT, xtok, w_ih, w_hh, condT, b_ih, b_hh, wgT, wdT, ng, nd, gwT, w13, w2, sel, idf, idb, out):
    ctx = ExitStack()
    with ctx:
        def sb(name, shape, dt):
            return ctx.enter_context(nc.sbuf_tensor(name, shape, dt))

        def pb(name, shape, dt):
            return ctx.enter_context(nc.psum_tensor(name, shape, dt))

        def sem(name):
            return ctx.enter_context(nc.semaphore(name))

        whh_hi, whh_lo = sb("whh_hi", [P, NC, 768], F16), sb("whh_lo", [P, NC, 768], F16)
        tg, td = sb("tg", [P, NC, 2 * FF], BF16), sb("td", [P, FC, D], BF16)
        identf, identb = sb("identf", [P, P], F32), sb("identb", [P, P], BF16)
        selb = sb("selb", [48, ROWS], BF16)
        ng_b, nd_b = sb("ng_b", [P, D], F32), sb("nd_b", [P, FF], F32)
        cond = sb("cond", [P, NC, NB], F32)
        gw = sb("gw", [P, NC, E], F32)
        ones = sb("ones", [P, P], F32)
        pw = sb("pw", [P, 32], F32)
        qp, qm = sb("qp", [P, 6], F32), sb("qm", [P, 2], F32)
        qc = sb("qc", [P, 3, 2], F32)
        gi = sb("gi", [P, 2, STEPS, 24], F32)
        bias = sb("bias", [P, 2, 6], F32)
        bsc = sb("bsc", [P, 2, 6], F32)
        tmpl = sb("tmpl", [P, 8, 2], F32)
        n_mul = sb("n_mul", [P, 8, 3], F32)
        n_sum = sb("n_sum", [P, 8, 3], F32)
        h_mul = sb("h_mul", [P, 8, 3], F32)
        steps = sb("steps", [P, RING, 25], F32)
        h16 = sb("h16", [P, 2, 24], F16)
        hist = sb("hist", [P, 2, NC, P], F32)
        hw, qb, qT = sb("hw", [P, D], F32), sb("qb", [P, D], BF16), sb("qT", [P, NC, P], BF16)
        junk = sb("junk", [P, D], F32)
        sg = sb("sg", [P, 256], F32)
        v = sb("v", [P, FF], F32)
        q2b, q2T = sb("q2b", [P, FF], BF16), sb("q2T", [P, FC, P], BF16)
        sm = sb("sm", [P, 24], F32)
        xt = sb("xt", [P, 2, D], F32)
        x1, x1b, yt = sb("x1", [P, 2, D], F32), sb("x1b", [P, 2, D], F32), sb("yt", [P, 2, D], F32)
        x1T = sb("x1T", [P, NC, HALO + 2 * P], F32)
        xc = sb("xc", [P, NC, BLOCK], F32)
        xc_hi, xc_lo = sb("xc_hi", [P, NC, BLOCK], F32R), sb("xc_lo", [P, NC, BLOCK], F32R)
        cT = sb("cT", [48, BLOCK], BF16)
        c3 = sb("c3", [P, 2, 3 * E], BF16)
        rt = sb("rt", [P, 8, 2, E + 2], F32)
        rs = sb("rs", [P, 8, 2], F32)
        m8 = sb("m8", [P, 2, 8], F32)

        base = nc.sbuf_base if not callable(nc.sbuf_base) else nc.sbuf_base()
        base = (int(base) + 63) // 64 * 64
        w13_bytes, w2_bytes = NF * 512 * 4, NF * 256 * 4
        arena = sb("arena", [P, (2 * w13_bytes + 2 * w2_bytes + 7 * BLOCK * 4 + 64) // 4], F32)

        place = [base]

        def at(name, shape, dt, size):
            t = nc.alloc_sbuf_tensor_at(name, shape, dt, offset=place[0])
            place[0] += size
            return t

        w13_hi = at("w13_hi", [P, NF, 2, NC, P], F32R, w13_bytes)
        w13_lo = at("w13_lo", [P, NF, 2, NC, P], F32R, w13_bytes)
        w2_hi = at("w2_hi", [P, NF, D], F32R, w2_bytes)
        w2_lo = at("w2_lo", [P, NF, D], F32R, w2_bytes)
        act = at("act", [P, 3, BLOCK], F32, 3 * BLOCK * 4)
        act_hi, act_lo = at("act_hi", [P, 2, BLOCK], F32R, 2 * BLOCK * 4), at("act_lo", [P, 2, BLOCK], F32R, 2 * BLOCK * 4)
        place[0] -= 7 * BLOCK * 4
        stage = at("stage", [P, 3, 512], F32, 6144)
        place[0] = base
        xf = at("xf", [P, NC, 1024], F32, 8192)
        xh = at("xh", [P, NC, 1024], F32R, 8192)
        xl = at("xl", [P, NC, 1024], F32R, 8192)
        wf = at("wf", [P, NC, 768], F32, 6144)
        wh = at("wh", [P, NC, 768], F32R, 6144)
        wl = at("wl", [P, NC, 768], F32R, 6144)
        whf = at("whf", [P, NC, 768], F32, 6144)
        zer = at("zer", [P, 512], BF16, 1024)
        place[0] = base + 2 * w13_bytes
        wgf = at("wgf", [P, 4, FF], F32, 11264)
        wdf = at("wdf", [P, 2, 768], F32, 6144)
        place[0] = base + 2 * w13_bytes + w2_bytes
        gis = at("gis", [P, T - 2 * STEPS, 24], F32, (T - 2 * STEPS) * 96)

        bR, bZ = pb("bR", [P, 512], F32), pb("bZ", [P, 512], F32)
        bN = pb("bN", [P, 512], F32)
        bA = pb("bA", [P, 512], F32)
        bM = [pb("bM0", [P, 512], F32), pb("bM1", [P, 512], F32)]
        bC = pb("bC", [P, 512], F32)
        bO = pb("bO", [P, 512], F32)
        R = bR[:, 0:RING * 8].rearrange("p (s c b) -> p s c b", s=RING, c=NC)
        Z = bZ[:, 0:RING * 8].rearrange("p (s c b) -> p s c b", s=RING, c=NC)
        N = bN[:, 0:RING * 24].rearrange("p (s c b e) -> p s c b e", s=RING, c=NC, e=3)
        bA16 = bA[:, :].bitcast(BF16)
        bC16 = bC[:, :].bitcast(BF16)

        gi_banks = (bM[0], bM[1], bC, bO)
        gi_dram = nc.dram_tensor("gi_scratch", [TILES + 1, P, STEPS * 24], F32, kind="Internal").ap()

        names = """ld_whh ld_x ld_const ld_quant x_split w_split x_hi w_hi gi_pe gi_ev gi_out gi_in0 gi_in1 gi_used
            setup zero banks_set x_low ld_w0 ld_w1 ld_x0 b_scaled whh_high h0_high whh_split
            r_ready n_ready z_ready r_done z_done n_summed n_done h_hi h_full h_lo hist_done
            q_abs q_pe q_step q_tern
            st_in0 st_in1 st_in2 prep_hi prep_lo
            ht_pe sq_act hw_dve amax_dve k_pool mag_dve q_dve qT_pe qT_act
            gu_pe sg_act gt_dve v_dve sq2_act vw_pool max2_dve k2_pool mag2_dve q2_dve q2T_pe q2T_act
            down_pe x1_dve x1T_pe x1T_act conv_dve halo_act x1_kept xhi_act xlo_pool
            xt_in0 xt_in1 sm_link r_link
            r_log r_max r_d r_sig r_e r_inv r_sum r_isum r_p r_m8 r_m8set r_rep r_chosen r_csum r_guard r_icsum r_c r_c3 r_cT r_cT_act
            m_g m_u m_c m_sig m_t m_t2 m_a m_hi m_lo m_o y_done y_out""".split()
        S = {n: sem(n) for n in names}
        block = ctx.enter_context(nc.Block())

        def some(count):
            return not isinstance(count, int) or count > 0

        def fixed(e, count):
            if isinstance(count, int):
                return count
            count = e.snap(e.to_reg(count))
            e.wait_ge(S["setup"], 1)
            return count

        def opened(B):
            return not (isinstance(B, int) and B >= BLOCKS)

        def flat(ap):
            return ap.rearrange("p a b -> p (a b)")

        def program(e, gru, rest):
            def half(i, par, prep=None, with_gru=True, attn=True, moe=True):
                m = 2 * i + par
                for s in range(STEPS):
                    if with_gru:
                        gru(m, par, s)
                    B, q = (i - 1, s) if par else (i - 2, STEPS + s)
                    rest(s, prep, m - 1 if attn else None, 1 - par, B if moe else None, q)
            half(0, 0, prep=0, attn=False, moe=False)
            half(0, 1, prep=1, moe=False)
            half(1, 0, prep=2, moe=False)
            half(1, 1)
            with e.Fori(2, TILES // 2) as i:
                half(i, 0)
                half(i, 1)
            half(TILES // 2, 0, with_gru=False)
            half(TILES // 2, 1, with_gru=False, attn=False)
            half(TILES // 2 + 1, 0, with_gru=False, attn=False)
            for q in range(M_RESULT + 1):
                rest(q, None, None, 0, BLOCKS, q)

        def prep_piece(prep, s):
            return PREP_AT.index(STEPS * prep + s) if prep is not None and STEPS * prep + s in PREP_AT else None

        def gi_piece(prep, s):
            k = -1 if prep is None else STEPS * prep + s - GI_AT
            return (1 + k // 12, k // 2 % 6, k % 2) if 0 <= k < 12 * (GROUPS - 1) else None

        def prep_views(k):
            if k < NF:
                return (stage[:, k % 3, :].rearrange("p (g c f) -> p g c f", g=2, c=NC), w13_hi[:, k], w13_lo[:, k])
            f = 2 * (k - NF)
            n = min(2, NF - f)
            return (stage[:, k % 3, 0:n * D].rearrange("p (f d) -> p f d", f=n), w2_hi[:, f:f + n, :], w2_lo[:, f:f + n, :])

        def released(j, B):
            return ("m_a", NF * B + j + 1) if j < NSH else ("m_t2", (NF - NSH) * B + j - NSH + 1)

        @block.sync
        def _(e):
            e.dma_start(xf[:, :, 0:GROUP], xT[:, :, 0:GROUP]).then_inc(S["ld_x0"], 16)
            e.dma_start(wf[:, :, 0:384], w_ih[:, :, 0:384]).then_inc(S["ld_w0"], 16)
            e.dma_start(wf[:, :, 384:768], w_ih[:, :, 384:768]).then_inc(S["ld_w1"], 16)
            e.dma_start(whf[:, :, :], w_hh).then_inc(S["ld_whh"], 16)
            e.dma_start(cond[:, :, :], condT).then_inc(S["ld_whh"], 16)
            e.dma_start(bias[:, 0, :], b_ih).then_inc(S["ld_whh"], 16)
            e.dma_start(bias[:, 1, :], b_hh).then_inc(S["ld_whh"], 16)
            e.dma_start(xf[:, :, GROUP:1024], xT[:, :, GROUP:1024]).then_inc(S["ld_x"], 16)
            e.dma_start(wgf[:, :, :], wgT).then_inc(S["ld_quant"], 16)
            e.dma_start(wdf[:, :, :], wdT).then_inc(S["ld_quant"], 16)
            e.dma_start(identf[:, :], idf).then_inc(S["ld_const"], 16)
            e.dma_start(identb[:, :], idb).then_inc(S["ld_const"], 16)
            e.dma_start(selb[:, :], sel).then_inc(S["ld_const"], 16)
            e.dma_start(gw[:, :, :], gwT).then_inc(S["ld_const"], 16)
            e.dma_start(ng_b[:, :], ng.broadcast_to([P, D])).then_inc(S["ld_const"], 16)
            e.dma_start(nd_b[:, :], nd.broadcast_to([P, FF])).then_inc(S["ld_const"], 16)
            def tile(dram, n):
                return dram[n] if isinstance(n, int) else dram[bass.ds(n, 1), :, :].rearrange("a p f -> (a p) f")

            def loads(m, par, gru=True, attn=True):
                if gru:
                    e.wait_ge(S["gi_used"], m)
                    e.dma_start(flat(gi[:, 1 - par, :, :]), tile(gi_dram, m + 1)).then_inc(S[f"gi_in{1 - par}"], 16)
                if attn:
                    if some(m - 2):
                        e.wait_ge(S["x1_dve"], m - 2)
                    e.dma_start(xt[:, 1 - par, :], tile(xtok, m - 1)).then_inc(S[f"xt_in{1 - par}"], 16)

            def result(B):
                e.wait_ge(S["y_done"], B + 1)
                for k in range(2):
                    e.dma_start(tile(out, 2 * B + k), yt[:, k, :]).then_inc(S["y_out"], 16)

            def prep_load(k):
                if k >= 3:
                    e.wait_ge(S["prep_lo"], k - 2)
                src = w13[:, k, :] if k < NF else w2[:, 512 * (k - NF):min(512 * (k - NF + 1), NF * D)]
                e.dma_start(stage[:, k % 3, 0:src.shape[1]], src).then_inc(S[f"st_in{k % 3}"], 16)

            for k in range(3):
                prep_load(k)
            for g in range(1, GROUPS):
                e.wait_ge(S["gi_ev"], 6 * (g + 1))
                for k in range(2):
                    o = 2 * STEPS * (g - 1) + STEPS * k
                    e.dma_start(gi_dram[2 * g + k], flat(gis[:, o:o + STEPS, :])).then_inc(S["gi_out"], 16)
                if g == 1:
                    e.wait_ge(S["gi_out"], 32)
                    loads(1, 1)
            e.dma_start(gi_dram[TILES], flat(gis[:, T - 3 * STEPS:T - 2 * STEPS, :])).then_inc(S["gi_out"], 16)
            for k in range(3, PREP):
                prep_load(k)
            e.wait_ge(S["gi_out"], 16 * (TILES - 1))
            loads(2, 0)
            loads(3, 1)
            with e.Fori(2, TILES // 2) as i:
                loads(2 * i, 0)
                loads(2 * i + 1, 1)
                result(i - 2)
            loads(TILES, 0, gru=False)
            result(2)
            result(3)
            e.wait_ge(S["y_out"], 16 * TILES)

        @block.tensor
        def _(e):
            e.wait_ge(S["zero"], 1)
            for bank in (bR, bZ, bN):
                mm = e.matmul(bank[:, :], zer[:, 0:P], zer[:, :], start=True, stop=True)
            mm.then_inc(S["banks_set"], 1)
            def project(g, m6, terms=range(3 * NC)):
                q = 6 * g + m6
                for t in terms:
                    if g == 0 and m6 % 3 == 0 and t == 0:
                        e.wait_ge(S["x_hi"], 1)
                        e.wait_ge(S["w_hi"], 1 + m6 // 3)
                    if g == 0 and m6 == 0 and t == NC:
                        e.wait_ge(S["x_split"], 1)
                    if g == 0 and m6 % 3 == 0 and t == 2 * NC:
                        e.wait_ge(S["w_split"], 1 + m6 // 3)
                    if g > 0 and m6 == 0 and t == 0:
                        e.wait_ge(S["x_low"], g)
                    if t == 0 and q > 3:
                        e.wait_ge(S["gi_ev"], q - 3)
                    (wt, xp), k = ((wh, xh), (wh, xl), (wl, xh))[t // NC], t % NC
                    mm = e.matmul(gi_banks[q % 4][:, 0:GROUP], wt[:, k, m6 * P:(m6 + 1) * P], xp[:, k, GROUP * g:GROUP * (g + 1)],
                                  start=(t == 0), stop=(t == 3 * NC - 1))
                    if t == 3 * NC - 1:
                        mm.then_inc(S["gi_pe"], 1)

            for m6 in range(6):
                project(0, m6)
            e.wait_ge(S["whh_split"], 1)

            def gate(out_of, g, wts, part):
                for c in range(NC):
                    for k in range(NC):
                        for wt in wts:
                            mm = e.matmul(out_of(c), wt[:, k, g * D + c * P:g * D + (c + 1) * P],
                                          h16[:, part, 12 * k + 2:12 * k + 12:3],
                                          start=False, stop=False, skip_group_check=True)
                return mm

            def gru(m, par, s):
                n, slot = 32 * m + s, s % RING
                r_of, z_of = lambda c: R[:, slot, c, :], lambda c: Z[:, slot, c, :]
                e.wait_ge(S["h_hi"], n + 1)
                gate(r_of, 0, (whh_hi, whh_lo), 0)
                gate(lambda c: N[:, slot, c, :, 0], 2, (whh_lo,), 0)
                e.wait_ge(S["h_lo"], n + 1)
                gate(r_of, 0, (whh_hi,), 1).then_inc(S["r_ready"], 1)
                for c in range(NC):
                    for k in range(NC):
                        mm = e.matmul(N[:, slot, c, :, 0:2].rearrange("p b e -> p e b"),
                                      whh_hi[:, k, 2 * D + c * P:2 * D + (c + 1) * P],
                                      h16[:, :, 12 * k + 2:12 * k + 12:3],
                                      start=False, stop=False, skip_group_check=True)
                mm.then_inc(S["n_ready"], 1)
                gate(z_of, 1, (whh_hi, whh_lo), 0)
                gate(z_of, 1, (whh_hi,), 1).then_inc(S["z_ready"], 1)

            def attn(s, n, npar, B):
                if s == S_HT:
                    if npar == 0 and some(kept(n, B)):
                        e.wait_ge(S["r_d"], kept(n, B))
                    e.wait_ge(S["hist_done"], 4 * n + 4)
                    if some(n):
                        e.wait_ge(S["x1T_act"], n)
                    for c in range(NC):
                        mm = e.transpose(bA[:, c * P:(c + 1) * P], hist[:, npar, c, :], identf[:, :])
                    mm.then_inc(S["ht_pe"], 1)
                if s == S_QT:
                    e.wait_ge(S["q_dve"], n + 1)
                    for c in range(NC):
                        mm = e.transpose(bA16[:, c * P:(c + 1) * P], qb[:, c * P:(c + 1) * P], identb[:, :])
                    mm.then_inc(S["qT_pe"], 1)
                for u, (off, w) in enumerate(UNITS):
                    if s == S_UNIT[u]:
                        if u == 0:
                            e.wait_ge(S["qT_act"], n + 1)
                            e.wait_ge(S["q_tern"], 6)
                        else:
                            e.wait_ge(S["v_dve"], 3 * n + u)
                        for g in range(2):
                            for k in range(NC):
                                mm = e.matmul(bA[:, 256 * g:256 * g + w], qT[:, k, :], tg[:, k, FF * g + off:FF * g + off + w],
                                              start=(k == 0), stop=(k == NC - 1))
                        mm.then_inc(S["gu_pe"], 1)
                if s == S_Q2T:
                    e.wait_ge(S["q2_dve"], n + 1)
                    for c in range(FC):
                        w = min(P, FF - c * P)
                        mm = e.transpose(bA16[0:w, c * P:(c + 1) * P], q2b[:, c * P:c * P + w], identb[:, :])
                    mm.then_inc(S["q2T_pe"], 1)
                if s == S_DOWN:
                    e.wait_ge(S["q2T_act"], n + 1)
                    for c in range(FC):
                        w = min(P, FF - c * P)
                        mm = e.matmul(bA[:, 0:D], q2T[0:w, c, :], td[0:w, c, :], start=(c == 0), stop=(c == FC - 1))
                    mm.then_inc(S["down_pe"], 1)
                if s == S_X1T:
                    e.wait_ge(S["x1_dve"], n + 1)
                    for c in range(NC):
                        mm = e.transpose(bA[:, c * P:(c + 1) * P], x1[:, npar, c * P:(c + 1) * P], identf[:, :])
                    mm.then_inc(S["x1T_pe"], 1)

            def keep_warm(count):
                for _ in range(count):
                    e.matmul(bM[1][:, 0:256], identb[:, :], tg[:, 0, 0:256], start=True, stop=True)

            def moe(q, B):
                if q in WARM and opened(B):
                    if q == min(w for w in WARM if w >= STEPS):
                        e.wait_ge(S["m_t2"], (NF - NSH) * (B + 1) - 1)
                    keep_warm(WARM[q])
                if q == R_LOG and opened(B):
                    e.wait_ge(S["conv_dve"], 8 * (2 * B + 2))
                    for t in range(2):
                        for c in range(NC):
                            mm = e.matmul(bA[:, t * E:(t + 1) * E], xc[:, c, t * P:(t + 1) * P], gw[:, c, :],
                                          start=(c == 0), stop=(c == NC - 1))
                    mm.then_inc(S["r_log"], 1)
                if q == R_CT and opened(B):
                    count = fixed(e, B + 1)
                    e.wait_ge(S["r_c3"], count)
                    if some(NF * B):
                        e.wait_ge(S["m_a"], NF * B)
                    for t in range(2):
                        mm = e.transpose(bC16[0:48, t * P:(t + 1) * P], c3[:, t, :], identb[:, :])
                    mm.then_inc(S["r_cT"], 1)
                for stage_at, gu, done in ((M_G, 0, "m_g"), (M_U, 1, "m_u")):
                    for j, B_ in at_slot(q, stage_at, B):
                        f, bank = ORDER[j], bM[j % 2]
                        if gu == 0 and j == 0:
                            e.wait_ge(S["xhi_act"], B_ + 1)
                            e.wait_ge(S["xlo_pool"], B_ + 1)
                            e.wait_ge(S["prep_lo"], PREP)
                            if some((NF - NSH) * B_):
                                e.wait_ge(S["m_t2"], (NF - NSH) * B_)
                        if gu == 0 and j >= 2:
                            name, count = released(j - 2, B_)
                            e.wait_ge(S[name], count)
                        terms = [(wt, xp, k) for wt, xp in ((w13_hi, xc_hi), (w13_lo, xc_hi), (w13_hi, xc_lo)) for k in range(NC)]
                        for t, (wt, xp, k) in enumerate(terms):
                            mm = e.matmul(bank[:, 256 * gu:256 * gu + 256], wt[:, f, gu, k, :], xp[:, k, :],
                                          start=(t == 0), stop=(t == len(terms) - 1))
                        mm.then_inc(S[done], 1)
                for j, B_ in at_slot(q, M_C, B, NSH):
                    if (j - NSH) % 2 == 0:
                        if j == NSH:
                            e.wait_ge(S["r_cT_act"], B_ + 1)
                        else:
                            e.wait_ge(S["m_a"], NF * B_ + j)
                        for d in range(2):
                            mm = e.matmul(bC[:, 256 * d:256 * d + 256], selb[:, (j + d - NSH) * P:(j + d - NSH + 1) * P], cT[:, :],
                                          start=True, stop=True)
                        mm.then_inc(S["m_c"], 1)
                for piece, wt in enumerate((w2_hi, w2_lo, w2_hi)):
                    for j, B_ in at_slot(q, [o[piece] for o in M_OUT], B):
                        if piece == 0:
                            if j == 0 and some(B_):
                                e.wait_ge(S["y_done"], B_)
                            e.wait_ge(S["m_hi"], NF * B_ + j + 1)
                        if piece == 2:
                            e.wait_ge(S["m_lo"], NF * B_ + j + 1)
                        part = act_lo if piece == 2 else act_hi
                        for t in range(2):
                            mm = e.matmul(bO[:, t * D:(t + 1) * D], part[:, j % 2, t * P:(t + 1) * P], wt[:, ORDER[j], :],
                                          start=(j == 0 and t == 0 and piece == 0), stop=(j == NF - 1 and piece == 2),
                                          skip_group_check=True)
                        if piece == 2:
                            mm.then_inc(S["m_o"], 1)

            def rest(s, prep, n, npar, B, q):
                if prep == 1 and s == 0:
                    e.wait_ge(S["ld_const"], 96)
                if gi_piece(prep, s):
                    g, m6, second = gi_piece(prep, s)
                    project(g, m6, range(3 * second, 3 * second + 3))
                if prep == 0 and s == Q_SUM:
                    e.wait_ge(S["q_abs"], 6)
                    e.wait_ge(S["setup"], 1)
                    e.matmul(bA[:, 0:6], ones[:, :], qp[:, :], start=True, stop=True).then_inc(S["q_pe"], 1)
                if prep == 2 and s in FIRST_WARM:
                    keep_warm(FIRST_WARM[s])
                if n is not None:
                    attn(s, n, npar, B)
                if B is not None:
                    moe(q, B)

            program(e, gru, rest)

        @block.scalar
        def _(e):
            e.wait_ge(S["zero"], 3)
            e.activation(junk[:, 0:1], h_mul[:, 0, 0:1], ACT.Sigmoid)
            e.wait_ge(S["ld_x0"], 16)
            e.activation(xh[:, :, 0:GROUP], xf[:, :, 0:GROUP], ACT.Copy).then_inc(S["x_hi"], 1)
            e.wait_ge(S["ld_w0"], 16)
            e.activation(wh[:, :, 0:384], wf[:, :, 0:384], ACT.Copy).then_inc(S["w_hi"], 1)
            e.wait_ge(S["ld_w1"], 16)
            e.activation(wh[:, :, 384:768], wf[:, :, 384:768], ACT.Copy).then_inc(S["w_hi"], 1)
            e.wait_ge(S["b_scaled"], 2)

            def projected(g, m6):
                q = 6 * g + m6
                dst = gi[:, :, :, 4 * m6:4 * m6 + 4].rearrange("p t s b -> p (t s) b") if g == 0 else \
                    gis[:, 2 * STEPS * (g - 1):2 * STEPS * g, 4 * m6:4 * m6 + 4]
                e.wait_ge(S["gi_pe"], q + 1)
                e.activation(dst, gi_banks[q % 4][:, 0:GROUP].rearrange("p (s b) -> p s b", b=NB),
                             ACT.Identity, scale=WS, bias=bsc[:, 0, m6:m6 + 1]).then_inc(S["gi_ev"], 1)

            for m6 in range(6):
                projected(0, m6)

            def gru(m, par, s):
                n, slot = 32 * m + s + 1, s % RING
                e.wait_ge(S["r_ready"], n)
                e.activation(n_mul[:, :, 2], flat(R[:, slot, :, :]), ACT.Sigmoid, scale=1 / WS).then_inc(S["r_done"], 1)
                e.wait_ge(S["z_ready"], n)
                e.activation(h_mul[:, :, 2], flat(Z[:, slot, :, :]), ACT.Sigmoid, scale=1 / WS).then_inc(S["z_done"], 1)
                e.wait_ge(S["n_summed"], n)
                e.activation(steps[:, slot, 1:25].rearrange("p (a b) -> p a b", b=3)[:, :, 0:3:2],
                             n_sum[:, :, 2:3].broadcast_to([P, 8, 2]), ACT.Tanh, scale=1 / WS).then_inc(S["n_done"], 1)

            def attn(s, n, npar):
                if s == S_STAT:
                    e.wait_ge(S["ht_pe"], n + 1)
                    e.activation(junk[:, :], bA[:, 0:D], ACT.Square, accum_out=sm[:, SS:SS + 1]).then_inc(S["sq_act"], 1)
                if s == S_QT:
                    e.wait_ge(S["qT_pe"], n + 1)
                    e.activation(flat(qT[:, :, :]), bA16[:, 0:D], ACT.Copy).then_inc(S["qT_act"], 1)
                for u, (off, w) in enumerate(UNITS):
                    if s == S_UNIT[u] + 1:
                        if some(3 * n + u):
                            e.wait_ge(S["gt_dve"], 3 * n + u)
                        e.wait_ge(S["gu_pe"], 3 * n + u + 1)
                        e.activation(sg[:, 0:w], bA[:, 0:w], ACT.Sigmoid, scale=sm[:, OSC:OSC + 1]).then_inc(S["sg_act"], 1)
                    if s == S_UNIT[u] + 3:
                        e.wait_ge(S["v_dve"], 3 * n + u + 1)
                        e.activation(junk[:, 0:w], v[:, off:off + w], ACT.Square,
                                     accum_out=sm[:, SS2 + u:SS2 + u + 1]).then_inc(S["sq2_act"], 1)
                if s == S_Q2T:
                    e.wait_ge(S["q2T_pe"], n + 1)
                    last = FF - (FC - 1) * P
                    e.activation(flat(q2T[:, 0:FC - 1, :]), bA16[:, 0:(FC - 1) * P], ACT.Copy)
                    e.activation(q2T[0:last, FC - 1, :], bA16[0:last, (FC - 1) * P:FC * P], ACT.Copy).then_inc(S["q2T_act"], 1)
                if s == S_X1T:
                    if some(8 * n):
                        e.wait_ge(S["conv_dve"], 8 * n)
                    e.wait_ge(S["x1T_pe"], n + 1)
                    e.activation(x1T[:, :, HALO + npar * P:HALO + npar * P + P], bA[:, 0:D].rearrange("p (c t) -> p c t", c=NC),
                                 ACT.Copy).then_inc(S["x1T_act"], 1)
                if s == S_HALO and npar == 1:
                    e.wait_ge(S["conv_dve"], 8 * n + 8)
                    e.activation(x1T[:, :, 0:HALO], x1T[:, :, BLOCK:BLOCK + HALO], ACT.Copy).then_inc(S["halo_act"], 1)

            def moe(q, B):
                if q == 0 and opened(B):
                    e.wait_ge(S["conv_dve"], 8 * (2 * B + 2))
                    if some(NF * B):
                        e.wait_ge(S["m_u"], NF * B)
                    e.activation(xc_hi[:, :, :], xc[:, :, :], ACT.Copy).then_inc(S["xhi_act"], 1)
                if q == R_SIG and opened(B):
                    e.wait_ge(S["r_d"], B + 1)
                    e.activation(rt[:, 1, :, 0:E], rt[:, 0, :, 0:E], ACT.Sigmoid)
                    e.activation(rt[:, 2, :, 0:E], rt[:, 0, :, 0:E], ACT.Sigmoid, scale=-1.0).then_inc(S["r_sig"], 1)
                if q == R_CT and opened(B):
                    e.wait_ge(S["r_cT"], B + 1)
                    e.activation(cT[:, :], bC16[0:48, 0:BLOCK], ACT.Copy).then_inc(S["r_cT_act"], 1)
                for j, B_ in at_slot(q, M_SIG, B):
                    if some(NF * B_ + max(0, j - 2)):
                        e.wait_ge(S["m_lo"], NF * B_ + max(0, j - 2))
                    e.wait_ge(S["m_u"], NF * B_ + j + 1)
                    e.activation(act[:, j % 3, :], bM[j % 2][:, 0:256], ACT.Sigmoid).then_inc(S["m_sig"], 1)
                for j, B_ in at_slot(q, M_SPLIT, B):
                    if some(NF * B_ + max(0, j - 1)):
                        e.wait_ge(S["m_o"], NF * B_ + max(0, j - 1))
                    e.wait_ge(S["m_a"], NF * B_ + j + 1)
                    e.activation(act_hi[:, j % 2, :], act[:, j % 3, :], ACT.Copy).then_inc(S["m_hi"], 1)

            def rest(s, prep, n, npar, B, q):
                if prep == 0 and s < 2 * (GROUPS - 1) and s % 2 == 0:
                    if s == 0:
                        e.wait_ge(S["ld_x"], 16)
                    cols = slice(GROUP * (1 + s // 2), GROUP * (2 + s // 2))
                    e.activation(xh[:, :, cols], xf[:, :, cols], ACT.Copy).then_inc(S["x_hi"], 1)
                if gi_piece(prep, s) and gi_piece(prep, s)[2]:
                    projected(*gi_piece(prep, s)[:2])
                k = prep_piece(prep, s)
                if k is not None:
                    if k == 0:
                        e.wait_ge(S["gi_pe"], 6 * GROUPS)
                        e.wait_ge(S["whh_split"], 1)
                    if k == NF:
                        e.wait_ge(S["q_tern"], 6)
                        e.wait_ge(S["gi_out"], 16 * (TILES - 1))
                    e.wait_ge(S[f"st_in{k % 3}"], 16 * (k // 3 + 1))
                    src, hi, _ = prep_views(k)
                    e.activation(hi, src, ACT.Copy).then_inc(S["prep_hi"], 1)
                if n is not None:
                    attn(s, n, npar)
                if B is not None:
                    moe(q, B)

            program(e, gru, rest)

        @block.vector
        def _(e):
            e.memset(zer[:, :], 0.0).then_inc(S["zero"], 1)
            e.memset(n_mul[:, :, :], 0.0)
            e.memset(h_mul[:, :, :], 0.0)
            e.memset(h16[:, :, :], 0.0)
            e.memset(tmpl[:, :, :], 0.0)
            e.memset(x1T[:, :, 0:HALO], 0.0)
            e.memset(rt[:, 4, :, E:E + 2], -1.0)
            e.memset(steps[:, :, :], 0.0).then_inc(S["zero"], 1)
            e.wait_ge(S["zero"], 2)
            e.memset(n_mul[:, :, 1], 1.0)
            e.memset(h_mul[:, :, 1], -1.0).then_inc(S["zero"], 1)
            e.wait_ge(S["x_hi"], 1)
            e.tensor_tensor(xl[:, :, 0:GROUP], xf[:, :, 0:GROUP], xh[:, :, 0:GROUP].bitcast(F32), ALU.subtract).then_inc(S["x_split"], 1)
            for k in range(2):
                cols = slice(384 * k, 384 * k + 384)
                e.wait_ge(S["w_hi"], k + 1)
                e.tensor_tensor(wl[:, :, cols], wf[:, :, cols], wh[:, :, cols].bitcast(F32), ALU.subtract).then_inc(S["w_split"], 1)
            e.wait_ge(S["ld_whh"], 64)
            e.tensor_scalar(whh_hi[:, :, :], whf[:, :, :], WS, None, ALU.mult).then_inc(S["whh_high"], 1)
            e.wait_ge(S["whh_high"], 1)
            e.scalar_tensor_tensor(whh_lo[:, :, :], whf[:, :, :], WS, whh_hi[:, :, :], ALU.mult, ALU.subtract).then_inc(S["whh_split"], 1)
            h_at = lambda ap: ap.rearrange("p (c b) -> p c b", c=NC)
            e.tensor_copy(h_at(steps[:, 0, 2:25:3]), cond[:, :, :])
            e.tensor_copy(h_at(h16[:, 0, 2:24:3]), cond[:, :, :]).then_inc(S["h0_high"], 1)
            e.wait_ge(S["h0_high"], 1)
            e.tensor_tensor(h_at(h16[:, 1, 2:24:3]), cond[:, :, :], h_at(h16[:, 0, 2:24:3]), ALU.subtract)
            e.wait_ge(S["b_scaled"], 2)
            for c in range(NC):
                e.tensor_scalar(tmpl[:, 4 * c:4 * c + 4, 0], n_mul[:, 0:4, 1], bsc[:, 1, 4 + c:5 + c], None, ALU.mult)
            e.tensor_scalar(tmpl[:, :, 1], n_mul[:, :, 0], 0.0, None, ALU.mult).then_inc(S["zero"], 1)
            e.wait_ge(S["zero"], 4)
            e.wait_ge(S["banks_set"], 1)
            e.wait_ge(S["gi_ev"], 6)

            def seed(which, par, s):
                src, o, r = gi[:, par if s < STEPS else 1 - par], s % STEPS, s % RING
                if which == 0:
                    return e.tensor_copy(R[:, r:r + 8].rearrange("p s c b -> p s (c b)"), src[:, o:o + 8, 0:8])
                if which == 1:
                    e.tensor_copy(N[:, r:r + 8, :, :, 2].rearrange("p s c b -> p s (c b)"), src[:, o:o + 8, 16:24])
                    return e.tensor_copy(N[:, r:r + 8, :, :, 0:2].rearrange("p s c b e -> p s (c b) e"),
                                         tmpl[:, :, :].rearrange("p (a f) e -> p a f e", a=1).broadcast_to([P, 8, 8, 2]))
                return e.tensor_copy(Z[:, r:r + 8].rearrange("p s c b -> p s (c b)"), src[:, o:o + 8, 8:16])

            seed(0, 0, 0)
            seed(1, 0, 0).then_inc(S["h_hi"], 1)
            seed(2, 0, 0).then_inc(S["h_lo"], 1)

            def gru(m, par, s):
                n, slot, nxt = 32 * m + s + 1, s % RING, (s + 1) % RING
                if s % 8 == 0:
                    if some(4 * m + s // 8 - 1):
                        e.wait_ge(S["hist_done"], 4 * m + s // 8 - 1)
                e.wait_ge(S["r_done"], n)
                e.wait_ge(S["n_ready"], n)
                e.tensor_tensor_scan(flat(n_sum[:, :, :]), flat(n_mul[:, :, :]), N[:, slot].rearrange("p c b e -> p (c b e)"),
                                     0.0, ALU.mult, ALU.add).then_inc(S["n_summed"], 1)
                if s % 8 == 0:
                    if s == STEPS - 8:
                        if some(8 * m + 8 * par):
                            e.wait_ge(S[f"gi_in{1 - par}"], 8 * m + 8 * par)
                    seed(0, par, s + 8)
                if s % 8 == 1:
                    seed(1, par, s + 7)
                if s % 8 == 2:
                    e.wait_ge(S["z_done"], n)
                    last = seed(2, par, s + 6)
                    if s == STEPS - 14:
                        last.then_inc(S["gi_used"], 1)
                e.wait_ge(S["n_done"], n)
                e.wait_ge(S["z_done"], n)
                row, nrow = steps[:, slot, 1:25], steps[:, nxt, 0:24]
                e.tensor_tensor_scan(h16[:, 0, :], flat(h_mul[:, :, :]), row, 0.0, ALU.mult, ALU.add).then_inc(S["h_hi"], 1)
                e.tensor_tensor_scan(nrow, flat(h_mul[:, :, :]), row, 0.0, ALU.mult, ALU.add).then_inc(S["h_full"], 1)
                e.wait_ge(S["h_full"], n)
                e.tensor_tensor(h16[:, 1, 2:24:3], steps[:, nxt, 2:25:3], h16[:, 0, 2:24:3], ALU.subtract).then_inc(S["h_lo"], 1)

            def quant(s):
                src = lambda j: wgf[:, j, :] if j < 4 else wdf[:, j - 4, :]
                if Q_ABS <= s < Q_ABS + 6:
                    if s == Q_ABS:
                        e.wait_ge(S["ld_quant"], 32)
                    e.tensor_reduce(qp[:, s:s + 1], src(s), X, ALU.add, apply_absolute_value=True).then_inc(S["q_abs"], 1)
                if s == Q_RED:
                    e.wait_ge(S["q_pe"], 1)
                    e.tensor_reduce(qm[:, 0:1], bA[:, 0:4], X, ALU.add)
                    e.tensor_reduce(qm[:, 1:2], bA[:, 4:6], X, ALU.add).then_inc(S["q_step"], 1)
                if s == Q_CLIP:
                    e.wait_ge(S["q_step"], 1)
                    e.tensor_scalar(qc[:, 0, 0:1], qm[:, 0:1], 1.0 / (2 * FF * D), EPS_Q, ALU.mult, ALU.max)
                    e.tensor_scalar(qc[:, 0, 1:2], qm[:, 1:2], 1.0 / (FF * D), EPS_Q, ALU.mult, ALU.max).then_inc(S["q_step"], 1)
                if s == Q_INV:
                    e.wait_ge(S["q_step"], 2)
                    e.reciprocal(qc[:, 1, :], qc[:, 0, :]).then_inc(S["q_step"], 1)
                if s == Q_DIV:
                    e.tensor_scalar(qc[:, 2, :], qc[:, 0, :], 1.0 / QMAX, None, ALU.mult).then_inc(S["q_step"], 1)
                if Q_TERN <= s < Q_TERN + 18:
                    o = s - Q_TERN
                    j, step = o // 3, o % 3
                    w = src(j)
                    e.wait_ge(S["q_step"], 4 + 2 * j + step)
                    if step == 0:
                        which = 0 if j < 4 else 1
                        e.tensor_scalar(w, w, qc[:, 1, which:which + 1], MAGIC, ALU.mult, ALU.add).then_inc(S["q_step"], 1)
                    elif step == 1:
                        e.tensor_scalar(w, w, MAGIC, 1.0, ALU.subtract, ALU.min).then_inc(S["q_step"], 1)
                    else:
                        dst = tg[:, j // 2, (j % 2) * FF:(j % 2) * FF + FF] if j < 4 else flat(td[:, 3 * (j - 4):3 * (j - 4) + 3, :])
                        e.tensor_scalar(dst, w, -1.0, None, ALU.max).then_inc(S["q_tern"], 1)

            def attn(s, n, npar, B):
                if s == S_STAT:
                    e.wait_ge(S["sq_act"], n + 1)
                    e.tensor_tensor(hw[:, :], bA[:, 0:D], ng_b[:, :], ALU.mult).then_inc(S["hw_dve"], 1)
                if s == S_AMAX:
                    e.wait_ge(S["hw_dve"], n + 1)
                    e.tensor_reduce(sm[:, AM:AM + 1], hw[:, :], X, ALU.max, apply_absolute_value=True).then_inc(S["amax_dve"], 1)
                if s == S_MAG:
                    e.wait_ge(S["k_pool"], n + 1)
                    e.tensor_scalar(hw[:, :], hw[:, :], sm[:, K1:K1 + 1], MAGIC, ALU.mult, ALU.add).then_inc(S["mag_dve"], 1)
                if s == S_Q:
                    e.wait_ge(S["mag_dve"], n + 1)
                    if some(n):
                        e.wait_ge(S["qT_pe"], n)
                    e.tensor_scalar(qb[:, :], hw[:, :], MAGIC, None, ALU.subtract).then_inc(S["q_dve"], 1)
                for u, (off, w) in enumerate(UNITS):
                    if s == S_UNIT[u] + 1:
                        e.wait_ge(S["sg_act"], 3 * n + u + 1)
                        e.tensor_tensor(v[:, off:off + w], bA[:, 0:w], sg[:, 0:w], ALU.mult).then_inc(S["gt_dve"], 1)
                    if s == S_UNIT[u] + 2:
                        e.wait_ge(S["gt_dve"], 3 * n + u + 1)
                        e.tensor_tensor(v[:, off:off + w], bA[:, 256:256 + w], v[:, off:off + w], ALU.mult).then_inc(S["v_dve"], 1)
                    if s == S_UNIT[u] + 4:
                        e.wait_ge(S["vw_pool"], 3 * n + u + 1)
                        e.tensor_reduce(sm[:, AM2 + u:AM2 + u + 1], v[:, off:off + w], X, ALU.max,
                                        apply_absolute_value=True).then_inc(S["max2_dve"], 1)
                if s == S_MAG2:
                    e.wait_ge(S["k2_pool"], n + 1)
                    e.tensor_scalar(v[:, :], v[:, :], sm[:, K2:K2 + 1], MAGIC, ALU.mult, ALU.add).then_inc(S["mag2_dve"], 1)
                if s == S_Q2:
                    e.wait_ge(S["mag2_dve"], n + 1)
                    if some(n):
                        e.wait_ge(S["q2T_pe"], n)
                    e.tensor_scalar(q2b[:, :], v[:, :], MAGIC, None, ALU.subtract).then_inc(S["q2_dve"], 1)
                if s == S_DOWN:
                    e.wait_ge(S[f"xt_in{npar}"], 8 * n - 8 * npar + 16)
                    if some(kept(n, B)):
                        e.wait_ge(S["x1_kept"], kept(n, B))
                    e.wait_ge(S["down_pe"], n + 1)
                    e.scalar_tensor_tensor(x1[:, npar, :], bA[:, 0:D], sm[:, OSC2:OSC2 + 1], xt[:, npar, :],
                                           ALU.mult, ALU.add).then_inc(S["x1_dve"], 1)
                if s in S_CONV:
                    for o in range(2 * (s - S_CONV[0]), 2 * (s - S_CONV[0]) + 2):
                        k, c = o // 2, o % 2
                        if o == 0:
                            e.wait_ge(S["x1T_act"], n + 1)
                            if some(kept(n, B)):
                                e.wait_ge(S["xlo_pool"], kept(n, B))
                            if some(kept(n, B)):
                                e.wait_ge(S["r_log"], kept(n, B))
                            if npar == 0:
                                if some(kept(n, B)):
                                    e.wait_ge(S["halo_act"], kept(n, B))
                        src = x1T[:, c, npar * P + NB * k:npar * P + NB * k + P]
                        dst = xc[:, c, npar * P:npar * P + P]
                        if k == 0:
                            e.tensor_scalar(dst, src, cond[:, c, k:k + 1], None, ALU.mult).then_inc(S["conv_dve"], 1)
                        else:
                            e.wait_ge(S["conv_dve"], 8 * n + o - 1)
                            e.scalar_tensor_tensor(dst, src, cond[:, c, k:k + 1], dst, ALU.mult, ALU.add).then_inc(S["conv_dve"], 1)

            def result(B):
                e.wait_ge(S["m_o"], NF * (B + 1))
                e.wait_ge(S["x1_kept"], B + 1)
                e.tensor_tensor(flat(yt[:, :, :]), bO[:, :], flat(x1b[:, :, :]), ALU.add).then_inc(S["y_done"], 1)

            def by_token(k):
                return rs[:, k, :].rearrange("p (t a) -> p t a", a=1).broadcast_to([P, 2, E])

            def moe(q, B):
                logits = bA[:, 0:2 * E].rearrange("p (t e) -> p t e", t=2)
                if q == M_RESULT and not (isinstance(B, int) and B == 0):
                    result(B - 1)
                if q == STEPS - 1 and opened(B):
                    if some(32 * B):
                        e.wait_ge(S["y_out"], 32 * B)
                if q == R_LOG and opened(B):
                    e.wait_ge(S["r_log"], B + 1)
                    e.tensor_reduce(rs[:, 0, :], logits, X, ALU.max).then_inc(S["r_max"], 1)
                if q == R_DIFF and opened(B):
                    e.wait_ge(S["r_max"], B + 1)
                    e.tensor_tensor(rt[:, 0, :, 0:E], logits, by_token(0), ALU.subtract).then_inc(S["r_d"], 1)
                if q == R_EXP and opened(B):
                    e.wait_ge(S["r_sig"], B + 1)
                    e.reciprocal(rt[:, 2, :, 0:E], rt[:, 2, :, 0:E]).then_inc(S["r_inv"], 1)
                if q == R_SUM and opened(B):
                    e.wait_ge(S["r_e"], B + 1)
                    e.tensor_reduce(rs[:, 1, :], rt[:, 3, :, 0:E], X, ALU.add).then_inc(S["r_sum"], 1)
                if q == R_P and opened(B):
                    e.wait_ge(S["r_sum"], B + 1)
                    e.reciprocal(rs[:, 2, :], rs[:, 1, :]).then_inc(S["r_isum"], 1)
                    e.wait_ge(S["r_isum"], B + 1)
                    e.tensor_tensor(rt[:, 4, :, 0:E], rt[:, 3, :, 0:E], by_token(2), ALU.mult).then_inc(S["r_p"], 1)
                if q == R_TOP and opened(B):
                    count = fixed(e, B + 1)
                    e.wait_ge(S["r_p"], count)
                    e.max(m8[:, 0, :], rt[:, 4, 0, 0:E])
                    e.max(m8[:, 1, :], rt[:, 4, 1, 0:E]).then_inc(S["r_m8"], 1)
                if q == R_REP and opened(B):
                    count = fixed(e, B + 1)
                    e.wait_ge(S["r_m8set"], count)
                    e.match_replace(rt[:, 5, 0, :], m8[:, 0, :], rt[:, 4, 0, :], -2.0)
                    e.match_replace(rt[:, 5, 1, :], m8[:, 1, :], rt[:, 4, 1, :], -2.0).then_inc(S["r_rep"], 1)
                    e.wait_ge(S["r_rep"], B + 1)
                    e.scalar_tensor_tensor(rt[:, 7, :, 0:E], rt[:, 5, :, 0:E], 0.0, rt[:, 4, :, 0:E],
                                           ALU.is_lt, ALU.mult).then_inc(S["r_chosen"], 1)
                if q == R_SEL and opened(B):
                    e.wait_ge(S["r_chosen"], B + 1)
                    e.tensor_reduce(rs[:, 3, :], rt[:, 7, :, 0:E], X, ALU.add).then_inc(S["r_csum"], 1)
                    e.wait_ge(S["r_csum"], B + 1)
                    e.tensor_scalar(rs[:, 4, :], rs[:, 3, :], 1e-20, None, ALU.add).then_inc(S["r_guard"], 1)
                if q == R_C3 and opened(B):
                    e.wait_ge(S["r_guard"], B + 1)
                    e.reciprocal(rs[:, 5, :], rs[:, 4, :]).then_inc(S["r_icsum"], 1)
                    e.wait_ge(S["r_icsum"], B + 1)
                    e.tensor_tensor(rt[:, 6, :, 0:E], rt[:, 7, :, 0:E], by_token(5), ALU.mult).then_inc(S["r_c"], 1)
                for j, B_ in at_slot(q, M_SIG, B):
                    e.wait_ge(S["m_sig"], NF * B_ + j + 1)
                    e.tensor_tensor(act[:, j % 3, :], bM[j % 2][:, 0:256], act[:, j % 3, :], ALU.mult).then_inc(S["m_t"], 1)
                for j, B_ in at_slot(q, M_T2, B):
                    e.wait_ge(S["m_t"], NF * B_ + j + 1)
                    e.tensor_tensor(act[:, j % 3, :], bM[j % 2][:, 256:512], act[:, j % 3, :],
                                    ALU.mult).then_inc(S["m_a" if j < NSH else "m_t2"], 1)
                for j, B_ in at_slot(q, M_A, B, NSH):
                    d = (j - NSH) % 2
                    e.wait_ge(S["m_c"], (NF - NSH) // 2 * B_ + (j - NSH) // 2 + 1)
                    e.wait_ge(S["m_t2"], (NF - NSH) * B_ + j - NSH + 1)
                    e.tensor_tensor(act[:, j % 3, :], bC[:, 256 * d:256 * d + 256], act[:, j % 3, :], ALU.mult).then_inc(S["m_a"], 1)

            def rest(s, prep, n, npar, B, q):
                if prep == 0:
                    quant(s)
                if prep == 1 and s == 0:
                    e.wait_ge(S["ld_const"], 96)
                if n is not None:
                    attn(s, n, npar, B)
                if B is not None:
                    moe(q, B)

            program(e, gru, rest)

        @block.gpsimd
        def _(e):
            e.memset(ones[:, :], 1.0)
            e.memset(pw[:, :], -1.0).then_inc(S["b_scaled"], 1)
            e.wait_ge(S["b_scaled"], 1)
            e.memset(pw[:, 0:1], -0.5)
            e.wait_ge(S["ld_whh"], 64)
            e.tensor_scalar(bsc[:, :, :], bias[:, :, :], WS, None, ALU.mult).then_inc(S["r_link"], 1)
            e.wait_ge(S["r_link"], 1)
            e.tensor_tensor(bsc[:, 0, 0:4], bsc[:, 0, 0:4], bsc[:, 1, 0:4], ALU.add).then_inc(S["b_scaled"], 1)
            e.memset(m8[:, :, :], 0.0).then_inc(S["setup"], 1)
            col = lambda k: sm[:, k:k + 1]
            half_, one_ = pw[:, 0:1], pw[:, 1:2]

            def gru(m, par, s):
                if s % 8 == 7:
                    count = fixed(e, 32 * m + s + 1)
                    e.wait_ge(S["h_full"], count)
                    if some(m - 1):
                        e.wait_ge(S["ht_pe"], m - 1)
                    first = (s - 6) % RING
                    runs = ((first, 8),) if first + 8 <= RING else ((first, RING - first), (0, 8 - (RING - first)))
                    t = NB * (s - 7)
                    for r, cnt in runs:
                        ins = e.tensor_copy(hist[:, par, :, t:t + NB * cnt].rearrange("p c (s b) -> p c s b", b=NB),
                                            steps[:, r:r + cnt, 2:25:3].rearrange("p s (c b) -> p c s b", c=NC))
                        t += NB * cnt
                    ins.then_inc(S["hist_done"], 1)

            def attn(s, n, npar):
                if s == S_AMAX:
                    count = fixed(e, n + 1)
                    e.wait_ge(S["sq_act"], count)
                    b = (LINK1 + LINK2) * n
                    e.tensor_scalar(col(VAR), col(SS), 1.0 / D, EPS_NORM, ALU.mult, ALU.add).then_inc(S["sm_link"], 1)
                    e.wait_ge(S["sm_link"], b + 1)
                    e.tensor_tensor(col(RR), col(VAR), half_, ALU.pow).then_inc(S["sm_link"], 1)
                    count = fixed(e, b + 2)
                    e.wait_ge(S["sm_link"], count)
                    count = fixed(e, n + 1)
                    e.wait_ge(S["amax_dve"], count)
                    e.tensor_scalar(col(MC), col(AM), col(RR), EPS_Q, ALU.mult, ALU.max).then_inc(S["sm_link"], 1)
                    e.wait_ge(S["sm_link"], b + 3)
                    e.tensor_tensor(col(RC), col(MC), one_, ALU.pow).then_inc(S["sm_link"], 1)
                    count = fixed(e, b + 4)
                    e.wait_ge(S["sm_link"], count)
                    e.tensor_scalar(col(K1), col(RC), QMAX, col(RR), ALU.mult, ALU.mult).then_inc(S["sm_link"], 1)
                    e.wait_ge(S["sm_link"], b + 5)
                    e.tensor_tensor(col(OSC), col(MC), qc[:, 2, 0:1], ALU.mult).then_inc(S["sm_link"], 1)
                    e.wait_ge(S["sm_link"], b + 6)
                    e.tensor_tensor(col(O2), col(OSC), col(OSC), ALU.mult).then_inc(S["k_pool"], 1)
                for u, (off, w) in enumerate(UNITS):
                    if s == S_UNIT[u] + 3:
                        e.wait_ge(S["sq2_act"], 3 * n + u + 1)
                        e.tensor_tensor(v[:, off:off + w], v[:, off:off + w], nd_b[:, off:off + w], ALU.mult).then_inc(S["vw_pool"], 1)
                if s == S_K2:
                    b = (LINK1 + LINK2) * n + LINK1
                    e.wait_ge(S["sq2_act"], 3 * n + 3)
                    e.wait_ge(S["k_pool"], n + 1)
                    e.tensor_tensor(col(VAR2), col(SS2), col(SS2 + 1), ALU.add).then_inc(S["sm_link"], 1)
                    e.wait_ge(S["sm_link"], b + 1)
                    e.tensor_tensor(col(VAR2), col(VAR2), col(SS2 + 2), ALU.add).then_inc(S["sm_link"], 1)
                    count = fixed(e, b + 2)
                    e.wait_ge(S["sm_link"], count)
                    e.tensor_scalar(col(VAR2), col(VAR2), col(O2), col(O2), ALU.mult, ALU.mult).then_inc(S["sm_link"], 1)
                    count = fixed(e, b + 3)
                    e.wait_ge(S["sm_link"], count)
                    e.tensor_scalar(col(VAR2), col(VAR2), 1.0 / FF, EPS_NORM, ALU.mult, ALU.add).then_inc(S["sm_link"], 1)
                    e.wait_ge(S["sm_link"], b + 4)
                    e.tensor_tensor(col(R2), col(VAR2), half_, ALU.pow).then_inc(S["sm_link"], 1)
                    e.wait_ge(S["sm_link"], b + 5)
                    e.tensor_tensor(col(OR2), col(R2), col(O2), ALU.mult).then_inc(S["sm_link"], 1)
                    count = fixed(e, b + 6)
                    e.wait_ge(S["sm_link"], count)
                    count = fixed(e, 3 * n + 3)
                    e.wait_ge(S["max2_dve"], count)
                    e.tensor_scalar(col(AMX), col(AM2), col(AM2 + 1), col(AM2 + 2), ALU.max, ALU.max).then_inc(S["sm_link"], 1)
                    count = fixed(e, b + 7)
                    e.wait_ge(S["sm_link"], count)
                    e.tensor_scalar(col(MC2), col(AMX), col(OR2), EPS_Q, ALU.mult, ALU.max).then_inc(S["sm_link"], 1)
                    e.wait_ge(S["sm_link"], b + 8)
                    e.tensor_tensor(col(RC2), col(MC2), one_, ALU.pow).then_inc(S["sm_link"], 1)
                    count = fixed(e, b + 9)
                    e.wait_ge(S["sm_link"], count)
                    e.tensor_scalar(col(K2), col(RC2), QMAX, col(OR2), ALU.mult, ALU.mult).then_inc(S["sm_link"], 1)
                    e.wait_ge(S["sm_link"], b + 10)
                    e.tensor_tensor(col(OSC2), col(MC2), qc[:, 2, 1:2], ALU.mult).then_inc(S["sm_link"], 1)
                    count = fixed(e, b + 11)
                    e.wait_ge(S["sm_link"], count)
                    e.tensor_copy(col(O2), col(O2)).then_inc(S["k2_pool"], 1)

            def moe(q, B):
                lb = 1 + LINKR * B
                t_ = lambda k: rt[:, k, :, 0:E]
                if q == 0 and opened(B):
                    e.wait_ge(S["xhi_act"], B + 1)
                    e.tensor_tensor(xc_lo[:, :, :], xc[:, :, :], xc_hi[:, :, :].bitcast(F32), ALU.subtract).then_inc(S["xlo_pool"], 1)
                if q == M_KEEP and opened(B):
                    count = fixed(e, 2 * B + 2)
                    e.wait_ge(S["x1_dve"], count)
                    if some(B):
                        e.wait_ge(S["y_done"], B)
                    e.tensor_copy(flat(x1b[:, :, :]), flat(x1[:, :, :])).then_inc(S["x1_kept"], 1)
                if q == R_EXP and opened(B):
                    e.wait_ge(S["r_inv"], B + 1)
                    e.tensor_tensor(t_(3), t_(1), t_(2), ALU.mult).then_inc(S["r_e"], 1)
                if q == R_TOP and opened(B):
                    count = fixed(e, B + 1)
                    e.wait_ge(S["r_m8"], count)
                    e.memset(m8[:, :, TOPK:8], -1.0).then_inc(S["r_m8set"], 1)
                if q == R_C3 and opened(B):
                    count = fixed(e, B + 1)
                    e.wait_ge(S["r_c"], count)
                    if some(B):
                        e.wait_ge(S["r_cT"], B)
                    e.tensor_copy(c3[:, :, 0:E], t_(6)).then_inc(S["r_link"], 1)
                    e.wait_ge(S["r_link"], lb + 1)
                    e.tensor_tensor(t_(0), t_(6), c3[:, :, 0:E], ALU.subtract).then_inc(S["r_link"], 1)
                    count = fixed(e, lb + 2)
                    e.wait_ge(S["r_link"], count)
                    e.tensor_copy(c3[:, :, E:2 * E], t_(0)).then_inc(S["r_link"], 1)
                    e.wait_ge(S["r_link"], lb + 3)
                    e.tensor_tensor(c3[:, :, 2 * E:3 * E], t_(0), c3[:, :, E:2 * E], ALU.subtract).then_inc(S["r_c3"], 1)
                for j, B_ in at_slot(q, M_SPLIT, B):
                    e.wait_ge(S["m_hi"], NF * B_ + j + 1)
                    e.tensor_tensor(act_lo[:, j % 2, :], act[:, j % 3, :], act_hi[:, j % 2, :].bitcast(F32), ALU.subtract).then_inc(S["m_lo"], 1)

            def rest(s, prep, n, npar, B, q):
                if prep == 0 and s < 2 * (GROUPS - 1) and s % 2 == 0:
                    cols = slice(GROUP * (1 + s // 2), GROUP * (2 + s // 2))
                    e.wait_ge(S["x_hi"], 2 + s // 2)
                    e.tensor_tensor(xl[:, :, cols], xf[:, :, cols], xh[:, :, cols].bitcast(F32), ALU.subtract).then_inc(S["x_low"], 1)
                if prep == 1 and s == 0:
                    e.wait_ge(S["ld_const"], 96)
                k = prep_piece(prep, s)
                if k is not None:
                    e.wait_ge(S["prep_hi"], k + 1)
                    src, hi, lo = prep_views(k)
                    e.tensor_tensor(lo, src, hi.bitcast(F32), ALU.subtract).then_inc(S["prep_lo"], 1)
                if n is not None:
                    attn(s, n, npar)
                if B is not None:
                    moe(q, B)

            program(e, gru, rest)


def kernel(x, cond_2048, L0_cond_W_ih, L0_cond_W_hh, L0_cond_b_ih, L0_cond_b_hh, L0_attn_w_gate, L0_attn_norm_gate,
           L0_attn_w_down, L0_attn_norm_down, L0_ffn_gate_w, L0_ffn_w13, L0_ffn_w2, L0_ffn_sw13, L0_ffn_sw2):
    import numpy as np
    import ml_dtypes
    import concourse.bacc as bacc
    from concourse.bass_utils import run_bass_kernel_spmd as run

    f = np.ascontiguousarray
    x, cond = np.asarray(x), np.asarray(cond_2048)
    tokens = x.transpose(1, 0, 2).reshape(T * NB, D)

    def by_chunk(a):
        return f(a.reshape(-1, P, a.shape[1]).transpose(1, 0, 2))

    w13, w2 = np.asarray(L0_ffn_w13), np.asarray(L0_ffn_w2)
    sw13, sw2 = np.asarray(L0_ffn_sw13), np.asarray(L0_ffn_sw2)
    gu = np.zeros((2, NF * P, D), np.float32)
    gu[0, :ROWS], gu[1, :ROWS] = w13[:, :EI].reshape(ROWS, D), w13[:, EI:].reshape(ROWS, D)
    gu[0, ROWS:ROWS + SI], gu[1, ROWS:ROWS + SI] = sw13[:SI], sw13[SI:]
    down = np.zeros((NF * P, D), np.float32)
    down[:ROWS], down[ROWS:ROWS + SI] = w2.transpose(0, 2, 1).reshape(ROWS, D), sw2.T
    w13_l = gu.reshape(2, NF, P, NC, P).transpose(4, 1, 0, 3, 2).reshape(P, NF, 512)
    w2_l = down.reshape(NF, P, D).transpose(1, 0, 2).reshape(P, NF * D)
    wg = np.asarray(L0_attn_w_gate).T.reshape(NC, P, 2 * FF).transpose(1, 0, 2).reshape(P, 4, FF)
    wd = np.zeros((FC * P, D), np.float32)
    wd[:FF] = np.asarray(L0_attn_w_down).T
    wd = wd.reshape(FC, P, D).transpose(1, 0, 2).reshape(P, 2, 768)
    sel = np.tile(np.repeat(np.eye(E), EI, axis=1), (3, 1)).astype(ml_dtypes.bfloat16)
    ins = {
        "xT": by_chunk(tokens.T), "xtok": f(tokens.reshape(TILES, P, D)),
        "w_ih": by_chunk(np.asarray(L0_cond_W_ih)), "w_hh": by_chunk(np.asarray(L0_cond_W_hh)),
        "condT": by_chunk(cond.T),
        "b_ih": f(np.asarray(L0_cond_b_ih).reshape(6, P).T), "b_hh": f(np.asarray(L0_cond_b_hh).reshape(6, P).T),
        "wgT": f(wg), "wdT": f(wd),
        "ng": f(np.asarray(L0_attn_norm_gate).reshape(1, D)), "nd": f(np.asarray(L0_attn_norm_down).reshape(1, FF)),
        "gwT": by_chunk(np.asarray(L0_ffn_gate_w).T), "w13": f(w13_l), "w2": f(w2_l),
        "sel": f(sel), "idf": np.eye(P, dtype=np.float32), "idb": np.eye(P).astype(ml_dtypes.bfloat16),
    }
    nc = bacc.Bacc("TRN2", target_bir_lowering=False, num_devices=1, dynamic_dma_scratch_size=1024)
    aps = {n: nc.dram_tensor(f"in_{n}", a.shape, mybir.dt.from_np(a.dtype), kind="ExternalInput").ap() for n, a in ins.items()}
    out = nc.dram_tensor("out_0", (TILES, P, D), F32, kind="ExternalOutput").ap()
    adaln_kernel(nc, out=out, **aps)
    r = run(nc, [{f"in_{n}": a for n, a in ins.items()}], core_ids=[0])
    y = r.results[0]["out_0"]
    return f(y.reshape(T, NB, D).transpose(1, 0, 2))
```

```python
from contextlib import ExitStack

import concourse.bass as bass
from concourse import mybir

F32 = mybir.dt.float32
F32R = mybir.dt.float32r
F16 = mybir.dt.float16
BF16 = mybir.dt.bfloat16
ALU = mybir.AluOpType
ACT = mybir.ActivationFunctionType
X = mybir.AxisListType.X

P = 128
D = 256
NC = D // P
G3 = 3 * D
NB = 4
T = 256
STEPS = P // NB
TILES = T // STEPS
FF = 704
FC = 6
UNITS = ((0, 256), (256, 256), (512, 192))
E, TOPK, EI = 16, 6, 176
ROWS = E * EI
SI = 2 * EI
NF = (ROWS + SI + P - 1) // P
NSH = NF - ROWS // P
ORDER = [*range(ROWS // P, NF), *range(ROWS // P)]
BLOCK = 2 * P
BLOCKS = TILES // 2
RING = 16
KK = 4
HALO = NB * (KK - 1)

WS = 256.0
MAGIC = 12582912.0
EPS_NORM, EPS_Q, QMAX = 1e-8, 1e-5, 127.0

S_HT, S_STAT, S_AMAX, S_MAG, S_Q, S_QT = 1, 2, 3, 5, 6, 7
S_UNIT = (8, 11, 14)
S_K2, S_MAG2, S_Q2, S_Q2T, S_DOWN, S_X1T = 18, 21, 22, 23, 24, 25
S_CONV, S_HALO = (26, 27, 28, 29), 30
R_LOG, R_DIFF, R_SIG, R_EXP, R_SUM, R_P, R_TOP, R_SIX, R_REP, R_SEL, R_C3, R_CT = 0, 0, 1, 2, 3, 4, 5, 6, 7, 8, 9, 11
R_EARLY = 28
M_G, M_U, M_SIG, M_T2, M_C, M_A, M_SPLIT = 0, 1, 2, 3, 3, 4, 5
M_RESULT, M_KEEP = 6, 7
M_OUT = ((7, 8, 8), (6, 6, 7), (6, 7, 8), (7, 8, 9))
WARM = {0: 3, 1: 4, 58: 4, 59: 4, 60: 3, 61: 5, 62: 5, 63: 5}
FIRST_WARM = {29: 6, 30: 12, 31: 12}


def start(j):
    return 2 + (9 * j) // 4


def at_slot(q, after, B, lo=0):
    slot = [start(j) + (after if isinstance(after, int) else after[j % 4]) for j in range(NF)]
    last = [(j, B - 1) for j in range(lo, NF) if slot[j] == q + 2 * STEPS and not (isinstance(B, int) and B == 0)]
    return last + [(j, B) for j in range(lo, NF) if slot[j] == q and not (isinstance(B, int) and B >= BLOCKS)]


def last_tile(n):
    return isinstance(n, int) and n == TILES - 1


def kept(n, B):
    return n // 2 if isinstance(n, int) else B + 1


PREP = NF + (NF + 1) // 2
PREP_EARLY = 10
PREP_AT = [*range(9, 29, 2), *[q for q in range(STEPS + 7, 3 * STEPS) if 5 <= q % STEPS < 17 or 22 <= q % STEPS < 26]][:PREP]
GROUP = 2 * P
GROUPS = T * NB // GROUP
GI_AT = 3
Q_ABS, Q_SUM, Q_RED, Q_CLIP, Q_INV, Q_DIV, Q_TERN = 0, 6, 7, 8, 9, 10, 11
SS, AM, VAR, RR, MC, RC, K1, OSC, O2, VAR2, R2, OR2, AMX, MC2, RC2, K2, OSC2 = range(17)
SS2, AM2, O4 = 17, 20, 23
LINK1, LINK2, LINKR = 7, 8, 3


def build(nc, xT, xtok, w_ih, w_hh, condT, b_ih, b_hh, wgT, wdT, ng, nd, gwT, w13, w2, sel, idf, idb, out):
    ctx = ExitStack()
    with ctx:
        def sb(name, shape, dt):
            return ctx.enter_context(nc.sbuf_tensor(name, shape, dt))

        def pb(name, shape, dt):
            return ctx.enter_context(nc.psum_tensor(name, shape, dt))

        def sem(name):
            return ctx.enter_context(nc.semaphore(name))

        whh_hi, whh_lo = sb("whh_hi", [P, NC, G3], F16), sb("whh_lo", [P, NC, G3], F16)
        tg, td = sb("tg", [P, NC, 2 * FF], BF16), sb("td", [P, FC, D], BF16)
        identf, identb = sb("identf", [P, P], F32), sb("identb", [P, P], BF16)
        selb = sb("selb", [48, ROWS], BF16)
        ng_b, nd_b = sb("ng_b", [P, D], F32), sb("nd_b", [P, FF], F32)
        cond = sb("cond", [P, NC, NB], F32)
        gw = sb("gw", [P, NC, E], F32)
        ones = sb("ones", [P, P], F32)
        pw = sb("pw", [P, 32], F32)
        qp, qm = sb("qp", [P, 6], F32), sb("qm", [P, 2], F32)
        qc = sb("qc", [P, 3, 2], F32)
        gi = sb("gi", [P, 2, STEPS, 24], F32)
        bias = sb("bias", [P, 2, 6], F32)
        bsc = sb("bsc", [P, 2, 6], F32)
        tmpl = sb("tmpl", [P, 8, 2], F32)
        n_mul = sb("n_mul", [P, 8, 3], F32)
        n_sum = sb("n_sum", [P, 8, 3], F32)
        h_mul = sb("h_mul", [P, 8, 3], F32)
        steps = sb("steps", [P, RING, 25], F32)
        h16 = sb("h16", [P, 2, 24], F16)
        hist = sb("hist", [P, 2, NC, P], F32)
        hw, qb, qT = sb("hw", [P, D], F32), sb("qb", [P, D], BF16), sb("qT", [P, NC, P], BF16)
        junk = sb("junk", [P, D], F32)
        sg = sb("sg", [P, 256], F32)
        v = sb("v", [P, FF], F32)
        q2b, q2T = sb("q2b", [P, FF], BF16), sb("q2T", [P, FC, P], BF16)
        sm = sb("sm", [P, 24], F32)
        xt = sb("xt", [P, 2, D], F32)
        x1, x1b, yt = sb("x1", [P, 2, D], F32), sb("x1b", [P, 2, D], F32), sb("yt", [P, 2, D], F32)
        x1T = sb("x1T", [P, NC, HALO + 2 * P], F32)
        xc = sb("xc", [P, NC, BLOCK], F32)
        tap = sb("tap", [P, NC, P], F32)
        xc_hi, xc_lo = sb("xc_hi", [P, NC, BLOCK], F32R), sb("xc_lo", [P, NC, BLOCK], F32R)
        cT = sb("cT", [48, BLOCK], BF16)
        c3 = sb("c3", [P, 2, 3 * E], BF16)
        rt = sb("rt", [P, 8, 2, E + 2], F32)
        rs = sb("rs", [P, 8, 2], F32)
        m8 = sb("m8", [P, 2, 8], F32)

        base = (int(nc.sbuf_base) + 63) // 64 * 64
        w13_bytes, w2_bytes = NF * 512 * 4, NF * 256 * 4
        arena = sb("arena", [P, (2 * w13_bytes + 2 * w2_bytes + 7 * BLOCK * 4 + 64) // 4], F32)

        place = [base]

        def at(name, shape, dt, size):
            t = nc.alloc_sbuf_tensor_at(name, shape, dt, offset=place[0])
            place[0] += size
            return t

        w13_hi = at("w13_hi", [P, NF, 2, NC, P], F32R, w13_bytes)
        w13_lo = at("w13_lo", [P, NF, 2, NC, P], F32R, w13_bytes)
        w2_hi = at("w2_hi", [P, NF, D], F32R, w2_bytes)
        w2_lo = at("w2_lo", [P, NF, D], F32R, w2_bytes)
        act = at("act", [P, 3, BLOCK], F32, 3 * BLOCK * 4)
        act_hi, act_lo = at("act_hi", [P, 2, BLOCK], F32R, 2 * BLOCK * 4), at("act_lo", [P, 2, BLOCK], F32R, 2 * BLOCK * 4)
        place[0] -= 7 * BLOCK * 4
        stage = at("stage", [P, 3, 512], F32, 6144)
        place[0] = base
        xf = at("xf", [P, NC, T * NB], F32, 8192)
        wf = at("wf", [P, NC, G3], F32, 6144)
        whf = at("whf", [P, NC, G3], F32, 6144)
        xh = at("xh", [P, NC, T * NB], F32R, 8192)
        xl = at("xl", [P, NC, T * NB], F32R, 8192)
        wh = at("wh", [P, NC, G3], F32R, 6144)
        wl = at("wl", [P, NC, G3], F32R, 6144)
        zer = at("zer", [P, 512], BF16, 1024)
        place[0] = base + 2 * w13_bytes
        wgf = at("wgf", [P, 4, FF], F32, 11264)
        wdf = at("wdf", [P, 2, FC * D // 2], F32, 6144)
        place[0] = base + 2 * w13_bytes + w2_bytes
        gis = at("gis", [P, T - 2 * STEPS, 24], F32, (T - 2 * STEPS) * 96)

        bR, bZ = pb("bR", [P, 512], F32), pb("bZ", [P, 512], F32)
        bN = pb("bN", [P, 512], F32)
        bA = pb("bA", [P, 512], F32)
        bM = [pb("bM0", [P, 512], F32), pb("bM1", [P, 512], F32)]
        bC = pb("bC", [P, 512], F32)
        bO = pb("bO", [P, 512], F32)
        R = bR[:, 0:RING * 8].rearrange("p (s c b) -> p s c b", s=RING, c=NC)
        Z = bZ[:, 0:RING * 8].rearrange("p (s c b) -> p s c b", s=RING, c=NC)
        N = bN[:, 0:RING * 24].rearrange("p (s c b e) -> p s c b e", s=RING, c=NC, e=3)
        bA16 = bA[:, :].bitcast(BF16)
        bC16 = bC[:, :].bitcast(BF16)

        gi_banks = (bM[0], bM[1], bC, bO)
        gi_dram = nc.dram_tensor("gi_scratch", [TILES + 1, P, STEPS * 24], F32, kind="Internal").ap()

        names = """ld_whh ld_x ld_const ld_quant x_split w_split x_hi w_hi gi_pe gi_ev gi_out gi_in0 gi_in1 gi_used
            setup zero banks_set x_low ld_w0 ld_w1 ld_x0 b_scaled whh_high h0_high whh_split
            r_ready n_ready z_ready r_done z_done n_summed n_done h_hi h_full h_lo hist_done
            q_abs q_pe q_step q_tern
            st_in0 st_in1 st_in2 prep_hi prep_lo
            ht_pe sq_act hw_dve amax_dve k_pool mag_dve q_dve qT_pe qT_act
            gu_pe sg_act gt_dve v_dve sq2_act vw_pool max2_dve k2_pool mag2_dve q2_dve q2T_pe q2T_act
            down_pe x1_dve x1T_pe x1T_act conv_tap conv_sum conv_last halo_act x1_kept xhi_act xlo_pool
            xt_in0 xt_in1 sm_link r_link
            r_log r_max r_d r_sig r_e r_inv r_sum r_isum r_p r_m8 r_m8set r_rep r_chosen r_csum r_guard r_icsum r_c r_c3 r_cT r_cT_act
            m_u m_c m_sig m_t m_t2 m_a m_hi m_lo m_o y_done y_out""".split()
        S = {n: sem(n) for n in names}
        block = ctx.enter_context(nc.Block())

        def some(count):
            return not isinstance(count, int) or count > 0

        def in_register(e, count):
            return count if isinstance(count, int) else e.snap(e.to_reg(count))

        def fixed(e, count):
            if isinstance(count, int):
                return count
            count = in_register(e, count)
            e.wait_ge(S["setup"], 1)
            return count

        def opened(B):
            return not (isinstance(B, int) and B >= BLOCKS)

        def flat(ap):
            return ap.rearrange("p a b -> p (a b)")

        def program(e, gru, rest):
            def half(i, par, prep=None, with_gru=True, attn=True, moe=True):
                m = 2 * i + par
                for s in range(STEPS):
                    if with_gru:
                        gru(m, par, s)
                    B, q = (i - 1, s) if par else (i - 2, STEPS + s)
                    rest(s, prep, m - 1 if attn else None, 1 - par, B if moe else None, q)

            half(0, 0, prep=0, attn=False, moe=False)
            half(0, 1, prep=1, moe=False)
            half(1, 0, prep=2, moe=False)
            half(1, 1)
            with e.Fori(2, TILES // 2) as i:
                half(i, 0)
                half(i, 1)
            half(TILES // 2, 0, with_gru=False)
            half(TILES // 2, 1, with_gru=False, attn=False)
            half(TILES // 2 + 1, 0, with_gru=False, attn=False)
            for q in range(M_RESULT + 1):
                rest(q, None, None, 0, BLOCKS, q)

        def prep_piece(prep, s):
            return PREP_AT.index(STEPS * prep + s) if prep is not None and STEPS * prep + s in PREP_AT else None

        def gi_piece(prep, s):
            k = -1 if prep is None else STEPS * prep + s - GI_AT
            return (1 + k // 12, k // 2 % 6, k % 2) if 0 <= k < 12 * (GROUPS - 1) else None

        def prep_views(k):
            if k < NF:
                return (stage[:, k % 3, :].rearrange("p (g c f) -> p g c f", g=2, c=NC), w13_hi[:, k], w13_lo[:, k])
            f = 2 * (k - NF)
            n = min(2, NF - f)
            return (stage[:, k % 3, 0:n * D].rearrange("p (f d) -> p f d", f=n), w2_hi[:, f:f + n, :], w2_lo[:, f:f + n, :])

        def released(j, B):
            return ("m_a", NF * B + j + 1) if j < NSH else ("m_t2", (NF - NSH) * B + j - NSH + 1)

        @block.sync
        def _(e):
            e.dma_start(xf[:, :, 0:GROUP], xT[:, :, 0:GROUP]).then_inc(S["ld_x0"], 16)
            e.dma_start(wf[:, :, 0:G3 // 2], w_ih[:, :, 0:G3 // 2]).then_inc(S["ld_w0"], 16)
            e.dma_start(wf[:, :, G3 // 2:G3], w_ih[:, :, G3 // 2:G3]).then_inc(S["ld_w1"], 16)
            e.dma_start(whf[:, :, :], w_hh).then_inc(S["ld_whh"], 16)
            e.dma_start(cond[:, :, :], condT).then_inc(S["ld_whh"], 16)
            e.dma_start(bias[:, 0, :], b_ih).then_inc(S["ld_whh"], 16)
            e.dma_start(bias[:, 1, :], b_hh).then_inc(S["ld_whh"], 16)
            e.dma_start(xf[:, :, GROUP:T * NB], xT[:, :, GROUP:T * NB]).then_inc(S["ld_x"], 16)
            e.dma_start(wgf[:, :, :], wgT).then_inc(S["ld_quant"], 16)
            e.dma_start(wdf[:, :, :], wdT).then_inc(S["ld_quant"], 16)
            e.dma_start(identf[:, :], idf).then_inc(S["ld_const"], 16)
            e.dma_start(identb[:, :], idb).then_inc(S["ld_const"], 16)
            e.dma_start(selb[:, :], sel).then_inc(S["ld_const"], 16)
            e.dma_start(gw[:, :, :], gwT).then_inc(S["ld_const"], 16)
            e.dma_start(ng_b[:, :], ng.broadcast_to([P, D])).then_inc(S["ld_const"], 16)
            e.dma_start(nd_b[:, :], nd.broadcast_to([P, FF])).then_inc(S["ld_const"], 16)

            def tile(dram, n):
                return dram[n] if isinstance(n, int) else dram[bass.ds(n, 1), :, :].rearrange("a p f -> (a p) f")

            def loads(m, par, gru=True, attn=True):
                if gru:
                    e.wait_ge(S["gi_used"], m)
                    e.dma_start(flat(gi[:, 1 - par, :, :]), tile(gi_dram, m + 1)).then_inc(S[f"gi_in{1 - par}"], 16)
                if attn:
                    if some(m - 2):
                        e.wait_ge(S["x1_dve"], m - 2)
                    e.dma_start(xt[:, 1 - par, :], tile(xtok, m - 1)).then_inc(S[f"xt_in{1 - par}"], 16)

            def result(B):
                e.wait_ge(S["y_done"], B + 1)
                for k in range(2):
                    e.dma_start(tile(out, 2 * B + k), yt[:, k, :]).then_inc(S["y_out"], 16)

            def prep_load(k):
                if k >= 3:
                    e.wait_ge(S["prep_lo"], k - 2)
                src = w13[:, k, :] if k < NF else w2[:, 512 * (k - NF):min(512 * (k - NF + 1), NF * D)]
                e.dma_start(stage[:, k % 3, 0:src.shape[1]], src).then_inc(S[f"st_in{k % 3}"], 16)

            for g, pieces in ((1, range(6)), (2, range(6, PREP_EARLY)), (3, range(PREP_EARLY, PREP_EARLY + 3))):
                for k in pieces:
                    prep_load(k)
                e.wait_ge(S["gi_ev"], 6 * (g + 1))
                for k in range(2):
                    o = 2 * STEPS * (g - 1) + STEPS * k
                    e.dma_start(gi_dram[2 * g + k], flat(gis[:, o:o + STEPS, :])).then_inc(S["gi_out"], 16)
                if g == 1:
                    e.wait_ge(S["gi_out"], 32)
                    loads(1, 1)
            e.dma_start(gi_dram[TILES], flat(gis[:, T - 3 * STEPS:T - 2 * STEPS, :])).then_inc(S["gi_out"], 16)
            for k in range(PREP_EARLY + 3, PREP):
                prep_load(k)
                if k == NF:
                    e.wait_ge(S["gi_out"], 16 * (TILES - 1))
                    loads(2, 0)
            loads(3, 1)
            with e.Fori(2, TILES // 2) as i:
                loads(2 * i, 0)
                loads(2 * i + 1, 1)
                result(i - 2)
            loads(TILES, 0, gru=False)
            result(2)
            result(3)
            e.wait_ge(S["y_out"], 16 * TILES)

        @block.tensor
        def _(e):
            e.wait_ge(S["zero"], 1)
            for bank in (bR, bZ, bN):
                mm = e.matmul(bank[:, :], zer[:, 0:P], zer[:, :], start=True, stop=True)
            mm.then_inc(S["banks_set"], 1)

            def project(g, m6, terms=range(3 * NC)):
                q = 6 * g + m6
                for t in terms:
                    if g == 0 and m6 % 3 == 0 and t == 0:
                        e.wait_ge(S["x_hi"], 1)
                        e.wait_ge(S["w_hi"], 1 + m6 // 3)
                    if g == 0 and m6 == 0 and t == NC:
                        e.wait_ge(S["x_split"], 1)
                    if g == 0 and m6 % 3 == 0 and t == 2 * NC:
                        e.wait_ge(S["w_split"], 1 + m6 // 3)
                    if g > 0 and m6 == 0 and t == 0:
                        e.wait_ge(S["x_low"], g)
                    if t == 0 and q > 3:
                        e.wait_ge(S["gi_ev"], q - 3)
                    (wt, xp), k = ((wh, xh), (wh, xl), (wl, xh))[t // NC], t % NC
                    mm = e.matmul(gi_banks[q % 4][:, 0:GROUP], wt[:, k, m6 * P:(m6 + 1) * P], xp[:, k, GROUP * g:GROUP * (g + 1)],
                                  start=(t == 0), stop=(t == 3 * NC - 1))
                    if t == 3 * NC - 1:
                        mm.then_inc(S["gi_pe"], 1)

            for m6 in range(6):
                project(0, m6)
            e.wait_ge(S["whh_split"], 1)

            def gate(out_of, g, wts, part):
                for c in range(NC):
                    for k in range(NC):
                        for wt in wts:
                            mm = e.matmul(out_of(c), wt[:, k, g * D + c * P:g * D + (c + 1) * P],
                                          h16[:, part, 12 * k + 2:12 * k + 12:3],
                                          start=False, stop=False, skip_group_check=True)
                return mm

            def gru(m, par, s):
                n, slot = 32 * m + s, s % RING
                r_of, z_of = lambda c: R[:, slot, c, :], lambda c: Z[:, slot, c, :]
                e.wait_ge(S["h_hi"], n + 1)
                gate(r_of, 0, (whh_hi, whh_lo), 0)
                gate(lambda c: N[:, slot, c, :, 0], 2, (whh_lo,), 0)
                e.wait_ge(S["h_lo"], n + 1)
                gate(r_of, 0, (whh_hi,), 1).then_inc(S["r_ready"], 1)
                for c in range(NC):
                    for k in range(NC):
                        mm = e.matmul(N[:, slot, c, :, 0:2].rearrange("p b e -> p e b"),
                                      whh_hi[:, k, 2 * D + c * P:2 * D + (c + 1) * P],
                                      h16[:, :, 12 * k + 2:12 * k + 12:3],
                                      start=False, stop=False, skip_group_check=True)
                mm.then_inc(S["n_ready"], 1)
                gate(z_of, 1, (whh_hi, whh_lo), 0)
                gate(z_of, 1, (whh_hi,), 1).then_inc(S["z_ready"], 1)

            def attn(s, n, npar, B):
                if s == S_HT:
                    e.wait_ge(S["hist_done"], 4 * n + 4)
                    if some(n):
                        e.wait_ge(S["x1T_act"], n)
                    for c in range(NC):
                        mm = e.transpose(bA[:, c * P:(c + 1) * P], hist[:, npar, c, :], identf[:, :])
                    mm.then_inc(S["ht_pe"], 1)
                if s == S_QT:
                    e.wait_ge(S["q_dve"], n + 1)
                    for c in range(NC):
                        mm = e.transpose(bA16[:, c * P:(c + 1) * P], qb[:, c * P:(c + 1) * P], identb[:, :])
                    mm.then_inc(S["qT_pe"], 1)
                for u, (off, w) in enumerate(UNITS):
                    if s == S_UNIT[u]:
                        if u == 0:
                            e.wait_ge(S["qT_act"], n + 1)
                            e.wait_ge(S["q_tern"], 6)
                        else:
                            e.wait_ge(S["v_dve"], 3 * n + u)
                        for g in range(2):
                            for k in range(NC):
                                mm = e.matmul(bA[:, 256 * g:256 * g + w], qT[:, k, :], tg[:, k, FF * g + off:FF * g + off + w],
                                              start=(k == 0), stop=(k == NC - 1))
                        mm.then_inc(S["gu_pe"], 1)
                if s == S_Q2T:
                    e.wait_ge(S["q2_dve"], n + 1)
                    for c in range(FC):
                        w = min(P, FF - c * P)
                        mm = e.transpose(bA16[0:w, c * P:(c + 1) * P], q2b[:, c * P:c * P + w], identb[:, :])
                    mm.then_inc(S["q2T_pe"], 1)
                if s == S_DOWN:
                    e.wait_ge(S["q2T_act"], n + 1)
                    for c in range(FC):
                        w = min(P, FF - c * P)
                        mm = e.matmul(bA[:, 0:D], q2T[0:w, c, :], td[0:w, c, :], start=(c == 0), stop=(c == FC - 1))
                    mm.then_inc(S["down_pe"], 1)
                if s == S_X1T:
                    e.wait_ge(S["x1_dve"], n + 1)
                    for c in range(NC):
                        mm = e.transpose(bA[:, c * P:(c + 1) * P], x1[:, npar, c * P:(c + 1) * P], identf[:, :])
                    mm.then_inc(S["x1T_pe"], 1)

            def keep_warm(count):
                for _ in range(count):
                    e.matmul(bM[1][:, 0:256], identb[:, :], tg[:, 0, 0:256], start=True, stop=True)

            def logits(t, B):
                e.wait_ge(S["conv_sum"], 3 * (2 * B + 1 + t))
                if some((NF - NSH) * B):
                    e.wait_ge(S["m_t2"], (NF - NSH) * B)
                for c in range(NC):
                    mm = e.matmul(bM[0][:, t * E:(t + 1) * E], xc[:, c, t * P:(t + 1) * P], gw[:, c, :],
                                  start=(c == 0), stop=(c == NC - 1))
                mm.then_inc(S["r_log"], 1)

            def moe(q, B):
                if q in WARM and not (isinstance(B, int) and B >= BLOCKS - 1):
                    if q == min(w for w in WARM if w >= STEPS):
                        e.wait_ge(S["m_t2"], (NF - NSH) * (B + 1) - 1)
                    keep_warm(WARM[q])
                if q == R_LOG and opened(B):
                    logits(1, B)
                if q == R_CT and opened(B):
                    count = fixed(e, B + 1)
                    e.wait_ge(S["r_c3"], count)
                    if some(NF * B):
                        e.wait_ge(S["m_a"], NF * B)
                    for t in range(2):
                        mm = e.transpose(bC16[0:48, t * P:(t + 1) * P], c3[:, t, :], identb[:, :])
                    mm.then_inc(S["r_cT"], 1)
                for gu, stage_at in enumerate((M_G, M_U)):
                    for j, B_ in at_slot(q, stage_at, B):
                        f, bank = ORDER[j], bM[j % 2]
                        if gu == 0 and j == 0:
                            e.wait_ge(S["xhi_act"], B_ + 1)
                            e.wait_ge(S["xlo_pool"], B_ + 1)
                            e.wait_ge(S["prep_lo"], PREP)
                            e.wait_ge(S["r_d"], B_ + 1)
                        if gu == 0 and j >= 2:
                            name, count = released(j - 2, B_)
                            e.wait_ge(S[name], count)
                        terms = [(wt, xp, k) for wt, xp in ((w13_hi, xc_hi), (w13_lo, xc_hi), (w13_hi, xc_lo)) for k in range(NC)]
                        for t, (wt, xp, k) in enumerate(terms):
                            mm = e.matmul(bank[:, 256 * gu:256 * gu + 256], wt[:, f, gu, k, :], xp[:, k, :],
                                          start=(t == 0), stop=(t == len(terms) - 1))
                        if gu == 1:
                            mm.then_inc(S["m_u"], 1)
                for j, B_ in at_slot(q, M_C, B, NSH):
                    if (j - NSH) % 2 == 0:
                        if j == NSH:
                            e.wait_ge(S["r_cT_act"], B_ + 1)
                        else:
                            e.wait_ge(S["m_a"], NF * B_ + j)
                        for d in range(2):
                            mm = e.matmul(bC[:, 256 * d:256 * d + 256], selb[:, (j + d - NSH) * P:(j + d - NSH + 1) * P], cT[:, :],
                                          start=True, stop=True)
                        mm.then_inc(S["m_c"], 1)
                for piece, wt in enumerate((w2_hi, w2_lo, w2_hi)):
                    for j, B_ in at_slot(q, [o[piece] for o in M_OUT], B):
                        if piece == 0:
                            if j == 0 and some(B_):
                                e.wait_ge(S["y_done"], B_)
                            e.wait_ge(S["m_hi"], NF * B_ + j + 1)
                        if piece == 2:
                            e.wait_ge(S["m_lo"], NF * B_ + j + 1)
                        part = act_lo if piece == 2 else act_hi
                        for t in range(2):
                            mm = e.matmul(bO[:, t * D:(t + 1) * D], part[:, j % 2, t * P:(t + 1) * P], wt[:, ORDER[j], :],
                                          start=(j == 0 and t == 0 and piece == 0), stop=(j == NF - 1 and piece == 2),
                                          skip_group_check=True)
                        if piece == 2:
                            mm.then_inc(S["m_o"], 1)

            def rest(s, prep, n, npar, B, q):
                if prep == 1 and s == 0:
                    e.wait_ge(S["ld_const"], 96)
                if gi_piece(prep, s):
                    g, m6, second = gi_piece(prep, s)
                    project(g, m6, range(3 * second, 3 * second + 3))
                if prep == 0 and s == Q_SUM:
                    e.wait_ge(S["q_abs"], 6)
                    e.wait_ge(S["setup"], 1)
                    e.matmul(bA[:, 0:6], ones[:, :], qp[:, :], start=True, stop=True).then_inc(S["q_pe"], 1)
                if prep == 2 and s in FIRST_WARM:
                    keep_warm(FIRST_WARM[s])
                if n is not None:
                    attn(s, n, npar, B)
                if B is not None:
                    moe(q, B)
                if n is not None and npar == 1 and s == R_EARLY:
                    logits(0, kept(n, B))

            program(e, gru, rest)

        @block.scalar
        def _(e):
            e.wait_ge(S["zero"], 3)
            e.activation(junk[:, 0:1], h_mul[:, 0, 0:1], ACT.Sigmoid)
            e.wait_ge(S["ld_x0"], 16)
            e.activation(xh[:, :, 0:GROUP], xf[:, :, 0:GROUP], ACT.Copy).then_inc(S["x_hi"], 1)
            e.wait_ge(S["ld_w0"], 16)
            e.activation(wh[:, :, 0:G3 // 2], wf[:, :, 0:G3 // 2], ACT.Copy).then_inc(S["w_hi"], 1)
            e.wait_ge(S["ld_w1"], 16)
            e.activation(wh[:, :, G3 // 2:G3], wf[:, :, G3 // 2:G3], ACT.Copy).then_inc(S["w_hi"], 1)
            e.wait_ge(S["b_scaled"], 2)

            def projected(g, m6):
                q = 6 * g + m6
                dst = gi[:, :, :, 4 * m6:4 * m6 + 4].rearrange("p t s b -> p (t s) b") if g == 0 else \
                    gis[:, 2 * STEPS * (g - 1):2 * STEPS * g, 4 * m6:4 * m6 + 4]
                e.wait_ge(S["gi_pe"], q + 1)
                e.activation(dst, gi_banks[q % 4][:, 0:GROUP].rearrange("p (s b) -> p s b", b=NB),
                             ACT.Identity, scale=WS, bias=bsc[:, 0, m6:m6 + 1]).then_inc(S["gi_ev"], 1)

            for m6 in range(6):
                projected(0, m6)

            def gru(m, par, s):
                n, slot = 32 * m + s + 1, s % RING
                e.wait_ge(S["r_ready"], n)
                e.activation(n_mul[:, :, 2], flat(R[:, slot, :, :]), ACT.Sigmoid, scale=1 / WS).then_inc(S["r_done"], 1)
                e.wait_ge(S["z_ready"], n)
                e.activation(h_mul[:, :, 2], flat(Z[:, slot, :, :]), ACT.Sigmoid, scale=1 / WS).then_inc(S["z_done"], 1)
                e.wait_ge(S["n_summed"], n)
                e.activation(steps[:, slot, 1:25].rearrange("p (a b) -> p a b", b=3)[:, :, 0:3:2],
                             n_sum[:, :, 2:3].broadcast_to([P, 8, 2]), ACT.Tanh, scale=1 / WS).then_inc(S["n_done"], 1)

            def attn(s, n, npar):
                if s == S_STAT:
                    e.wait_ge(S["ht_pe"], n + 1)
                    e.activation(junk[:, :], bA[:, 0:D], ACT.Square, accum_out=sm[:, SS:SS + 1]).then_inc(S["sq_act"], 1)
                if s == S_QT:
                    e.wait_ge(S["qT_pe"], n + 1)
                    e.activation(flat(qT[:, :, :]), bA16[:, 0:D], ACT.Copy).then_inc(S["qT_act"], 1)
                for u, (off, w) in enumerate(UNITS):
                    if s == S_UNIT[u] + 1:
                        if some(3 * n + u):
                            e.wait_ge(S["gt_dve"], 3 * n + u)
                        e.wait_ge(S["gu_pe"], 3 * n + u + 1)
                        e.activation(sg[:, 0:w], bA[:, 0:w], ACT.Sigmoid, scale=sm[:, OSC:OSC + 1]).then_inc(S["sg_act"], 1)
                    if s == S_UNIT[u] + 3:
                        e.wait_ge(S["v_dve"], 3 * n + u + 1)
                        e.activation(junk[:, 0:w], v[:, off:off + w], ACT.Square,
                                     accum_out=sm[:, SS2 + u:SS2 + u + 1]).then_inc(S["sq2_act"], 1)
                if s == S_Q2T:
                    e.wait_ge(S["q2T_pe"], n + 1)
                    last = FF - (FC - 1) * P
                    e.activation(flat(q2T[:, 0:FC - 1, :]), bA16[:, 0:(FC - 1) * P], ACT.Copy)
                    e.activation(q2T[0:last, FC - 1, :], bA16[0:last, (FC - 1) * P:FC * P], ACT.Copy).then_inc(S["q2T_act"], 1)
                if s == S_X1T:
                    if some(n):
                        e.wait_ge(S["conv_tap"], 4 * n)
                    e.wait_ge(S["x1T_pe"], n + 1)
                    e.activation(x1T[:, :, HALO + npar * P:HALO + npar * P + P], bA[:, 0:D].rearrange("p (c t) -> p c t", c=NC),
                                 ACT.Copy).then_inc(S["x1T_act"], 1)
                if s == S_HALO and npar == 1 and not last_tile(n):
                    e.wait_ge(S["conv_tap"], 4 * n + 4)
                    e.activation(x1T[:, :, 0:HALO], x1T[:, :, BLOCK:BLOCK + HALO], ACT.Copy).then_inc(S["halo_act"], 1)

            def moe(q, B):
                if q == 0 and opened(B):
                    e.wait_ge(S["conv_sum"], 3 * (2 * B + 2))
                    if some(NF * B):
                        e.wait_ge(S["m_u"], NF * B)
                    e.activation(xc_hi[:, :, :], xc[:, :, :], ACT.Copy).then_inc(S["xhi_act"], 1)
                if q == R_SIG and opened(B):
                    e.wait_ge(S["r_d"], B + 1)
                    e.activation(rt[:, 1, :, 0:E], rt[:, 0, :, 0:E], ACT.Sigmoid)
                    e.activation(rt[:, 2, :, 0:E], rt[:, 0, :, 0:E], ACT.Sigmoid, scale=-1.0).then_inc(S["r_sig"], 1)
                if q == R_CT and opened(B):
                    e.wait_ge(S["r_cT"], B + 1)
                    e.activation(cT[:, :], bC16[0:48, 0:BLOCK], ACT.Copy).then_inc(S["r_cT_act"], 1)
                for j, B_ in at_slot(q, M_SIG, B):
                    if some(NF * B_ + max(0, j - 2)):
                        e.wait_ge(S["m_lo"], NF * B_ + max(0, j - 2))
                    e.wait_ge(S["m_u"], NF * B_ + j + 1)
                    e.activation(act[:, j % 3, :], bM[j % 2][:, 0:256], ACT.Sigmoid).then_inc(S["m_sig"], 1)
                for j, B_ in at_slot(q, M_SPLIT, B):
                    if some(NF * B_ + max(0, j - 1)):
                        e.wait_ge(S["m_o"], NF * B_ + max(0, j - 1))
                    e.wait_ge(S["m_a"], NF * B_ + j + 1)
                    e.activation(act_hi[:, j % 2, :], act[:, j % 3, :], ACT.Copy).then_inc(S["m_hi"], 1)

            def rest(s, prep, n, npar, B, q):
                if prep == 0 and s < 2 * (GROUPS - 1) and s % 2 == 0:
                    if s == 0:
                        e.wait_ge(S["ld_x"], 16)
                    cols = slice(GROUP * (1 + s // 2), GROUP * (2 + s // 2))
                    e.activation(xh[:, :, cols], xf[:, :, cols], ACT.Copy).then_inc(S["x_hi"], 1)
                if gi_piece(prep, s) and gi_piece(prep, s)[2]:
                    projected(*gi_piece(prep, s)[:2])
                k = prep_piece(prep, s)
                if k is not None:
                    if k == 0:
                        e.wait_ge(S["x_low"], GROUPS - 1)
                        e.wait_ge(S["w_split"], 2)
                        e.wait_ge(S["whh_split"], 1)
                    if k == PREP_EARLY:
                        e.wait_ge(S["gi_pe"], 6 * GROUPS)
                    if k == NF:
                        e.wait_ge(S["q_tern"], 6)
                        e.wait_ge(S["gi_out"], 16 * (TILES - 1))
                    e.wait_ge(S[f"st_in{k % 3}"], 16 * (k // 3 + 1))
                    src, hi, _ = prep_views(k)
                    e.activation(hi, src, ACT.Copy).then_inc(S["prep_hi"], 1)
                if n is not None:
                    attn(s, n, npar)
                if B is not None:
                    moe(q, B)

            program(e, gru, rest)

        @block.vector
        def _(e):
            e.memset(zer[:, :], 0.0).then_inc(S["zero"], 1)
            e.memset(n_mul[:, :, :], 0.0)
            e.memset(h_mul[:, :, :], 0.0)
            e.memset(h16[:, :, :], 0.0)
            e.memset(tmpl[:, :, :], 0.0)
            e.memset(x1T[:, :, 0:HALO], 0.0)
            e.memset(rt[:, 4, :, E:E + 2], -1.0)
            e.memset(steps[:, :, :], 0.0).then_inc(S["zero"], 1)
            e.wait_ge(S["zero"], 2)
            e.memset(n_mul[:, :, 1], 1.0)
            e.memset(h_mul[:, :, 1], -1.0).then_inc(S["zero"], 1)
            e.wait_ge(S["x_hi"], 1)
            e.tensor_tensor(xl[:, :, 0:GROUP], xf[:, :, 0:GROUP], xh[:, :, 0:GROUP].bitcast(F32), ALU.subtract).then_inc(S["x_split"], 1)
            for k in range(2):
                cols = slice(G3 // 2 * k, G3 // 2 * (k + 1))
                e.wait_ge(S["w_hi"], k + 1)
                e.tensor_tensor(wl[:, :, cols], wf[:, :, cols], wh[:, :, cols].bitcast(F32), ALU.subtract).then_inc(S["w_split"], 1)
            e.wait_ge(S["ld_whh"], 64)
            e.tensor_scalar(whh_hi[:, :, :], whf[:, :, :], WS, None, ALU.mult).then_inc(S["whh_high"], 1)
            e.wait_ge(S["whh_high"], 1)
            e.scalar_tensor_tensor(whh_lo[:, :, :], whf[:, :, :], WS, whh_hi[:, :, :], ALU.mult, ALU.subtract).then_inc(S["whh_split"], 1)
            h_at = lambda ap: ap.rearrange("p (c b) -> p c b", c=NC)
            e.tensor_copy(h_at(steps[:, 0, 2:25:3]), cond[:, :, :])
            e.tensor_copy(h_at(h16[:, 0, 2:24:3]), cond[:, :, :]).then_inc(S["h0_high"], 1)
            e.wait_ge(S["h0_high"], 1)
            e.tensor_tensor(h_at(h16[:, 1, 2:24:3]), cond[:, :, :], h_at(h16[:, 0, 2:24:3]), ALU.subtract)
            e.wait_ge(S["b_scaled"], 2)
            for c in range(NC):
                e.tensor_scalar(tmpl[:, 4 * c:4 * c + 4, 0], n_mul[:, 0:4, 1], bsc[:, 1, 4 + c:5 + c], None, ALU.mult)
            e.tensor_scalar(tmpl[:, :, 1], n_mul[:, :, 0], 0.0, None, ALU.mult).then_inc(S["zero"], 1)
            e.wait_ge(S["zero"], 4)
            e.wait_ge(S["banks_set"], 1)
            e.wait_ge(S["gi_ev"], 6)

            def seed(which, par, s):
                src, o, r = gi[:, par if s < STEPS else 1 - par], s % STEPS, s % RING
                if which == 0:
                    return e.tensor_copy(R[:, r:r + 8].rearrange("p s c b -> p s (c b)"), src[:, o:o + 8, 0:8])
                if which == 1:
                    e.tensor_copy(N[:, r:r + 8, :, :, 2].rearrange("p s c b -> p s (c b)"), src[:, o:o + 8, 16:24])
                    return e.tensor_copy(N[:, r:r + 8, :, :, 0:2].rearrange("p s c b e -> p s (c b) e"),
                                         tmpl[:, :, :].rearrange("p (a f) e -> p a f e", a=1).broadcast_to([P, 8, 8, 2]))
                return e.tensor_copy(Z[:, r:r + 8].rearrange("p s c b -> p s (c b)"), src[:, o:o + 8, 8:16])

            seed(0, 0, 0)
            seed(1, 0, 0).then_inc(S["h_hi"], 1)
            seed(2, 0, 0).then_inc(S["h_lo"], 1)

            def gru(m, par, s):
                n, slot, nxt = 32 * m + s + 1, s % RING, (s + 1) % RING
                if s % 8 == 0:
                    if some(4 * m + s // 8 - 1):
                        e.wait_ge(S["hist_done"], 4 * m + s // 8 - 1)
                e.wait_ge(S["r_done"], n)
                e.wait_ge(S["n_ready"], n)
                e.tensor_tensor_scan(flat(n_sum[:, :, :]), flat(n_mul[:, :, :]), N[:, slot].rearrange("p c b e -> p (c b e)"),
                                     0.0, ALU.mult, ALU.add).then_inc(S["n_summed"], 1)
                if s % 8 == 0:
                    if s == STEPS - 8:
                        if some(8 * m + 8 * par):
                            e.wait_ge(S[f"gi_in{1 - par}"], 8 * m + 8 * par)
                    seed(0, par, s + 8)
                if s % 8 == 1:
                    seed(1, par, s + 7)
                if s % 8 == 2:
                    e.wait_ge(S["z_done"], n)
                    last = seed(2, par, s + 6)
                    if s == STEPS - 14:
                        last.then_inc(S["gi_used"], 1)
                e.wait_ge(S["n_done"], n)
                e.wait_ge(S["z_done"], n)
                row, nrow = steps[:, slot, 1:25], steps[:, nxt, 0:24]
                e.tensor_tensor_scan(h16[:, 0, :], flat(h_mul[:, :, :]), row, 0.0, ALU.mult, ALU.add).then_inc(S["h_hi"], 1)
                e.tensor_tensor_scan(nrow, flat(h_mul[:, :, :]), row, 0.0, ALU.mult, ALU.add).then_inc(S["h_full"], 1)
                e.wait_ge(S["h_full"], n)
                e.tensor_tensor(h16[:, 1, 2:24:3], steps[:, nxt, 2:25:3], h16[:, 0, 2:24:3], ALU.subtract).then_inc(S["h_lo"], 1)

            def quant(s):
                src = lambda j: wgf[:, j, :] if j < 4 else wdf[:, j - 4, :]
                if Q_ABS <= s < Q_ABS + 6:
                    if s == Q_ABS:
                        e.wait_ge(S["ld_quant"], 32)
                    e.tensor_reduce(qp[:, s:s + 1], src(s), X, ALU.add, apply_absolute_value=True).then_inc(S["q_abs"], 1)
                if s == Q_RED:
                    e.wait_ge(S["q_pe"], 1)
                    e.tensor_reduce(qm[:, 0:1], bA[:, 0:4], X, ALU.add)
                    e.tensor_reduce(qm[:, 1:2], bA[:, 4:6], X, ALU.add).then_inc(S["q_step"], 1)
                if s == Q_CLIP:
                    e.wait_ge(S["q_step"], 1)
                    e.tensor_scalar(qc[:, 0, 0:1], qm[:, 0:1], 1.0 / (2 * FF * D), EPS_Q, ALU.mult, ALU.max)
                    e.tensor_scalar(qc[:, 0, 1:2], qm[:, 1:2], 1.0 / (FF * D), EPS_Q, ALU.mult, ALU.max).then_inc(S["q_step"], 1)
                if s == Q_INV:
                    e.wait_ge(S["q_step"], 2)
                    e.reciprocal(qc[:, 1, :], qc[:, 0, :]).then_inc(S["q_step"], 1)
                if s == Q_DIV:
                    e.tensor_scalar(qc[:, 2, :], qc[:, 0, :], 1.0 / QMAX, None, ALU.mult).then_inc(S["q_step"], 1)
                if Q_TERN <= s < Q_TERN + 18:
                    o = s - Q_TERN
                    j, step = o // 3, o % 3
                    w = src(j)
                    e.wait_ge(S["q_step"], 4 + 2 * j + step)
                    if step == 0:
                        which = 0 if j < 4 else 1
                        e.tensor_scalar(w, w, qc[:, 1, which:which + 1], MAGIC, ALU.mult, ALU.add).then_inc(S["q_step"], 1)
                    elif step == 1:
                        e.tensor_scalar(w, w, MAGIC, 1.0, ALU.subtract, ALU.min).then_inc(S["q_step"], 1)
                    else:
                        dst = tg[:, j // 2, (j % 2) * FF:(j % 2) * FF + FF] if j < 4 else flat(td[:, 3 * (j - 4):3 * (j - 4) + 3, :])
                        e.tensor_scalar(dst, w, -1.0, None, ALU.max).then_inc(S["q_tern"], 1)

            def attn(s, n, npar, B):
                if s == S_STAT:
                    e.wait_ge(S["sq_act"], n + 1)
                    e.tensor_tensor(hw[:, :], bA[:, 0:D], ng_b[:, :], ALU.mult).then_inc(S["hw_dve"], 1)
                if s == S_AMAX:
                    e.wait_ge(S["hw_dve"], n + 1)
                    e.tensor_reduce(sm[:, AM:AM + 1], hw[:, :], X, ALU.max, apply_absolute_value=True).then_inc(S["amax_dve"], 1)
                if s == S_MAG:
                    e.wait_ge(S["k_pool"], n + 1)
                    e.tensor_scalar(hw[:, :], hw[:, :], sm[:, K1:K1 + 1], MAGIC, ALU.mult, ALU.add).then_inc(S["mag_dve"], 1)
                if s == S_Q:
                    e.wait_ge(S["mag_dve"], n + 1)
                    if some(n):
                        e.wait_ge(S["qT_pe"], n)
                    e.tensor_scalar(qb[:, :], hw[:, :], MAGIC, None, ALU.subtract).then_inc(S["q_dve"], 1)
                for u, (off, w) in enumerate(UNITS):
                    if s == S_UNIT[u] + 1:
                        e.wait_ge(S["sg_act"], 3 * n + u + 1)
                        e.tensor_tensor(v[:, off:off + w], bA[:, 0:w], sg[:, 0:w], ALU.mult).then_inc(S["gt_dve"], 1)
                    if s == S_UNIT[u] + 2:
                        e.wait_ge(S["gt_dve"], 3 * n + u + 1)
                        e.tensor_tensor(v[:, off:off + w], bA[:, 256:256 + w], v[:, off:off + w], ALU.mult).then_inc(S["v_dve"], 1)
                    if s == S_UNIT[u] + 4:
                        e.wait_ge(S["vw_pool"], 3 * n + u + 1)
                        e.tensor_reduce(sm[:, AM2 + u:AM2 + u + 1], v[:, off:off + w], X, ALU.max,
                                        apply_absolute_value=True).then_inc(S["max2_dve"], 1)
                if s == S_MAG2:
                    e.wait_ge(S["k2_pool"], n + 1)
                    e.tensor_scalar(v[:, :], v[:, :], sm[:, K2:K2 + 1], MAGIC, ALU.mult, ALU.add).then_inc(S["mag2_dve"], 1)
                if s == S_Q2:
                    e.wait_ge(S["mag2_dve"], n + 1)
                    if some(n):
                        e.wait_ge(S["q2T_pe"], n)
                    e.tensor_scalar(q2b[:, :], v[:, :], MAGIC, None, ALU.subtract).then_inc(S["q2_dve"], 1)
                if s == S_DOWN:
                    e.wait_ge(S[f"xt_in{npar}"], 8 * n - 8 * npar + 16)
                    if some(kept(n, B)):
                        e.wait_ge(S["x1_kept"], kept(n, B))
                    e.wait_ge(S["down_pe"], n + 1)
                    e.scalar_tensor_tensor(x1[:, npar, :], bA[:, 0:D], sm[:, OSC2:OSC2 + 1], xt[:, npar, :],
                                           ALU.mult, ALU.add).then_inc(S["x1_dve"], 1)
                if s in S_CONV and last_tile(n):
                    k = s - S_CONV[0]
                    for c in range(NC):
                        src = x1T[:, c, npar * P + NB * k:npar * P + NB * k + P]
                        dst = xc[:, c, npar * P:npar * P + P]
                        if k == 0:
                            if c == 0:
                                e.wait_ge(S["x1T_act"], n + 1)
                                e.wait_ge(S["xlo_pool"], kept(n, B))
                                e.wait_ge(S["r_log"], 2 * kept(n, B))
                            e.tensor_scalar(dst, src, cond[:, c, k:k + 1], None, ALU.mult).then_inc(S["conv_last"], 1)
                        else:
                            e.wait_ge(S["conv_last"], NC * (k - 1) + c + 1)
                            ins = e.scalar_tensor_tensor(dst, src, cond[:, c, k:k + 1], dst, ALU.mult, ALU.add)
                            if k < KK - 1:
                                ins.then_inc(S["conv_last"], 1)
                            elif c == NC - 1:
                                ins.then_inc(S["conv_sum"], KK - 1)
            def result(B):
                e.wait_ge(S["m_o"], NF * (B + 1))
                e.wait_ge(S["x1_kept"], B + 1)
                e.tensor_tensor(flat(yt[:, :, :]), bO[:, :], flat(x1b[:, :, :]), ALU.add).then_inc(S["y_done"], 1)

            def by_token(k):
                return rs[:, k, :].rearrange("p (t a) -> p t a", a=1).broadcast_to([P, 2, E])

            def moe(q, B):
                logits = bM[0][:, 0:2 * E].rearrange("p (t e) -> p t e", t=2)
                if q == M_RESULT and not (isinstance(B, int) and B == 0):
                    result(B - 1)
                if q == STEPS - 1 and opened(B):
                    if some(32 * B):
                        e.wait_ge(S["y_out"], 32 * B)
                if q == R_DIFF and opened(B):
                    e.wait_ge(S["r_log"], 2 * (B + 1))
                    e.tensor_reduce(rs[:, 0, :], logits, X, ALU.max).then_inc(S["r_max"], 1)
                if q == R_DIFF and opened(B):
                    e.wait_ge(S["r_max"], B + 1)
                    e.tensor_tensor(rt[:, 0, :, 0:E], logits, by_token(0), ALU.subtract).then_inc(S["r_d"], 1)
                if q == R_EXP and opened(B):
                    e.wait_ge(S["r_sig"], B + 1)
                    e.reciprocal(rt[:, 2, :, 0:E], rt[:, 2, :, 0:E]).then_inc(S["r_inv"], 1)
                if q == R_SUM and opened(B):
                    e.wait_ge(S["r_e"], B + 1)
                    e.tensor_reduce(rs[:, 1, :], rt[:, 3, :, 0:E], X, ALU.add).then_inc(S["r_sum"], 1)
                if q == R_P and opened(B):
                    e.wait_ge(S["r_sum"], B + 1)
                    e.reciprocal(rs[:, 2, :], rs[:, 1, :]).then_inc(S["r_isum"], 1)
                    e.wait_ge(S["r_isum"], B + 1)
                    e.tensor_tensor(rt[:, 4, :, 0:E], rt[:, 3, :, 0:E], by_token(2), ALU.mult).then_inc(S["r_p"], 1)
                if q == R_TOP and opened(B):
                    count = fixed(e, B + 1)
                    e.wait_ge(S["r_p"], count)
                    e.max(m8[:, 0, :], rt[:, 4, 0, 0:E])
                    e.max(m8[:, 1, :], rt[:, 4, 1, 0:E]).then_inc(S["r_m8"], 1)
                if q == R_SIX and opened(B):
                    count = fixed(e, B + 1)
                    e.wait_ge(S["r_m8"], count)
                    e.memset(m8[:, :, TOPK:8], -1.0).then_inc(S["r_m8set"], 1)
                if q == R_REP and opened(B):
                    count = fixed(e, B + 1)
                    e.wait_ge(S["r_m8set"], count)
                    e.match_replace(rt[:, 5, 0, :], m8[:, 0, :], rt[:, 4, 0, :], -2.0)
                    e.match_replace(rt[:, 5, 1, :], m8[:, 1, :], rt[:, 4, 1, :], -2.0).then_inc(S["r_rep"], 1)
                    e.wait_ge(S["r_rep"], B + 1)
                    e.scalar_tensor_tensor(rt[:, 7, :, 0:E], rt[:, 5, :, 0:E], 0.0, rt[:, 4, :, 0:E],
                                           ALU.is_lt, ALU.mult).then_inc(S["r_chosen"], 1)
                if q == R_SEL and opened(B):
                    e.wait_ge(S["r_chosen"], B + 1)
                    e.tensor_reduce(rs[:, 3, :], rt[:, 7, :, 0:E], X, ALU.add).then_inc(S["r_csum"], 1)
                    e.wait_ge(S["r_csum"], B + 1)
                    e.tensor_scalar(rs[:, 4, :], rs[:, 3, :], 1e-20, None, ALU.add).then_inc(S["r_guard"], 1)
                if q == R_C3 and opened(B):
                    e.wait_ge(S["r_guard"], B + 1)
                    e.reciprocal(rs[:, 5, :], rs[:, 4, :]).then_inc(S["r_icsum"], 1)
                    e.wait_ge(S["r_icsum"], B + 1)
                    e.tensor_tensor(rt[:, 6, :, 0:E], rt[:, 7, :, 0:E], by_token(5), ALU.mult).then_inc(S["r_c"], 1)
                for j, B_ in at_slot(q, M_SIG, B):
                    e.wait_ge(S["m_sig"], NF * B_ + j + 1)
                    e.tensor_tensor(act[:, j % 3, :], bM[j % 2][:, 0:256], act[:, j % 3, :], ALU.mult).then_inc(S["m_t"], 1)
                for j, B_ in at_slot(q, M_T2, B):
                    e.wait_ge(S["m_t"], NF * B_ + j + 1)
                    e.tensor_tensor(act[:, j % 3, :], bM[j % 2][:, 256:512], act[:, j % 3, :],
                                    ALU.mult).then_inc(S["m_a" if j < NSH else "m_t2"], 1)
                for j, B_ in at_slot(q, M_A, B, NSH):
                    d = (j - NSH) % 2
                    e.wait_ge(S["m_c"], (NF - NSH) // 2 * B_ + (j - NSH) // 2 + 1)
                    e.wait_ge(S["m_t2"], (NF - NSH) * B_ + j - NSH + 1)
                    e.tensor_tensor(act[:, j % 3, :], bC[:, 256 * d:256 * d + 256], act[:, j % 3, :], ALU.mult).then_inc(S["m_a"], 1)

            def rest(s, prep, n, npar, B, q):
                if prep == 0:
                    quant(s)
                if prep == 1 and s == 0:
                    e.wait_ge(S["ld_const"], 96)
                if n is not None:
                    attn(s, n, npar, B)
                if B is not None:
                    moe(q, B)

            program(e, gru, rest)

        @block.gpsimd
        def _(e):
            e.memset(ones[:, :], 1.0)
            e.memset(pw[:, :], -1.0).then_inc(S["b_scaled"], 1)
            e.wait_ge(S["b_scaled"], 1)
            e.memset(pw[:, 0:1], -0.5)
            e.wait_ge(S["ld_whh"], 64)
            e.tensor_scalar(bsc[:, :, :], bias[:, :, :], WS, None, ALU.mult).then_inc(S["r_link"], 1)
            e.wait_ge(S["r_link"], 1)
            e.tensor_tensor(bsc[:, 0, 0:4], bsc[:, 0, 0:4], bsc[:, 1, 0:4], ALU.add).then_inc(S["b_scaled"], 1)
            e.memset(m8[:, :, :], 0.0).then_inc(S["setup"], 1)
            col = lambda k: sm[:, k:k + 1]
            half_, one_ = pw[:, 0:1], pw[:, 1:2]

            def gru(m, par, s):
                if s % 8 == 7:
                    count = fixed(e, 32 * m + s + 1)
                    e.wait_ge(S["h_full"], count)
                    if some(m - 1):
                        e.wait_ge(S["ht_pe"], m - 1)
                    first = (s - 6) % RING
                    runs = ((first, 8),) if first + 8 <= RING else ((first, RING - first), (0, 8 - (RING - first)))
                    t = NB * (s - 7)
                    for r, cnt in runs:
                        ins = e.tensor_copy(hist[:, par, :, t:t + NB * cnt].rearrange("p c (s b) -> p c s b", b=NB),
                                            steps[:, r:r + cnt, 2:25:3].rearrange("p s (c b) -> p c s b", c=NC))
                        t += NB * cnt
                    ins.then_inc(S["hist_done"], 1)

            def attn(s, n, npar, B):
                if s == S_AMAX:
                    b = (LINK1 + LINK2) * n
                    count = fixed(e, n + 1)
                    e.wait_ge(S["sq_act"], count)
                    e.tensor_scalar(col(VAR), col(SS), 1.0 / D, EPS_NORM, ALU.mult, ALU.add).then_inc(S["sm_link"], 1)
                    e.wait_ge(S["sm_link"], b + 1)
                    e.tensor_tensor(col(RR), col(VAR), half_, ALU.pow).then_inc(S["sm_link"], 1)
                    links, count = in_register(e, b + 2), fixed(e, n + 1)
                    e.wait_ge(S["amax_dve"], count)
                    e.wait_ge(S["sm_link"], links)
                    e.tensor_scalar(col(MC), col(AM), col(RR), EPS_Q, ALU.mult, ALU.max).then_inc(S["sm_link"], 1)
                    e.wait_ge(S["sm_link"], b + 3)
                    e.tensor_tensor(col(OSC), col(MC), qc[:, 2, 0:1], ALU.mult).then_inc(S["sm_link"], 1)
                    e.tensor_tensor(col(RC), col(MC), one_, ALU.pow).then_inc(S["sm_link"], 1)
                    count = fixed(e, b + 5)
                    e.wait_ge(S["sm_link"], count)
                    e.tensor_scalar(col(K1), col(RC), QMAX, col(RR), ALU.mult, ALU.mult).then_inc(S["k_pool"], 1)
                    e.tensor_tensor(col(O2), col(OSC), col(OSC), ALU.mult).then_inc(S["sm_link"], 1)
                    count = fixed(e, b + 6)
                    e.wait_ge(S["sm_link"], count)
                    e.tensor_scalar(col(O4), col(O2), col(O2), 1.0 / FF, ALU.mult, ALU.mult).then_inc(S["sm_link"], 1)
                for u, (off, w) in enumerate(UNITS):
                    if s == S_UNIT[u] + 3:
                        e.wait_ge(S["sq2_act"], 3 * n + u + 1)
                        e.tensor_tensor(v[:, off:off + w], v[:, off:off + w], nd_b[:, off:off + w], ALU.mult).then_inc(S["vw_pool"], 1)
                if s == S_K2:
                    b = (LINK1 + LINK2) * n + LINK1
                    links, count = in_register(e, b), fixed(e, 3 * n + 3)
                    e.wait_ge(S["sq2_act"], count)
                    e.wait_ge(S["sm_link"], links)
                    e.tensor_scalar(col(VAR2), col(SS2), col(SS2 + 1), col(SS2 + 2), ALU.add, ALU.add).then_inc(S["sm_link"], 1)
                    count = fixed(e, b + 1)
                    e.wait_ge(S["sm_link"], count)
                    e.tensor_scalar(col(VAR2), col(VAR2), col(O4), EPS_NORM, ALU.mult, ALU.add).then_inc(S["sm_link"], 1)
                    e.wait_ge(S["sm_link"], b + 2)
                    e.tensor_tensor(col(R2), col(VAR2), half_, ALU.pow).then_inc(S["sm_link"], 1)
                    count = fixed(e, 3 * n + 3)
                    e.wait_ge(S["max2_dve"], count)
                    e.tensor_scalar(col(AMX), col(AM2), col(AM2 + 1), col(AM2 + 2), ALU.max, ALU.max).then_inc(S["sm_link"], 1)
                    e.wait_ge(S["sm_link"], b + 4)
                    e.tensor_tensor(col(OR2), col(R2), col(O2), ALU.mult).then_inc(S["sm_link"], 1)
                    count = fixed(e, b + 5)
                    e.wait_ge(S["sm_link"], count)
                    e.tensor_scalar(col(MC2), col(AMX), col(OR2), EPS_Q, ALU.mult, ALU.max).then_inc(S["sm_link"], 1)
                    e.wait_ge(S["sm_link"], b + 6)
                    e.tensor_tensor(col(OSC2), col(MC2), qc[:, 2, 1:2], ALU.mult).then_inc(S["sm_link"], 1)
                    e.tensor_tensor(col(RC2), col(MC2), one_, ALU.pow).then_inc(S["sm_link"], 1)
                    count = fixed(e, b + 8)
                    e.wait_ge(S["sm_link"], count)
                    e.tensor_scalar(col(K2), col(RC2), QMAX, col(OR2), ALU.mult, ALU.mult).then_inc(S["k2_pool"], 1)
                if s in S_CONV and not last_tile(n):
                    k = s - S_CONV[0]
                    if k == 0:
                        behind, two_behind = in_register(e, kept(n, B)), in_register(e, 2 * kept(n, B))
                        count = fixed(e, n + 1)
                        e.wait_ge(S["x1T_act"], count)
                        if some(behind):
                            e.wait_ge(S["xlo_pool"], behind)
                            e.wait_ge(S["r_log"], two_behind)
                            if npar == 0:
                                e.wait_ge(S["halo_act"], behind)
                    else:
                        count = fixed(e, 4 * n + 1 if k == 1 else 3 * n + k - 1)
                        e.wait_ge(S["conv_tap" if k == 1 else "conv_sum"], count)
                    own = xc[:, :, npar * P:npar * P + P]
                    for c in range(NC):
                        ins = e.tensor_scalar((own if k == 0 else tap)[:, c, :], x1T[:, c, npar * P + NB * k:npar * P + NB * k + P],
                                              cond[:, c, k:k + 1], None, ALU.mult)
                    ins.then_inc(S["conv_tap"], 1)
                    if k > 0:
                        e.wait_ge(S["conv_tap"], 4 * n + k + 1)
                        e.tensor_tensor(own, own, tap[:, :, :], ALU.add).then_inc(S["conv_sum"], 1)

            def moe(q, B):
                lb = 1 + LINKR * B
                t_ = lambda k: rt[:, k, :, 0:E]
                if q == 0 and opened(B):
                    e.wait_ge(S["xhi_act"], B + 1)
                    e.tensor_tensor(xc_lo[:, :, :], xc[:, :, :], xc_hi[:, :, :].bitcast(F32), ALU.subtract).then_inc(S["xlo_pool"], 1)
                if q == M_KEEP and opened(B):
                    count = fixed(e, 2 * B + 2)
                    e.wait_ge(S["x1_dve"], count)
                    if some(B):
                        e.wait_ge(S["y_done"], B)
                    e.tensor_copy(flat(x1b[:, :, :]), flat(x1[:, :, :])).then_inc(S["x1_kept"], 1)
                if q == R_EXP and opened(B):
                    e.wait_ge(S["r_inv"], B + 1)
                    e.tensor_tensor(t_(3), t_(1), t_(2), ALU.mult).then_inc(S["r_e"], 1)
                if q == R_C3 and opened(B):
                    count = fixed(e, B + 1)
                    e.wait_ge(S["r_c"], count)
                    if some(B):
                        e.wait_ge(S["r_cT"], B)
                    e.tensor_copy(c3[:, :, 0:E], t_(6)).then_inc(S["r_link"], 1)
                    e.wait_ge(S["r_link"], lb + 1)
                    e.tensor_tensor(t_(0), t_(6), c3[:, :, 0:E], ALU.subtract).then_inc(S["r_link"], 1)
                    count = fixed(e, lb + 2)
                    e.wait_ge(S["r_link"], count)
                    e.tensor_copy(c3[:, :, E:2 * E], t_(0)).then_inc(S["r_link"], 1)
                    e.wait_ge(S["r_link"], lb + 3)
                    e.tensor_tensor(c3[:, :, 2 * E:3 * E], t_(0), c3[:, :, E:2 * E], ALU.subtract).then_inc(S["r_c3"], 1)
                for j, B_ in at_slot(q, M_SPLIT, B):
                    e.wait_ge(S["m_hi"], NF * B_ + j + 1)
                    e.tensor_tensor(act_lo[:, j % 2, :], act[:, j % 3, :], act_hi[:, j % 2, :].bitcast(F32), ALU.subtract).then_inc(S["m_lo"], 1)

            def rest(s, prep, n, npar, B, q):
                if prep == 0 and s < 2 * (GROUPS - 1) and s % 2 == 0:
                    cols = slice(GROUP * (1 + s // 2), GROUP * (2 + s // 2))
                    e.wait_ge(S["x_hi"], 2 + s // 2)
                    e.tensor_tensor(xl[:, :, cols], xf[:, :, cols], xh[:, :, cols].bitcast(F32), ALU.subtract).then_inc(S["x_low"], 1)
                if prep == 1 and s == 0:
                    e.wait_ge(S["ld_const"], 96)
                k = prep_piece(prep, s)
                if k is not None:
                    e.wait_ge(S["prep_hi"], k + 1)
                    src, hi, lo = prep_views(k)
                    e.tensor_tensor(lo, src, hi.bitcast(F32), ALU.subtract).then_inc(S["prep_lo"], 1)
                if n is not None:
                    attn(s, n, npar, B)
                if B is not None:
                    moe(q, B)

            program(e, gru, rest)


def kernel(x, cond_2048, L0_cond_W_ih, L0_cond_W_hh, L0_cond_b_ih, L0_cond_b_hh, L0_attn_w_gate, L0_attn_norm_gate,
           L0_attn_w_down, L0_attn_norm_down, L0_ffn_gate_w, L0_ffn_w13, L0_ffn_w2, L0_ffn_sw13, L0_ffn_sw2):
    import numpy as np
    import ml_dtypes
    import concourse.bacc as bacc
    from concourse.bass_utils import run_bass_kernel_spmd as run

    f = np.ascontiguousarray
    x, cond = np.asarray(x), np.asarray(cond_2048)
    tokens = x.transpose(1, 0, 2).reshape(T * NB, D)

    def by_chunk(a):
        return f(a.reshape(-1, P, a.shape[1]).transpose(1, 0, 2))

    w13, w2 = np.asarray(L0_ffn_w13), np.asarray(L0_ffn_w2)
    sw13, sw2 = np.asarray(L0_ffn_sw13), np.asarray(L0_ffn_sw2)
    gu = np.zeros((2, NF * P, D), np.float32)
    gu[0, :ROWS], gu[1, :ROWS] = w13[:, :EI].reshape(ROWS, D), w13[:, EI:].reshape(ROWS, D)
    gu[0, ROWS:ROWS + SI], gu[1, ROWS:ROWS + SI] = sw13[:SI], sw13[SI:]
    down = np.zeros((NF * P, D), np.float32)
    down[:ROWS], down[ROWS:ROWS + SI] = w2.transpose(0, 2, 1).reshape(ROWS, D), sw2.T
    w13_l = gu.reshape(2, NF, P, NC, P).transpose(4, 1, 0, 3, 2).reshape(P, NF, 512)
    w2_l = down.reshape(NF, P, D).transpose(1, 0, 2).reshape(P, NF * D)
    wg = np.asarray(L0_attn_w_gate).T.reshape(NC, P, 2 * FF).transpose(1, 0, 2).reshape(P, 4, FF)
    wd = np.zeros((FC * P, D), np.float32)
    wd[:FF] = np.asarray(L0_attn_w_down).T
    wd = wd.reshape(FC, P, D).transpose(1, 0, 2).reshape(P, 2, FC * D // 2)
    sel = np.tile(np.repeat(np.eye(E), EI, axis=1), (3, 1)).astype(ml_dtypes.bfloat16)
    ins = {
        "xT": by_chunk(tokens.T), "xtok": f(tokens.reshape(TILES, P, D)),
        "w_ih": by_chunk(np.asarray(L0_cond_W_ih)), "w_hh": by_chunk(np.asarray(L0_cond_W_hh)),
        "condT": by_chunk(cond.T),
        "b_ih": f(np.asarray(L0_cond_b_ih).reshape(6, P).T), "b_hh": f(np.asarray(L0_cond_b_hh).reshape(6, P).T),
        "wgT": f(wg), "wdT": f(wd),
        "ng": f(np.asarray(L0_attn_norm_gate).reshape(1, D)), "nd": f(np.asarray(L0_attn_norm_down).reshape(1, FF)),
        "gwT": by_chunk(np.asarray(L0_ffn_gate_w).T), "w13": f(w13_l), "w2": f(w2_l),
        "sel": f(sel), "idf": np.eye(P, dtype=np.float32), "idb": np.eye(P).astype(ml_dtypes.bfloat16),
    }
    nc = bacc.Bacc("TRN2", target_bir_lowering=False, num_devices=1, dynamic_dma_scratch_size=1024)
    aps = {n: nc.dram_tensor(f"in_{n}", a.shape, mybir.dt.from_np(a.dtype), kind="ExternalInput").ap() for n, a in ins.items()}
    out = nc.dram_tensor("out_0", (TILES, P, D), F32, kind="ExternalOutput").ap()
    build(nc, out=out, **aps)
    r = run(nc, [{f"in_{n}": a for n, a in ins.items()}], core_ids=[0])
    y = r.results[0]["out_0"]
    return f(y.reshape(T, NB, D).transpose(1, 0, 2))
```
